# Optimizing a Trainium2 kernel written in Bass

```python
import numpy as np
import jax
import jax.numpy as jnp

def _softmax(x, axis=-1):
    return jax.nn.softmax(x, axis=axis)

def _gelu(x):
    return jax.nn.gelu(x, approximate=True)

def _silu(x):
    return jax.nn.silu(x)

def _sigmoid(x):
    return jax.nn.sigmoid(x)

def _layernorm(x, axis=-1, eps=1e-05):
    m = jnp.mean(x, axis=axis, keepdims=True)
    v = jnp.var(x, axis=axis, keepdims=True)
    return (x - m) / jnp.sqrt(v + eps)

def _scatter_add(tgt, idx, src, axis=0):
    return tgt.at[idx].add(src)

def _segment_sum(src, seg, n):
    return jax.ops.segment_sum(src, seg, n)
kernel_name = 'mk_gps_d1_gnn_r16_c138eb'

def setup_inputs(seed: int=0):
    np.random.seed(seed)
    _w = jnp.asarray

    def _rec_inputs():
        import jax
        import jax.numpy as jnp
        _gk = jax.random.key(seed)
        x = -0.0001126 + 1 * jax.random.normal(jax.random.fold_in(_gk, 1), (625, 768), jnp.float32)
        _s = jax.random.randint(jax.random.fold_in(_gk, 2), (10000,), 0, 625, jnp.int32)
        _d = jax.random.randint(jax.random.fold_in(_gk, 3), (10000,), 0, 625, jnp.int32)
        _loop = jnp.arange(625, dtype=jnp.int32)
        src = jnp.concatenate([_s, _d, _loop])
        dst = jnp.concatenate([_d, _s, _loop])
        _o = jnp.argsort(dst, stable=True)
        src = src[_o]
        dst = dst[_o]
        return (x, src, dst)
    x, src, dst = _rec_inputs()

    def _L0_gnn_setup():
        import jax, jax.numpy as jnp
        import numpy as np
        N_NODES = 625
        N_EDGES = 6250
        DIM = 768
        key = jax.random.key(seed)
        k1, k2, k3, k4 = jax.random.split(key, 4)
        x = jax.random.normal(k1, (N_NODES, DIM), dtype=jnp.float32)
        edge_index = jax.random.randint(k2, (2, N_EDGES), 0, N_NODES, dtype=jnp.int32)
        W = jax.random.normal(k3, (DIM, DIM), dtype=jnp.float32) / np.sqrt(DIM)
        b = jnp.zeros((DIM,), dtype=jnp.float32)
        return {'x': x, 'edge_index': edge_index, 'W': W, 'b': b}
    _L0_gnn_all = _L0_gnn_setup()
    _L0_gnn_in = {k: v for k, v in _L0_gnn_all.items() if k in ('W', 'b')}
    del _L0_gnn_all

    def _L0_mix_setup():
        import math
        import jax, jax.numpy as jnp
        import numpy as np
        NUM_HEADS = 12
        EPS = 0.0001

        def softmax_kernel_features(data, proj, is_query):
            d = data.shape[-1]
            data_normalizer = 1.0 / math.sqrt(math.sqrt(d))
            ratio = 1.0 / math.sqrt(proj.shape[0])
            data_dash = jnp.einsum('bhnd,md->bhnm', data_normalizer * data, proj)
            diag_data = jnp.sum(jnp.square(data), axis=-1, keepdims=True) * 0.5 * data_normalizer * data_normalizer
            if is_query:
                stab = jnp.max(data_dash, axis=-1, keepdims=True)
            else:
                stab = jnp.max(data_dash)
            return ratio * (jnp.exp(data_dash - diag_data - stab) + EPS)
        key = jax.random.key(seed)
        k0, k1, k2, k3, k4 = jax.random.split(key, 5)
        B, N, C, H = (8, 256, 768, NUM_HEADS)
        hd = C // H
        m = int(hd * math.log(hd))
        x = jax.random.normal(k0, (B, N, C), dtype=jnp.float32)
        W_qkv = jax.random.normal(k1, (C, 3 * C), dtype=jnp.float32) / math.sqrt(C)
        W_proj = jax.random.normal(k2, (C, C), dtype=jnp.float32) / math.sqrt(C)
        b_proj = jnp.zeros((C,), dtype=jnp.float32)
        proj_mat = jax.random.normal(k3, (m, hd), dtype=jnp.float32)
        return {'x': x, 'W_qkv': W_qkv, 'W_proj': W_proj, 'b_proj': b_proj, 'proj_mat': proj_mat}
    _L0_mix_all = _L0_mix_setup()
    _L0_mix_in = {k: v for k, v in _L0_mix_all.items() if k in ('W_qkv', 'W_proj', 'b_proj', 'proj_mat')}
    del _L0_mix_all

    def _L0_ffn_setup():
        import jax, jax.numpy as jnp
        import numpy as np
        SEQ, BATCH, EMBED = (1024, 2, 768)
        E = 16
        FFN_H = 1536
        K_SHARED = 1
        K_ROUTE = 3
        LN_EPS = 1e-05
        NEG_INF = -1000000000.0
        key = jax.random.key(seed)
        ks = jax.random.split(key, 4)
        x = jax.random.normal(ks[0], (SEQ, BATCH, EMBED), dtype=jnp.float32)
        gate_w = jax.random.normal(ks[1], (EMBED, E), dtype=jnp.float32) * 0.02
        gate_b = jnp.zeros((E,), jnp.float32)
        fc1_w = jax.random.normal(ks[2], (E, EMBED, FFN_H), dtype=jnp.float32) * 0.02
        fc1_b = jnp.zeros((E, FFN_H), jnp.float32)
        ln_w = jnp.ones((E, FFN_H), jnp.float32)
        ln_b = jnp.zeros((E, FFN_H), jnp.float32)
        fc2_w = jax.random.normal(ks[3], (E, FFN_H, EMBED), dtype=jnp.float32) * 0.02
        fc2_b = jnp.zeros((E, EMBED), jnp.float32)
        return {'x': x, 'gate_w': gate_w, 'gate_b': gate_b, 'fc1_w': fc1_w, 'fc1_b': fc1_b, 'ln_w': ln_w, 'ln_b': ln_b, 'fc2_w': fc2_w, 'fc2_b': fc2_b}
    _L0_ffn_all = _L0_ffn_setup()
    _L0_ffn_in = {k: v for k, v in _L0_ffn_all.items() if k in ('gate_w', 'gate_b', 'fc1_w', 'fc1_b', 'ln_w', 'ln_b', 'fc2_w', 'fc2_b')}
    del _L0_ffn_all
    return {'x': x, 'src': src, 'dst': dst, 'L0_gnn_W': _L0_gnn_in['W'], 'L0_gnn_b': _L0_gnn_in['b'], 'L0_mix_W_qkv': _L0_mix_in['W_qkv'], 'L0_mix_W_proj': _L0_mix_in['W_proj'], 'L0_mix_b_proj': _L0_mix_in['b_proj'], 'L0_mix_proj_mat': _L0_mix_in['proj_mat'], 'L0_ffn_gate_w': _L0_ffn_in['gate_w'], 'L0_ffn_gate_b': _L0_ffn_in['gate_b'], 'L0_ffn_fc1_w': _L0_ffn_in['fc1_w'], 'L0_ffn_fc1_b': _L0_ffn_in['fc1_b'], 'L0_ffn_ln_w': _L0_ffn_in['ln_w'], 'L0_ffn_ln_b': _L0_ffn_in['ln_b'], 'L0_ffn_fc2_w': _L0_ffn_in['fc2_w'], 'L0_ffn_fc2_b': _L0_ffn_in['fc2_b']}

def reference(x, src, dst, L0_gnn_W, L0_gnn_b, L0_mix_W_qkv, L0_mix_W_proj, L0_mix_b_proj, L0_mix_proj_mat, L0_ffn_gate_w, L0_ffn_gate_b, L0_ffn_fc1_w, L0_ffn_fc1_b, L0_ffn_ln_w, L0_ffn_ln_b, L0_ffn_fc2_w, L0_ffn_fc2_b):
    import jax
    import jax.numpy as jnp

    def _L0_gnn_ref(x, edge_index, W, b):
        import jax, jax.numpy as jnp
        import numpy as np
        N_NODES = 625
        N_EDGES = 6250
        DIM = 768
        n = x.shape[0]
        loop = jnp.arange(n, dtype=edge_index.dtype)
        src = jnp.concatenate([edge_index[0], loop])
        dst = jnp.concatenate([edge_index[1], loop])
        deg = jax.ops.segment_sum(jnp.ones_like(dst, dtype=x.dtype), dst, num_segments=n)
        deg_inv_sqrt = jnp.where(deg > 0, jax.lax.rsqrt(deg), 0.0)
        norm = deg_inv_sqrt[src] * deg_inv_sqrt[dst]
        h = x @ W
        msg = h[src] * norm[:, None]
        out = jax.ops.segment_sum(msg, dst, num_segments=n)
        return out + b

    def _L0_mix_ref(x, W_qkv, W_proj, b_proj, proj_mat):
        import math
        import jax, jax.numpy as jnp
        import numpy as np
        NUM_HEADS = 12
        EPS = 0.0001

        def softmax_kernel_features(data, proj, is_query):
            d = data.shape[-1]
            data_normalizer = 1.0 / math.sqrt(math.sqrt(d))
            ratio = 1.0 / math.sqrt(proj.shape[0])
            data_dash = jnp.einsum('bhnd,md->bhnm', data_normalizer * data, proj)
            diag_data = jnp.sum(jnp.square(data), axis=-1, keepdims=True) * 0.5 * data_normalizer * data_normalizer
            if is_query:
                stab = jnp.max(data_dash, axis=-1, keepdims=True)
            else:
                stab = jnp.max(data_dash)
            return ratio * (jnp.exp(data_dash - diag_data - stab) + EPS)
        B, N, C = x.shape
        H = NUM_HEADS
        hd = C // H
        qkv = (x @ W_qkv).reshape(B, N, 3, H, hd)
        qkv = jnp.transpose(qkv, (2, 0, 3, 1, 4))
        q, k, v = (qkv[0], qkv[1], qkv[2])
        q1 = softmax_kernel_features(q, proj_mat, is_query=True)
        k1 = softmax_kernel_features(k, proj_mat, is_query=False)
        kv = jnp.einsum('bhnm,bhnd->bhmd', k1, v)
        ksum = jnp.sum(k1, axis=2)
        z = 1.0 / jnp.einsum('bhnm,bhm->bhn', q1, ksum)
        out = jnp.einsum('bhnm,bhmd->bhnd', q1, kv) * z[..., None]
        out = jnp.transpose(out, (0, 2, 1, 3)).reshape(B, N, C)
        return out @ W_proj + b_proj

    def _L0_ffn_ref(x, gate_w, gate_b, fc1_w, fc1_b, ln_w, ln_b, fc2_w, fc2_b):
        import jax, jax.numpy as jnp
        import numpy as np
        SEQ, BATCH, EMBED = (1024, 2, 768)
        E = 16
        FFN_H = 1536
        K_SHARED = 1
        K_ROUTE = 3
        LN_EPS = 1e-05
        NEG_INF = -1000000000.0
        S, B, D = x.shape
        T = S * B
        xf = x.reshape(T, D)
        scores = xf @ gate_w + gate_b
        scores = scores.at[:, :K_SHARED].set(NEG_INF)
        probs = jax.nn.softmax(scores, axis=-1)
        topv, topi = jax.lax.top_k(probs, K_ROUTE)
        combine = jnp.zeros((T, E), xf.dtype)
        combine = combine.at[jnp.arange(T)[:, None], topi].add(topv)
        combine = combine.at[:, :K_SHARED].add(1.0)
        h = jnp.einsum('td,edh->eth', xf, fc1_w) + fc1_b[:, None, :]
        h = jax.nn.gelu(h, approximate=False)
        mu = h.mean(-1, keepdims=True)
        var = h.var(-1, keepdims=True)
        h = (h - mu) * jax.lax.rsqrt(var + LN_EPS) * ln_w[:, None, :] + ln_b[:, None, :]
        y = jnp.einsum('eth,ehd->etd', h, fc2_w) + fc2_b[:, None, :]
        out = jnp.einsum('te,etd->td', combine, y)
        return out.reshape(S, B, D)
    edge_index = jnp.stack([src, dst])
    xn = _layernorm(x, axis=-1)
    x = x + _L0_gnn_ref(xn, edge_index, L0_gnn_W, L0_gnn_b) + _L0_mix_ref(xn[None], L0_mix_W_qkv, L0_mix_W_proj, L0_mix_b_proj, L0_mix_proj_mat)[0]
    x = x + _L0_ffn_ref(_layernorm(x, axis=-1)[None], L0_ffn_gate_w, L0_ffn_gate_b, L0_ffn_fc1_w, L0_ffn_fc1_b, L0_ffn_ln_w, L0_ffn_ln_b, L0_ffn_fc2_w, L0_ffn_fc2_b)[0]
    return x

_drawn_inputs = setup_inputs


def setup_inputs(seed=0):
    import zlib

    import numpy as np

    out = dict(_drawn_inputs(seed))
    spreads = {'L0_gnn_b': (0.0, 0.1),
     'L0_mix_b_proj': (0.0, 0.1),
     'L0_ffn_gate_b': (0.0, 0.1),
     'L0_ffn_fc1_b': (0.0, 0.1),
     'L0_ffn_ln_w': (1.0, 0.2),
     'L0_ffn_ln_b': (0.0, 0.1),
     'L0_ffn_fc2_b': (0.0, 0.1)}
    factors = {}
    for name, (base, spread) in spreads.items():
        noise = np.random.default_rng([zlib.crc32(name.encode()), seed]).standard_normal(out[name].shape)
        drawn = base * np.exp(spread * noise) if base else spread * noise
        out[name] = jnp.asarray(drawn.astype(out[name].dtype))
    for name, factor in factors.items():
        out[name] = (out[name] * factor).astype(out[name].dtype)
    return out
```

```python
import math
from contextlib import ExitStack

import concourse.bass as bass
from concourse import mybir

F32 = mybir.dt.float32
F32R = mybir.dt.float32r
BF16 = mybir.dt.bfloat16
F16 = mybir.dt.float16
I32 = mybir.dt.int32
U32 = mybir.dt.uint32
ALU = mybir.AluOpType
ACT = mybir.ActivationFunctionType
AX = mybir.AxisListType

N, D = 625, 768
TP, NT = 125, 5
C = D // 128
EDGES = 20625
ET = EDGES // TP
HALF = 313
PACK = 4096
CHUNK, CHUNKS = 28, 5
LASTC = ET - CHUNK * CHUNKS
RING = 4
H, HD, M = 12, 64, 266
MC = 89
MP = 3 * MC
E, F = 16, 1536
FC = F // 128
LN_EPS, FEAT_EPS = 1e-5, 1e-4
NEG = -1e9
TOPK = 3
SLOTS = 128
BLOCKS = NT + (E - 1) + (N * TOPK - (E - 1)) // SLOTS
TW = BLOCKS + 2
ROUND = 12582912.0
EXPERT, LAST_OF, NEW_BEFORE, GROUP1, GROUP2 = range(5)
RMAX = bass.bass_isa.ReduceOp.max
TSPLIT = [(0, 320), (320, N)]
STG = 3


class Chain:

    def __init__(self, eng, sem, base=0):
        self.eng, self.sem, self.base, self.n = eng, sem, base, 0

    def __call__(self, ins):
        ins.then_inc(self.sem, 1)
        self.n += 1
        self.eng.wait_ge(self.sem, self.base + self.n)


def row(v):
    return v.rearrange("(a n) -> a n", a=1)


def rsqrt(dve, link, y, v, half, tmp):
    seed_i, v_i = y.bitcast(I32), v.bitcast(I32)
    link(dve.tensor_scalar(seed_i, v_i, 1, None, ALU.arith_shift_right))
    link(dve.tensor_scalar(seed_i, seed_i, -1.0, float(0x5F3759DF), ALU.mult, ALU.add))
    link(dve.tensor_scalar(half, v, -0.5, None, ALU.mult))
    for _ in range(3):
        link(dve.tensor_tensor(tmp, y, y, ALU.mult))
        link(dve.tensor_tensor(tmp, tmp, half, ALU.mult))
        link(dve.scalar_tensor_tensor(out=y, in0=tmp, scalar=1.5, in1=y, op0=ALU.add, op1=ALU.mult))


def gps_kernel(nc, x, src, dst, gnn_w, gnn_b, w_qkv, w_proj, b_proj, proj_mat, gate_w, gate_b,
               fc1_w, fc1_b, ln_w, ln_b, fc2_w, fc2_b, out, xn2_dram, table_dram):
    ctx = ExitStack()
    with ctx:
        base0 = (nc.sbuf_base + 31) // 32 * 32

        def at(name, offset, shape, dt=F32):
            return nc.alloc_sbuf_tensor_at(name, shape, dt, offset=base0 + offset)

        KB6 = F * 4
        w1hi = at("w1hi", 0, [128, C, F], F32R)
        w1lo = at("w1lo", 6 * KB6, [128, C, F], F32R)
        w2hi = at("w2hi", 12 * KB6, [128, FC, D], F32R)
        w2lo = at("w2lo", 18 * KB6, [128, FC, D], F32R)
        stage = at("stage", 24 * KB6, [128, STG, F])
        LOOP = 27 * KB6
        xg = at("xg", LOOP, [128, D])
        xthi = at("xthi", LOOP + 3072, [128, C, 128], F32R)
        xtlo = at("xtlo", LOOP + 6144, [128, C, 128], F32R)
        hid = at("hid", LOOP + 9216, [128, F])
        hthi = at("hthi", LOOP + 15360, [128, FC, 128], F32R)
        htlo = at("htlo", LOOP + 21504, [128, FC, 128], F32R)
        ysb = at("ysb", LOOP + 27648, [128, D])
        SMALL = LOOP + 30720 + 3104
        wqkv = at("wqkv", 0, [128, C, 3 * D])
        wg = at("wg", 55296, [128, C, D])
        kfeat = at("kfeat", 0, [TP, NT, H, MP])
        xnt = at("xnt", 73728, [128, C, N])
        kv = at("kv", 73728, [MC, H, 3, HD + 1])
        q1t = at("q1t", 83200, [MC, 3, 3, TP])
        aot = at("aot", 73728, [128, C, N])
        xn = at("xn", 88832, [TP, NT, D])
        ao = at("ao", 88832, [TP, NT, D])
        xn2 = at("xn2", 88832, [TP, NT, D])
        qt = at("qt", 104192, [128, C, N])
        xn2t = at("xn2t", 104192, [128, C, N])
        kt = at("kt", 119296, [128, C, N])
        q1 = [at("q1a", 119296, [TP, H, MP]), at("q1b", 132128, [TP, H, MP])]
        vext = at("vext", 134400, [TP, NT, H, HD + 1])
        adj = at("adj", 150016, [TP, NT, 2 * HALF])
        hrow = at("hrow", 162560, [TP, NT, D])
        wp = at("wp", 165888, [128, C, D])
        xs = at("xs", 184320, [TP, NT, D])
        ohs = at("ohs", 104192, [TP, RING, N], BF16)
        ohd = at("ohd", 109216, [TP, RING, HALF + 1], BF16)
        pk = at("pk", 111744, [TP, NT, HALF])
        pkh = at("pkh", 118016, [TP, NT, HALF])
        iota_n = at("iota_n", 124288, [TP, N], F16)
        iota_i = at("iota_i", 125568, [TP, N], I32)
        src_i = at("src_i", 128096, [TP, 2, ET], I32)
        ef = at("ef", 129440, [TP, 5, ET])
        bias2 = at("bias2", 132768, [TP, 2, D], F32)
        sq = at("sq", 64096, [128, 2, N])
        r0 = 119296

        def rt(name, shape, dt=F32):
            nonlocal r0
            size = 4 if dt != BF16 else 2
            t = at(name, r0, shape, dt)
            r0 += (math.prod(shape[1:]) * size + 31) // 32 * 32
            return t

        sc = rt("sc", [TP, NT, E])
        pr = rt("pr", [TP, NT, E])
        mx = rt("mx", [TP, NT])
        cmp1 = rt("cmp1", [TP, NT, E, E])
        cmp2 = rt("cmp2", [TP, NT, E, E])
        rank = rt("rank", [TP, NT, E])
        comb = rt("comb", [TP, NT, E])
        member = rt("member", [TP, NT, E], BF16)
        pos = rt("pos", [TP, NT, E])
        quo = rt("quo", [TP, NT, E])
        pick = rt("pick", [TP, 2, NT, E])
        slotf = rt("slotf", [TP, 4, NT])
        nblk = rt("nblk", [128, E])
        base = rt("base", [128, E])
        btmp = rt("btmp", [128, E, E])
        biota_i = rt("biota_i", [128, TW], I32)
        biota = rt("biota", [128, TW])
        bcmp = rt("bcmp", [128, TW, E])
        bsum = rt("bsum", [128, TW])
        single = rt("single", [128, E])
        gateb = rt("gateb", [TP, E])
        padt = rt("padt", [128, TW, 2], I32)
        padrow = rt("padrow", [1, D])
        assert r0 <= 147456
        bl = at("bl", 0, [80, F + D])
        bl2 = at("bl2", 9216, [80, F + D])
        bh = at("bh", 18432, [80, F + D], BF16)
        prow = at("prow", 138912, [MC, 3, 2 * HD])
        s0 = SMALL

        def small(name, shape, dt=F32):
            nonlocal s0
            size = 2 if dt in (BF16, F16) else 4
            t = at(name, s0, shape, dt)
            s0 += (math.prod(shape[1:]) * size + 31) // 32 * 32
            return t

        assert SMALL >= 184320 + NT * D * 4
        ident = small("ident", [128, 128])
        lnw = small("lnw", [128, E, FC])
        lnb = small("lnb", [128, E, FC])
        bsplit = small("bsplit", [128, F + D], BF16)
        selw = at("selw", s0, [128, E, 128], BF16)
        projt = at("projt", s0, [128, M])
        gatew = at("gatew", s0 + 1088, [128, C, E])
        nbias = at("nbias", s0 + 1472, [TP, 4, 60])
        sel2 = at("sel2", s0 + 2432, [128, 2])
        ones = at("ones", s0 + 2464, [128, 1])
        dinv = at("dinv", s0 + 2752, [TP, 5, NT])
        kmax = at("kmax", s0 + 2880, [128, 4])
        rden = at("rden", s0 + 2912, [TP, 6])
        prefix = at("prefix", s0 + 2944, [TP, 128], BF16)
        onesb = at("onesb", s0 + 3200, [TP, 128], BF16)
        kmax5 = at("kmax5", s0 + 3456, [TP, 5])
        s0 += 4096
        table = small("table", [128, TW, 2], I32)
        pair = at("pair", s0, [TP, 4, NT, 2], I32)
        slot = at("slot", s0 + 160, [TP, 4, NT], U32)
        tri = at("tri", s0 + 256, [128, E, E], BF16)
        s0 += 768
        btab = small("btab", [128, 5, TW + 1], I32)
        st6 = small("st6", [128, 3, 6])
        mv = small("mv", [128, 2])
        rs = small("rs", [128, 4])
        gidx = small("gidx", [128, 1], U32)
        sidx = small("sidx", [128, 2], U32)
        assert base0 + s0 <= nc.sbuf_usable_end, (base0 + s0, nc.sbuf_usable_end)

        bank = [ctx.enter_context(nc.psum_tensor(f"bank{b}", [128, 512], F32)) for b in range(8)]
        hid_ps = bank[0:3]
        tr_ps = bank[3:6]
        y_ps = bank[6:8]

        def sem(name):
            return ctx.enter_context(nc.semaphore(name))

        plan, uses, turn = {}, [0] * 8, 0

        def groups(keys, banks):
            nonlocal turn
            for key in keys:
                b = banks[turn % len(banks)]
                turn += 1
                uses[b] += 1
                plan[key] = (b, uses[b])

        R3, R8 = [5, 6, 7], list(range(8))
        T8 = [("c", c) for c in range(C)] + [("l", 0), ("l", 4)]
        groups([("pt", 0)], R3)
        groups([("xt",) + k for k in T8], R3)
        groups([("k", o, s) for o in range(C) for s in range(2)], R3)
        groups([("q", o, s) for o in range(C) for s in range(2)], R3)
        groups([("v", i, s) for i in range(NT) for s in range(2)], R3)
        groups([("deg", 0)], R3)
        groups([("h", i, s) for i in range(NT) for s in range(2)], R3)
        turn = 0
        groups([("sqk", 0), ("sqq", 0)], R8)
        groups([("ddk", i, h) for i in range(NT) for h in range(H)], R8)
        groups([("gnn", i, s) for i in range(NT) for s in range(2)], R8)
        groups([("kv", h) for h in range(H)], R8)

        def q_groups(i):
            groups([("ddq", i, h) for h in range(H)], R8)

        def o_groups(i):
            for g in range(2):
                for h in range(6 * g, 6 * g + 6):
                    groups([("q1t", i, h)], R8)
                groups([("o", i, g)], R8)

        q_groups(0)
        for i in range(NT):
            if i + 1 < NT:
                q_groups(i + 1)
            o_groups(i)
        groups([("at",) + k for k in T8], R8)
        groups([("pj", i, s) for i in range(NT) for s in range(2)], R8)
        groups([("x2",) + k for k in T8], R8)
        groups([("gate", 0), ("pos", 0), ("cnt", 0)], R8)

        full = [sem(f"full{b}") for b in range(8)]
        free = [sem(f"free{b}") for b in range(8)]

        def fill(pe, key):
            b, n = plan[key]
            if n > 1:
                pe.wait_ge(free[b], n - 1)
            return bank[b]

        def filled(last, key):
            last.then_inc(full[plan[key][0]], 1)

        def read(eng, key):
            b, n = plan[key]
            eng.wait_ge(full[b], n)
            return bank[b]

        def emptied(ins, key):
            ins.then_inc(free[plan[key][0]], 1)

        def sems(names):
            return [sem(n) for n in names.split()]

        ld_x, ld_idx, ld_bias, ld_qkv, ld_wg, ld_proj, ld_gate, ld_ln, ld_wp, ld_eb, ld_gb, ld_table = sems(
            "ld_x ld_idx ld_bias ld_qkv ld_wg ld_proj ld_gate ld_ln ld_wp ld_eb ld_gb ld_table")
        st_x1, st_xn2, st_pad, st_slot = sems("st_x1 st_xn2 st_pad st_slot")
        const_ok, route_const, sel_ok, dve_own, passed = sems("const_ok route_const sel_ok dve_own passed")
        xn_ok, x_biased, edges_ok, oh_free, oh_ready, adj_full, adj_read, unpacked, pk_free, adj_ok, deg_ok = sems(
            "xn_ok x_biased edges_ok oh_free oh_ready adj_full adj_read unpacked pk_free adj_ok deg_ok")
        xt_ok, vones_ok, sq_ok, sq_used, kmax_ok, kall_ok, kbias_ok, kexp_ok, k1_ok = sems(
            "xt_ok vones_ok sq_ok sq_used kmax_ok kall_ok kbias_ok kexp_ok k1_ok")
        qbias_ok, q1_ok, q1_free, q1t_used, ao_ok, bsplit_ok, bl_zero = sems("qbias_ok q1_ok q1_free q1t_used ao_ok bsplit_ok bl_zero")
        x1_ok, xn2_ok, pad_ok, sc_ok, ex_ok, member_ok, slots_ok, btab_ok = sems(
            "x1_ok xn2_ok pad_ok sc_ok ex_ok member_ok slots_ok btab_ok")
        ld_stage = [sem(f"ld_stage{s}") for s in range(STG)]
        w_hi, w_lo, w1_used, w2_used = sems("w_hi w_lo w1_used w2_used")
        gidx_ok, gathered, x_turned, xthi_ok, xtlo_ok = sems("gidx_ok gathered x_turned xthi_ok xtlo_ok")
        fc1_ok, gelu_ok, ln_own, ln_ok, h_turned, v_scaled, hthi_ok, htlo_ok = sems(
            "fc1_ok gelu_ok ln_own ln_ok h_turned v_scaled hthi_ok htlo_ok")
        fc2_ok, y_ok, sidx_ok, scattered = sems("fc2_ok y_ok sidx_ok scattered")

        def done(eng, key):
            b, n = plan[key]
            eng.wait_ge(full[b], n)

        def taken(eng, key):
            b, n = plan[key]
            eng.wait_ge(free[b], n)

        def turn_tokens(pe, name, rows, ready, per_tile):
            for kind, k in T8:
                ps = fill(pe, (name, kind, k))
                if kind == "c":
                    todo = [(k, i, i) for i in range(4)]
                else:
                    todo = [(c, 4, c - k) for c in range(k, min(C, k + 4))]
                for c, i, place in todo:
                    pe.wait_ge(ready, per_tile * (i + 1))
                    last = pe.transpose(ps[:, place * TP:(place + 1) * TP], rows[:, i, c::C], ident[0:TP, 0:TP])
                filled(last, (name, kind, k))

        def take_turned(act, name, to):
            for kind, k in T8:
                ps = read(act, (name, kind, k))
                if kind == "c":
                    ins = act.activation(to[:, k, 0:4 * TP], ps[:, 0:4 * TP], ACT.Copy)
                else:
                    n = min(C, k + 4) - k
                    ins = act.activation(to[:, k:k + n, 4 * TP:N],
                                         ps[:, 0:n * TP].rearrange("p (c t) -> p c t", t=TP), ACT.Copy)
                emptied(ins, (name, kind, k))

        def all_turned(eng, name):
            for kind, k in T8:
                taken(eng, (name, kind, k))

        def edge(plane, t):
            return ef[:, plane, bass.ds(t, 1)]

        def take_q1t(eng, i, h, copy):
            n = H * i + h
            ps = read(eng, ("q1t", i, h))
            if n >= 3:
                eng.wait_ge(q1t_used, n - 2)
            emptied(copy(q1t[:, n % 3, :, :], ps[0:MC, 0:3 * TP].rearrange("p (m t) -> p m t", m=3)), ("q1t", i, h))

        def target(parts, u):
            w1, w2, second = parts
            return w2[:, 2 * u:2 * u + 2, :].rearrange("p c n -> p (c n)") if second else w1[:, u, :]

        def split_hi(act, second, g, u):
            act.wait_ge(ld_stage[u % STG], 16 * (C // STG * g + u // STG + 1))
            act.activation(target((w1hi, w2hi, second), u), stage[:, u % STG, :], ACT.Copy).then_inc(w_hi, 1)

        def split_lo(dve, second, g, u):
            dve.wait_ge(w_hi, C * g + u + 1)
            dve.tensor_tensor(target((w1lo, w2lo, second), u), stage[:, u % STG, :],
                              target((w1hi, w2hi, second), u).bitcast(F32), ALU.subtract).then_inc(w_lo, 1)

        def entry(eng, r, j, top):
            return eng.value_load(btab[0:1, r, bass.ds(j, 1)], min_val=0, max_val=top)

        block = ctx.enter_context(nc.Block())

        @block.sync
        def _(sp):
            sp.dma_start(src_i[:, 0, :], src.rearrange("(p k) -> p k", p=TP)).then_inc(ld_idx, 16)
            sp.dma_start(src_i[:, 1, :], dst.rearrange("(p k) -> p k", p=TP)).then_inc(ld_idx, 16)
            sp.dma_start(xs[:, :, :], x.rearrange("(i p) d -> p i d", p=TP)).then_inc(ld_x, 16)
            sp.dma_start(bias2[:, 0, :], row(gnn_b).broadcast_to([TP, D])).then_inc(ld_bias, 16)
            sp.dma_start(bias2[:, 1, :], row(b_proj).broadcast_to([TP, D])).then_inc(ld_bias, 16)
            for m in range(3):
                rows = min(MC, M - MC * m)
                for half in range(2):
                    sp.dma_start(prow[0:rows, m, HD * half:HD * half + HD],
                                 proj_mat[MC * m:MC * m + rows, :]).then_inc(ld_proj, 16)
            sp.dma_start(wqkv[:, :, :], w_qkv.rearrange("(p c) n -> p c n", c=C)).then_inc(ld_qkv, 16)
            sp.dma_start(wg[:, :, :], gnn_w.rearrange("(p c) n -> p c n", c=C)).then_inc(ld_wg, 16)
            sp.dma_start(gatew[:, :, :], gate_w.rearrange("(p c) n -> p c n", c=C)).then_inc(ld_gate, 16)
            sp.dma_start(lnw[:, :, :], ln_w.rearrange("e (p c) -> p e c", c=FC)).then_inc(ld_ln, 16)
            sp.dma_start(lnb[:, :, :], ln_b.rearrange("e (p c) -> p e c", c=FC)).then_inc(ld_ln, 16)
            done(sp, ("gnn", NT - 1, 1))
            sp.dma_start(wp[:, :, :], w_proj.rearrange("(p c) n -> p c n", c=C)).then_inc(ld_wp, 16)
            sp.wait_ge(bl_zero, 1)
            for g in range(3):
                sp.dma_start(bl[32 * g:32 * g + E, 0:F], fc1_b).then_inc(ld_eb, 16)
                sp.dma_start(bl[32 * g:32 * g + E, F:F + D], fc2_b).then_inc(ld_eb, 16)

            fc1_units = fc1_w.rearrange("e (p c) n -> e p c n", c=C)
            fc2_units = fc2_w.rearrange("e (p c) n -> e p (c n)", c=FC)

            def load(second, e, g, units):
                for u in units:
                    sp.wait_ge(w_lo, C * g + u + 1)
                    of = fc2_units[bass.ds(e, 1), :, F * u:F * u + F] if second else fc1_units[bass.ds(e, 1), :, u, :]
                    sp.dma_start(stage[:, u % STG, :], of.rearrange("a p n -> (a p) n")).then_inc(ld_stage[u % STG], 16)

            load(False, 0, 0, range(C))
            load(True, 0, 1, range(STG))
            done(sp, ("o", NT - 1, 1))
            sp.dma_start(gateb[:, :], row(gate_b).broadcast_to([TP, E])).then_inc(ld_gb, 16)
            for i in range(NT):
                sp.wait_ge(x1_ok, i + 1)
                sp.dma_start(out[TP * i:TP * i + TP, :], xs[:, i, :]).then_inc(st_x1, 16)
                sp.wait_ge(xn2_ok, i + 1)
                sp.dma_start(xn2_dram[TP * i:TP * i + TP, :], xn2[:, i, :]).then_inc(st_xn2, 16)
            sp.wait_ge(pad_ok, 1)
            sp.dma_start(xn2_dram[N:N + 1, :], padrow[0:1, :]).then_inc(st_xn2, 16)
            sp.wait_ge(route_const, 2)
            sp.dma_start(table_dram.rearrange("(p w) a -> p w a", p=128), padt[:, :, :]).then_inc(st_pad, 16)
            sp.wait_ge(st_slot, 16 * 4 * NT)
            sp.dma_start(table[:, :, :], table_dram.rearrange("(p w) a -> p w a", p=128)).then_inc(ld_table, 16)
            load(True, 0, 1, range(STG, C))
            sp.wait_ge(btab_ok, 1)
            nb = sp.value_load(btab[0:1, LAST_OF, TW:TW + 1], min_val=NT + E - 1, max_val=BLOCKS)

            def load_second(j):
                with sp.If(entry(sp, NEW_BEFORE, j, 1)):
                    e = entry(sp, EXPERT, j - 1, E - 1)
                    load(True, e, entry(sp, GROUP2, e, 2 * E), range(C))

            with sp.Fori(1, nb) as j:
                load_second(j)
                with sp.If(entry(sp, LAST_OF, j, 1)):
                    e = entry(sp, EXPERT, j + 1, E - 1)
                    load(False, e, entry(sp, GROUP1, e, 2 * E), range(C))
            load_second(nb)
            sp.wait_ge(st_x1, 16 * NT)

        @block.gpsimd
        def _(pool):
            pool.iota(iota_i[:, :], [[1, N]], base=0, channel_multiplier=0)
            pool.memset(ident[:, :], 0.0)
            pool.memset(onesb[:, :], 1.0)
            pool.memset(prefix[:, :], 1.0)
            pool.memset(tri[:, :, :], 1.0)
            pool.memset(ones[:, :], 1.0)
            pool.memset(sel2[:, :], 0.0)
            pool.memset(bsplit[:, :], 0.0)
            pool.memset(adj[:, :, :], 0.0).then_inc(const_ok, 1)
            pool.wait_ge(const_ok, 1)
            pool.affine_select(out=ident[:, :], in_=ident[:, :], compare_op=ALU.not_equal, fill=1.0, base=0,
                               pattern=[[-1, 128]], channel_multiplier=1)
            pool.affine_select(out=prefix[:, :], in_=prefix[:, :], compare_op=ALU.is_ge, fill=0.0, base=-1,
                               pattern=[[1, 128]], channel_multiplier=-1)
            pool.affine_select(out=tri[:, :, :], in_=tri[:, :, :], compare_op=ALU.is_ge, fill=0.0, base=-1,
                               pattern=[[1, E], [-1, E]], channel_multiplier=0)
            pool.memset(sel2[0:64, 0:1], 0.5).then_inc(const_ok, 1)
            pool.wait_ge(const_ok, 2)
            pool.memset(sel2[64:128, 1:2], 0.5).then_inc(const_ok, 1)
            pool.wait_ge(ld_bias, 32)
            pool.wait_ge(xn_ok, NT)
            for i in range(NT):
                for b in range(2):
                    pool.tensor_tensor(xs[:, i, :], xs[:, i, :], bias2[:, b, :], ALU.add).then_inc(x_biased, 1)
                    pool.wait_ge(x_biased, 2 * i + b + 1)
            pool.wait_ge(adj_ok, 1)
            done(pool, ("pt", 0))
            pool.memset(vext[:, :, :, HD:HD + 1], 1.0).then_inc(vones_ok, 1)
            pool.wait_ge(kmax_ok, 1)
            pool.partition_all_reduce(kmax[0:TP, 1:2], kmax[0:TP, 0:1], TP, RMAX).then_inc(kall_ok, 1)
            done(pool, ("kv", H - 1))
            pool.memset(bl[:, :], 0.0).then_inc(bl_zero, 1)
            done(pool, ("o", NT - 1, 1))
            pool.iota(biota_i[:, :], [[1, TW]], base=0, channel_multiplier=0)
            pool.memset(padrow[0:1, :], 0.0).then_inc(pad_ok, 1)
            pool.iota(padt[:, :, 0], [[0, TW]], base=N, channel_multiplier=0)
            pool.memset(padt[:, :, 1], 0)
            pool.iota(pair[:, :, :, 0], [[0, 4], [TP, NT]], base=0, channel_multiplier=1).then_inc(route_const, 2)
            pool.wait_ge(slots_ok, 1)
            pool.wait_ge(st_pad, 16)
            for k in range(4):
                for i in range(NT):
                    pool.indirect_dma_start(
                        out=table_dram, out_offset=bass.IndirectOffsetOnAxis(ap=slot[:, k, i:i + 1], axis=0),
                        in_=pair[:, k, i, :], in_offset=None).then_inc(st_slot, 16)
            done(pool, ("cnt", 0))
            pool.wait_ge(btab_ok, 1)
            pool.memset(selw[:, :, :], 0.0).then_inc(sel_ok, 1)
            for g in range(3):
                pool.wait_ge(sel_ok, g + 1)
                pool.affine_select(out=selw[:, :, :], in_=selw[:, :, :], compare_op=ALU.not_equal, fill=1.0,
                                   base=-32 * g, pattern=[[-1, E], [0, 128]], channel_multiplier=1).then_inc(sel_ok, 1)

            pool.wait_ge(ld_table, 16)
            pool.wait_ge(st_xn2, 16 * (NT + 1))
            pool.wait_ge(st_x1, 16 * NT)
            taken(pool, ("pj", NT - 1, 1))

            def gather(b):
                pool.tensor_copy(gidx[:, 0:1], table[:, bass.ds(b, 1), 0]).then_inc(gidx_ok, 1)
                pool.wait_ge(gidx_ok, b + 1)
                pool.sem_inc(passed, 1)
                pool.indirect_dma_start(out=xg[:, :], out_offset=None, in_=xn2_dram,
                                        in_offset=bass.IndirectOffsetOnAxis(ap=gidx[:, 0:1], axis=0)).then_inc(gathered, 16)

            def scatter(j):
                pool.tensor_copy(sidx[:, :], table[:, bass.ds(j - 1, 1), :].rearrange("p w a -> p (w a)")).then_inc(sidx_ok, 1)
                pool.wait_ge(y_ok, j + 1)
                pool.sem_inc(passed, 1)
                pool.indirect_dma_start(out=out, out_offset=bass.IndirectOffsetOnAxis(ap=sidx[:, 0:1], axis=0),
                                        in_=ysb[:, :], in_offset=None, bounds_check=N - 1, oob_is_err=False,
                                        compute_op=ALU.add).then_inc(scattered, 16)
                pool.wait_ge(scattered, 16 * j)

            gather(0)
            for b in range(1, 3):
                pool.wait_ge(x_turned, b)
                pool.wait_ge(gathered, 16 * b)
                gather(b)
            nb = pool.value_load(btab[0:1, LAST_OF, TW:TW + 1], min_val=NT + E - 1, max_val=BLOCKS)
            with pool.Fori(1, nb) as j:
                pool.wait_ge(x_turned, j + 2)
                pool.wait_ge(gathered, 16 * j + 32)
                gather(j + 2)
                scatter(j)
            scatter(nb)
            pool.wait_ge(gathered, 16 * nb + 32)

        @block.vector
        def _(dve):
            link = Chain(dve, dve_own)
            dve.wait_ge(ld_idx, 32)
            dve.tensor_copy(ef[:, 0, :], src_i[:, 0, :])
            link(dve.tensor_copy(ef[:, 1, :], src_i[:, 1, :]))
            link(dve.tensor_scalar(ef[:, 2, :], ef[:, 1, :], float(HALF), None, ALU.is_ge))
            dve.scalar_tensor_tensor(out=ef[:, 3, :], in0=ef[:, 2, :], scalar=-float(HALF), in1=ef[:, 1, :],
                                     op0=ALU.mult, op1=ALU.add)
            link(dve.tensor_scalar(ef[:, 4, :], ef[:, 2, :], PACK - 1.0, 1.0, ALU.mult, ALU.add))
            dve.wait_ge(const_ok, 3)
            link(dve.tensor_copy(iota_n[:, :], iota_i[:, :]))

            def norm(rows, to, p, own):
                width = rows.shape[-1]
                step = 512 if width % 512 == 0 else 384
                parts = width // step
                for n in range(parts):
                    last = dve.bn_stats(st6[0:p, n, :], rows[:, n * step:(n + 1) * step])
                own(last)
                dve.sem_inc(passed, 1)
                own(dve.bn_aggr(mv[0:p, :], st6[0:p, 0:parts, :]))
                own(dve.tensor_scalar(rs[0:p, 0:1], mv[0:p, 1:2], LN_EPS, None, ALU.add))
                rsqrt(dve, own, rs[0:p, 3:4], rs[0:p, 0:1], rs[0:p, 1:2], rs[0:p, 2:3])
                return dve.tensor_scalar(to, rows, mv[0:p, 0:1], rs[0:p, 3:4], ALU.subtract, ALU.mult)

            dve.wait_ge(ld_x, 16)
            for i in range(NT):
                norm(xs[:, i, :], xn[:, i, :], TP, link).then_inc(xn_ok, 1)

            def unpack(c, step):
                lo, hi = adj[:, :, 0:HALF], adj[:, :, HALF:2 * HALF]
                if step == 0:
                    dve.wait_ge(adj_read, NT * c + NT)
                    dve.tensor_scalar(pkh[:, :, :], pk[:, :, :], 1.0 / PACK, -0.4375, ALU.mult, ALU.add).then_inc(unpacked, 1)
                elif step == 1:
                    dve.wait_ge(unpacked, 3 * c - 2)
                    dve.tensor_scalar(pkh[:, :, :], pkh[:, :, :], ROUND, ROUND, ALU.add, ALU.subtract).then_inc(unpacked, 1)
                elif step == 2:
                    dve.wait_ge(unpacked, 3 * c - 1)
                    dve.scalar_tensor_tensor(out=pk[:, :, :], in0=pkh[:, :, :], scalar=-float(PACK), in1=pk[:, :, :],
                                             op0=ALU.mult, op1=ALU.add).then_inc(unpacked, 1)
                elif step == 3:
                    dve.wait_ge(pk_free, 2 * c - 1)
                    dve.tensor_tensor(hi, hi, pkh[:, :, :], ALU.add).then_inc(pk_free, 1)
                else:
                    dve.wait_ge(unpacked, 3 * c)
                    dve.tensor_tensor(lo, lo, pk[:, :, :], ALU.add).then_inc(pk_free, 1)

            def one_hots(c, tiles, before):
                for k in range(tiles):
                    t = CHUNK * c + k
                    dve.wait_ge(oh_free, t + 1)
                    dve.tensor_scalar(ohs[:, k % RING, :], iota_n[:, :], edge(0, t), None, ALU.is_equal)
                    dve.tensor_scalar(ohd[:, k % RING, 0:HALF], iota_n[:, 0:HALF], edge(3, t), edge(4, t),
                                      ALU.is_equal, ALU.mult).then_inc(oh_ready, 1)
                    if before and k >= 6 and k % 4 == 2 and k < 26:
                        unpack(c, (k - 6) // 4)

            dve.wait_ge(const_ok, 3)
            dve.sem_inc(pk_free, 1)
            one_hots(0, CHUNK, False)
            with dve.Fori(1, CHUNKS) as c:
                one_hots(c, CHUNK, True)
            one_hots(CHUNKS, LASTC, True)
            for step in range(5):
                unpack(CHUNKS + 1, step)
            dve.wait_ge(pk_free, 2 * CHUNKS + 3)
            for b in range(NT):
                last = dve.tensor_tensor(adj[:, b, TP * b:TP * b + TP], adj[:, b, TP * b:TP * b + TP],
                                         ident[0:TP, 0:TP], ALU.add)
            last.then_inc(adj_ok, 1)

            ps = read(dve, ("deg", 0))
            emptied(dve.tensor_copy(dinv[:, 0, :], ps[0:TP, 0:NT]), ("deg", 0))
            taken(dve, ("deg", 0))
            rsqrt(dve, link, dinv[:, 3, :], dinv[:, 0, :], dinv[:, 1, :], dinv[:, 2, :])
            for i in range(NT):
                for s in range(2):
                    ps = read(dve, ("h", i, s))
                    emptied(dve.tensor_scalar(hrow[:, i, 384 * s:384 * s + 384], ps[0:TP, 0:384], dinv[:, 3, i:i + 1],
                                              None, ALU.mult), ("h", i, s))

            for n, name in ((0, "sqk"), (1, "sqq")):
                ps = read(dve, (name, 0))
                emptied(dve.tensor_copy(nbias[:, n, :], ps[0:TP, 0:60]), (name, 0))
            for i in range(NT):
                taken(dve, ("ddk", i, H - 1))
                last = dve.tensor_reduce(kmax5[:, i:i + 1], kfeat[:, i, :, 0:M], AX.XY, ALU.max)
            link(last)
            dve.tensor_reduce(kmax[0:TP, 0:1], kmax5[:, :], AX.X, ALU.max).then_inc(kmax_ok, 1)
            dve.wait_ge(kall_ok, 1)
            taken(dve, ("sqk", 0))
            taken(dve, ("sqq", 0))
            dve.tensor_scalar(nbias[:, 2, :], nbias[:, 0, :], -1.0, kmax[0:TP, 1:2], ALU.mult, ALU.subtract).then_inc(kbias_ok, 1)

            ratio = 1.0 / math.sqrt(M)
            dve.wait_ge(x_biased, 2 * NT)
            for i in range(NT):
                for s in range(2):
                    ps = read(dve, ("gnn", i, s))
                    part = xs[:, i, 384 * s:384 * s + 384]
                    emptied(dve.scalar_tensor_tensor(out=part, in0=ps[0:TP, 0:384], scalar=dinv[:, 3, i:i + 1], in1=part,
                                                     op0=ALU.mult, op1=ALU.add), ("gnn", i, s))
                dve.wait_ge(kexp_ok, i + 1)
                feat = kfeat[:, i, :, 0:M]
                dve.memset(kfeat[:, i, :, M:MP], 0.0)
                dve.tensor_scalar(feat, feat, FEAT_EPS, ratio, ALU.add, ALU.mult).then_inc(k1_ok, 1)
            for h in range(H):
                ps = read(dve, ("kv", h))
                emptied(dve.tensor_copy(kv[:, h, :, :], ps[0:MC, 0:3 * (HD + 1)].rearrange("p (m d) -> p m d", m=3)), ("kv", h))

            def q_bias(i):
                for h in range(H):
                    ps = read(dve, ("ddq", i, h))
                    n = H * i + h
                    link(dve.tensor_reduce(nbias[:, 3, n:n + 1], ps[0:TP, 0:M], AX.X, ALU.max, negate=True))
                    dve.tensor_tensor(nbias[:, 3, n:n + 1], nbias[:, 3, n:n + 1], nbias[:, 1, n:n + 1],
                                      ALU.subtract).then_inc(qbias_ok, 1)

            def q_features(i):
                taken(dve, ("ddq", i, H - 1))
                feat = q1[i % 2][:, :, 0:M]
                dve.memset(q1[i % 2][:, :, M:MP], 0.0)
                dve.tensor_scalar(feat, feat, FEAT_EPS, ratio, ALU.add, ALU.mult).then_inc(q1_ok, 1)

            q_bias(0)
            q_features(0)
            for i in range(NT):
                if i + 1 < NT:
                    q_bias(i + 1)
                for h in range(H):
                    if h % 2:
                        take_q1t(dve, i, h, lambda o, a: dve.tensor_copy(o, a))
                    if h % 6 == 5:
                        g = h // 6
                        ps = read(dve, ("o", i, g))
                        sums = ps[0:TP, 0:6 * (HD + 1)].rearrange("p (h d) -> p h d", h=6)
                        link(dve.reciprocal(rden[:, :], sums[:, :, HD]))
                        emptied(dve.tensor_tensor(
                            ao[:, i, 384 * g:384 * g + 384].rearrange("p (h d) -> p h d", h=6), sums[:, :, 0:HD],
                            rden[:, :].unsqueeze(2).broadcast_to([TP, 6, HD]), ALU.mult), ("o", i, g))
                if i + 1 < NT:
                    q_features(i + 1)

            dve.wait_ge(ld_eb, 96)
            link(dve.tensor_copy(bh[:, :], bl[:, :]))
            link(dve.tensor_tensor(bl2[:, :], bl[:, :], bh[:, :], ALU.subtract))
            dve.tensor_copy(bsplit[0:E, :], bl[0:E, :])
            dve.tensor_copy(bsplit[32:32 + E, :], bl2[32:32 + E, :])
            link(dve.tensor_copy(bh[64:64 + E, :], bl2[64:64 + E, :]))
            link(dve.tensor_tensor(bl[64:64 + E, :], bl2[64:64 + E, :], bh[64:64 + E, :], ALU.subtract))
            dve.tensor_copy(bsplit[64:64 + E, :], bl[64:64 + E, :]).then_inc(bsplit_ok, 1)
            dve.sem_inc(w_lo, STG)
            for u in range(C):
                split_lo(dve, False, 0, u)

            for i in range(NT):
                for s in range(2):
                    ps = read(dve, ("pj", i, s))
                    part = xs[:, i, 384 * s:384 * s + 384]
                    last = dve.tensor_tensor(part, ps[0:TP, 0:384], part, ALU.add)
                    emptied(last, ("pj", i, s))
                taken(dve, ("pj", i, 1))
                dve.sem_inc(x1_ok, 1)
                norm(xs[:, i, :], xn2[:, i, :], TP, link).then_inc(xn2_ok, 1)

            ps = read(dve, ("gate", 0))
            dve.wait_ge(ld_gb, 16)
            link(dve.tensor_tensor(sc[:, :, :], ps[0:TP, 0:NT * E].rearrange("p (i e) -> p i e", e=E),
                                   gateb[:, :].unsqueeze(1).broadcast_to([TP, NT, E]), ALU.add))
            dve.sem_inc(free[plan[("gate", 0)][0]], 1)
            link(dve.memset(sc[:, :, 0:1], NEG))
            link(dve.tensor_reduce(mx[:, :], sc[:, :, :], AX.X, ALU.max))
            dve.tensor_tensor(sc[:, :, :], sc[:, :, :], mx[:, :].unsqueeze(2).broadcast_to([TP, NT, E]),
                              ALU.subtract).then_inc(sc_ok, 1)
            dve.wait_ge(ex_ok, 1)
            link(dve.tensor_reduce(mx[:, :], sc[:, :, :], AX.X, ALU.add))
            link(dve.reciprocal(mx[:, :], mx[:, :]))
            link(dve.tensor_tensor(pr[:, :, :], sc[:, :, :], mx[:, :].unsqueeze(2).broadcast_to([TP, NT, E]), ALU.mult))
            mine = pr[:, :, :].unsqueeze(3).broadcast_to([TP, NT, E, E])
            other = pr[:, :, :].unsqueeze(2).broadcast_to([TP, NT, E, E])
            before = tri[0:TP, :, :].unsqueeze(1).broadcast_to([TP, NT, E, E])
            dve.tensor_tensor(cmp1[:, :, :, :], other, mine, ALU.is_gt)
            link(dve.tensor_tensor(cmp2[:, :, :, :], other, mine, ALU.is_equal))
            link(dve.tensor_tensor(cmp2[:, :, :, :], cmp2[:, :, :, :], before, ALU.mult))
            link(dve.tensor_tensor(cmp1[:, :, :, :], cmp1[:, :, :, :], cmp2[:, :, :, :], ALU.add))
            link(dve.tensor_reduce(rank[:, :, :], cmp1[:, :, :, :], AX.X, ALU.add))
            link(dve.tensor_scalar(member[:, :, :], rank[:, :, :], float(TOPK), None, ALU.is_lt))
            link(dve.tensor_tensor(comb[:, :, :], member[:, :, :], pr[:, :, :], ALU.mult))
            link(dve.tensor_scalar(comb[:, :, 0:1], comb[:, :, 0:1], 1.0, None, ALU.add))
            dve.memset(member[:, :, 0:1], 1.0).then_inc(member_ok, 1)
            ps = read(dve, ("cnt", 0))
            link(dve.tensor_scalar(nblk[:, :], ps[:, 0:E], 1.0 / SLOTS, (SLOTS - 1.0) / SLOTS - 0.5 + 0.5 / SLOTS,
                                   ALU.mult, ALU.add))
            dve.sem_inc(free[plan[("cnt", 0)][0]], 1)
            link(dve.tensor_scalar(nblk[:, :], nblk[:, :], ROUND, ROUND, ALU.add, ALU.subtract))
            link(dve.tensor_scalar(nblk[:, :], nblk[:, :], 1.0, None, ALU.max))
            link(dve.tensor_tensor(btmp[:, :, :], tri[:, :, :], nblk[:, :].unsqueeze(1).broadcast_to([128, E, E]), ALU.mult))
            link(dve.tensor_reduce(base[:, :], btmp[:, :, :], AX.X, ALU.add))
            ps = read(dve, ("pos", 0))
            link(dve.tensor_copy(pos[:, :, :], ps[0:TP, 0:NT * E].rearrange("p (i e) -> p i e", e=E)))
            dve.sem_inc(free[plan[("pos", 0)][0]], 1)
            link(dve.tensor_scalar(quo[:, :, :], pos[:, :, :], 1.0 / SLOTS, -0.5 + 0.5 / SLOTS, ALU.mult, ALU.add))
            link(dve.tensor_scalar(quo[:, :, :], quo[:, :, :], ROUND, ROUND, ALU.add, ALU.subtract))
            link(dve.tensor_scalar(quo[:, :, :], quo[:, :, :], 1.0 - SLOTS * TW, None, ALU.mult))
            link(dve.scalar_tensor_tensor(out=pos[:, :, :], in0=pos[:, :, :], scalar=float(TW), in1=quo[:, :, :],
                                          op0=ALU.mult, op1=ALU.add))
            link(dve.tensor_tensor(pos[:, :, :], pos[:, :, :], base[0:TP, :].unsqueeze(1).broadcast_to([TP, NT, E]), ALU.add))
            dve.wait_ge(route_const, 2)
            wcol = pair[:, :, :, 1].bitcast(F32)
            for k in range(TOPK):
                dve.scalar_tensor_tensor(out=pick[:, 0, :, :], in0=rank[:, :, :], scalar=float(k), in1=pos[:, :, :],
                                         op0=ALU.is_equal, op1=ALU.mult)
                link(dve.scalar_tensor_tensor(out=pick[:, 1, :, :], in0=rank[:, :, :], scalar=float(k), in1=comb[:, :, :],
                                              op0=ALU.is_equal, op1=ALU.mult))
                dve.tensor_reduce(slotf[:, k, :], pick[:, 0, :, :], AX.X, ALU.add)
                link(dve.tensor_reduce(wcol[:, k, :], pick[:, 1, :, :], AX.X, ALU.add))
            dve.tensor_copy(wcol[:, TOPK, :], comb[:, :, 0])
            link(dve.tensor_copy(slotf[:, TOPK, :], pos[:, :, 0]))
            dve.tensor_copy(slot[:, :, :], slotf[:, :, :]).then_inc(slots_ok, 1)
            link(dve.tensor_copy(biota[:, :], biota_i[:, :]))
            link(dve.tensor_tensor(bcmp[:, :, :], base[:, :].unsqueeze(1).broadcast_to([128, TW, E]),
                                   biota[:, :].unsqueeze(2).broadcast_to([128, TW, E]), ALU.is_le))
            link(dve.tensor_reduce(bsum[:, :], bcmp[:, :, :], AX.X, ALU.add))
            dve.tensor_scalar(btab[:, EXPERT, 0:TW], bsum[:, :], -1.0, None, ALU.add)
            dve.tensor_tensor(btab[:, LAST_OF, 0:TW - 1], bsum[:, 1:TW], bsum[:, 0:TW - 1], ALU.subtract)
            dve.memset(btab[:, NEW_BEFORE, 0:2], 0)
            dve.tensor_tensor(btab[:, NEW_BEFORE, 2:TW], bsum[:, 1:TW - 1], bsum[:, 0:TW - 2], ALU.subtract)
            dve.tensor_tensor(btab[:, LAST_OF, TW:TW + 1], base[:, E - 1:E], nblk[:, E - 1:E], ALU.add)
            dve.memset(single[:, E - 1:E], 0.0)
            link(dve.tensor_scalar(single[:, 0:E - 1], nblk[:, 0:E - 1], 1.0, None, ALU.is_equal))
            dve.memset(btab[:, GROUP1, 0:1], 0)
            link(dve.scalar_tensor_tensor(out=btab[:, GROUP1, 1:E], in0=biota[:, 1:E], scalar=2.0, in1=single[:, 0:E - 1],
                                          op0=ALU.mult, op1=ALU.subtract))
            link(dve.tensor_scalar(single[:, :], single[:, :], 1.0, None, ALU.add))
            dve.scalar_tensor_tensor(out=btab[:, GROUP2, 0:E], in0=biota[:, 0:E], scalar=2.0, in1=single[:, :],
                                     op0=ALU.mult, op1=ALU.add).then_inc(btab_ok, 1)

            STEPS = 15

            def hidden_parts(j, e):
                dve.wait_ge(h_turned, j)
                for c in range(FC):
                    last = dve.tensor_scalar(hid[:, 128 * c:128 * c + 128], tr_ps[c // 4][:, 128 * (c % 4):128 * (c % 4) + 128],
                                             lnw[:, bass.ds(e, 1), c], lnb[:, bass.ds(e, 1), c], ALU.mult, ALU.add)
                last.then_inc(v_scaled, 1)
                dve.wait_ge(hthi_ok, j)
                dve.tensor_tensor(htlo[:, :, :].rearrange("p c t -> p (c t)"), hid[:, :],
                                  hthi[:, :, :].rearrange("p c t -> p (c t)").bitcast(F32), ALU.subtract).then_inc(htlo_ok, 1)

            def normalise(j):
                dve.wait_ge(gelu_ok, 3 * j + 3)
                norm(hid[:, :], hid[:, :], 128, Chain(dve, ln_own, STEPS * j)).then_inc(ln_ok, 1)

            def x_low(b):
                dve.wait_ge(xthi_ok, b + 1)
                dve.tensor_tensor(xtlo[:, 0:4, :].rearrange("p c t -> p (c t)"), tr_ps[0][:, :],
                                  xthi[:, 0:4, :].rearrange("p c t -> p (c t)").bitcast(F32), ALU.subtract)
                dve.tensor_tensor(xtlo[:, 4:6, :].rearrange("p c t -> p (c t)"), tr_ps[1][:, 0:256],
                                  xthi[:, 4:6, :].rearrange("p c t -> p (c t)").bitcast(F32), ALU.subtract).then_inc(xtlo_ok, 1)

            def split_second(j):
                with dve.If(entry(dve, NEW_BEFORE, j, 1)):
                    g = entry(dve, GROUP2, entry(dve, EXPERT, j - 1, E - 1), 2 * E)
                    for u in range(C):
                        split_lo(dve, True, g, u)

            x_low(0)
            for u in range(C):
                split_lo(dve, True, 1, u)
            normalise(0)
            x_low(1)
            dve.wait_ge(ld_ln, 32)
            dve.wait_ge(btab_ok, 1)
            nb = dve.value_load(btab[0:1, LAST_OF, TW:TW + 1], min_val=NT + E - 1, max_val=BLOCKS)
            with dve.Fori(1, nb) as j:
                hidden_parts(j, entry(dve, EXPERT, j - 1, E - 1))
                split_second(j)
                normalise(j)
                x_low(j + 1)
                with dve.If(entry(dve, LAST_OF, j, 1)):
                    g = entry(dve, GROUP1, entry(dve, EXPERT, j + 1, E - 1), 2 * E)
                    for u in range(C):
                        split_lo(dve, False, g, u)
            hidden_parts(nb, E - 1)
            split_second(nb)

        @block.scalar
        def _(act):
            ps = read(act, ("pt", 0))
            emptied(act.activation(projt[:, :], ps[:, 0:M], ACT.Copy), ("pt", 0))
            take_turned(act, "xt", xnt)

            def counts(c):
                act.wait_ge(adj_full, c + 1)
                act.wait_ge(pk_free, 2 * c + 1)
                for b in range(NT):
                    act.activation(pk[:, b, :], bank[b][0:TP, 0:HALF], ACT.Copy).then_inc(adj_read, 1)

            counts(0)
            with act.Fori(1, CHUNKS) as c:
                counts(c)
            counts(CHUNKS)
            act.wait_ge(adj_ok, 1)
            act.wait_ge(x_biased, 2 * NT)
            for name, to in (("k", kt), ("q", qt)):
                for o in range(C):
                    for s, (a, b) in enumerate(TSPLIT):
                        ps = read(act, (name, o, s))
                        emptied(act.activation(to[:, o, a:b], ps[:, 0:b - a], ACT.Copy, scale=HD ** -0.25), (name, o, s))
            act.wait_ge(x_biased, 2 * NT)
            for i in range(NT):
                for s in range(2):
                    ps = read(act, ("v", i, s))
                    emptied(act.activation(vext[:, i, 6 * s:6 * s + 6, 0:HD],
                                           ps[0:TP, 0:384].rearrange("p (h d) -> p h d", d=HD), ACT.Copy), ("v", i, s))
            done(act, ("h", NT - 1, 1))
            for n, (name, of) in enumerate((("k", kt), ("q", qt))):
                for o in range(C):
                    taken(act, (name, o, 1))
                    taken(act, (name, o, 0))
                    g = C * n + o
                    if g >= 2:
                        act.wait_ge(sq_used, g - 1)
                    act.activation(sq[:, g % 2, :], of[:, o, :], ACT.Square).then_inc(sq_ok, 1)
            for i in range(NT):
                for h in range(H):
                    ps = read(act, ("ddk", i, h))
                    emptied(act.activation(kfeat[:, i, h, 0:M], ps[0:TP, 0:M], ACT.Copy), ("ddk", i, h))
            act.wait_ge(kbias_ok, 1)
            for i in range(NT):
                for h in range(H):
                    n = H * i + h
                    last = act.activation(kfeat[:, i, h, 0:M], kfeat[:, i, h, 0:M], ACT.Exp, bias=nbias[:, 2, n:n + 1])
                last.then_inc(kexp_ok, 1)

            def q_exp(i):
                if i >= 1:
                    done(act, ("kv", H - 1))
                if i >= 2:
                    act.wait_ge(q1_free, i - 1)
                for h in range(H):
                    n = H * i + h
                    ps = read(act, ("ddq", i, h))
                    act.wait_ge(qbias_ok, n + 1)
                    emptied(act.activation(q1[i % 2][:, h, 0:M], ps[0:TP, 0:M], ACT.Exp, bias=nbias[:, 3, n:n + 1]), ("ddq", i, h))

            q_exp(0)
            for i in range(NT):
                if i + 1 < NT:
                    q_exp(i + 1)
                for h in range(0, H, 2):
                    take_q1t(act, i, h, lambda o, a: act.activation(o, a, ACT.Copy))
            take_turned(act, "at", aot)
            act.wait_ge(bsplit_ok, 1)
            for u in range(C):
                split_hi(act, False, 0, u)
            take_turned(act, "x2", xn2t)
            act.wait_ge(sc_ok, 1)
            act.activation(sc[:, :, :], sc[:, :, :], ACT.Exp).then_inc(ex_ok, 1)

            def hidden_high(j):
                act.wait_ge(v_scaled, j)
                act.activation(hthi[:, :, :].rearrange("p c t -> p (c t)"), hid[:, :], ACT.Copy).then_inc(hthi_ok, 1)

            def gelu(j):
                for n in range(3):
                    act.wait_ge(fc1_ok, 3 * j + n + 1)
                    act.activation(hid[:, 512 * n:512 * n + 512], hid_ps[n][:, :], ACT.Gelu).then_inc(gelu_ok, 1)

            def x_high(b):
                act.wait_ge(x_turned, b + 1)
                act.activation(xthi[:, 0:4, :].rearrange("p c t -> p (c t)"), tr_ps[0][:, :], ACT.Copy)
                act.activation(xthi[:, 4:6, :].rearrange("p c t -> p (c t)"), tr_ps[1][:, 0:256], ACT.Copy).then_inc(xthi_ok, 1)

            def weigh(j):
                act.wait_ge(fc2_ok, j)
                act.wait_ge(sidx_ok, j)
                act.activation(ysb[:, 0:384], y_ps[0][:, 0:384], ACT.Copy, scale=sidx[:, 1:2].bitcast(F32))
                act.activation(ysb[:, 384:768], y_ps[1][:, 0:384], ACT.Copy, scale=sidx[:, 1:2].bitcast(F32)).then_inc(y_ok, 1)

            act.sem_inc(y_ok, 1)
            x_high(0)
            act.wait_ge(btab_ok, 1)
            act.wait_ge(st_xn2, 16 * (NT + 1))
            act.wait_ge(st_pad, 16)
            for u in range(C):
                split_hi(act, True, 1, u)
            gelu(0)
            x_high(1)
            nb = act.value_load(btab[0:1, LAST_OF, TW:TW + 1], min_val=NT + E - 1, max_val=BLOCKS)

            def split_second(j):
                with act.If(entry(act, NEW_BEFORE, j, 1)):
                    g = entry(act, GROUP2, entry(act, EXPERT, j - 1, E - 1), 2 * E)
                    for u in range(C):
                        act.wait_ge(w2_used, C * j + u + 1)
                        split_hi(act, True, g, u)

            with act.Fori(1, nb) as j:
                hidden_high(j)
                split_second(j)
                act.wait_ge(htlo_ok, j)
                gelu(j)
                x_high(j + 1)
                with act.If(entry(act, LAST_OF, j, 1)):
                    g = entry(act, GROUP1, entry(act, EXPERT, j + 1, E - 1), 2 * E)
                    for u in range(C):
                        act.wait_ge(w1_used, C * j + u + 1)
                        split_hi(act, False, g, u)
                weigh(j)
            hidden_high(nb)
            split_second(nb)
            weigh(nb)

        @block.tensor
        def _(pe):
            pe.wait_ge(const_ok, 3)
            pe.wait_ge(ld_proj, 96)
            ps = fill(pe, ("pt", 0))
            for m in range(3):
                rows = min(MC, M - MC * m)
                last = pe.transpose(ps[:, MC * m:MC * m + rows], prow[0:rows, m, :], ident[0:rows, 0:rows])
            filled(last, ("pt", 0))
            turn_tokens(pe, "xt", xn, xn_ok, 1)

            pe.sem_inc(oh_free, RING)
            pe.sem_inc(adj_read, NT)

            def count(c, tiles):
                for k in range(tiles):
                    pe.wait_ge(oh_ready, CHUNK * c + k + 1)
                    for b in range(NT):
                        if k == 0:
                            pe.wait_ge(adj_read, NT * c + b + 1)
                        last = pe.matmul(bank[b][0:TP, 0:HALF], ohs[:, k % RING, TP * b:TP * b + TP],
                                         ohd[:, k % RING, 0:HALF], start=k == 0, stop=k == tiles - 1)
                    if k == tiles - 1:
                        last.then_inc(adj_full, 1)
                        pe.wait_ge(adj_full, c + 1)
                        pe.sem_inc(oh_free, 1)
                    else:
                        last.then_inc(oh_free, 1)

            count(0, CHUNK)
            with pe.Fori(1, CHUNKS) as c:
                count(c, CHUNK)
            count(CHUNKS, LASTC)

            pe.wait_ge(ld_qkv, 16)
            all_turned(pe, "xt")
            for name, first in (("k", D), ("q", 0)):
                for o in range(C):
                    for s, (a, b) in enumerate(TSPLIT):
                        ps = fill(pe, (name, o, s))
                        for c in range(C):
                            last = pe.matmul(ps[:, 0:b - a], wqkv[:, c, first + 128 * o:first + 128 * o + 128],
                                             xnt[:, c, a:b], start=c == 0, stop=c == C - 1)
                        filled(last, (name, o, s))

            def rows_times(name, xt_, w, first):
                for i in range(NT):
                    for s in range(2):
                        ps = fill(pe, (name, i, s))
                        for c in range(C):
                            last = pe.matmul(ps[0:TP, 0:384], xt_[:, c, TP * i:TP * i + TP],
                                             w[:, c, first + 384 * s:first + 384 * s + 384], start=c == 0, stop=c == C - 1)
                        filled(last, (name, i, s))

            rows_times("v", xnt, wqkv, 2 * D)
            pe.wait_ge(adj_ok, 1)
            ps = fill(pe, ("deg", 0))
            for i in range(NT):
                for b in range(NT):
                    last = pe.matmul(ps[0:TP, i:i + 1], adj[:, b, TP * i:TP * i + TP], ones[0:TP, :],
                                     start=b == 0, stop=b == NT - 1)
            filled(last, ("deg", 0))
            pe.wait_ge(ld_wg, 16)
            rows_times("h", xnt, wg, 0)

            for n, name in enumerate(("sqk", "sqq")):
                ps = fill(pe, (name, 0))
                for o in range(C):
                    g = C * n + o
                    pe.wait_ge(sq_ok, g + 1)
                    for i in range(NT):
                        last = pe.matmul(ps[0:TP, H * i + 2 * o:H * i + 2 * o + 2], sq[:, g % 2, TP * i:TP * i + TP],
                                         sel2[:, :], start=True, stop=True)
                    if o == C - 1:
                        filled(last, (name, 0))
                        done(pe, (name, 0))
                        pe.sem_inc(sq_used, 1)
                    else:
                        last.then_inc(sq_used, 1)

            def project(name, of, i, h):
                ps = fill(pe, (name, i, h))
                r = HD * (h % 2)
                filled(pe.matmul(ps[0:TP, 0:M], of[r:r + HD, h // 2, TP * i:TP * i + TP], projt[r:r + HD, :],
                                 start=True, stop=True), (name, i, h))

            taken(pe, ("pt", 0))
            for i in range(NT):
                for h in range(H):
                    project("ddk", kt, i, h)
            taken(pe, ("h", NT - 1, 0))
            taken(pe, ("h", NT - 1, 1))
            for i in range(NT):
                for s in range(2):
                    ps = fill(pe, ("gnn", i, s))
                    for b in range(NT):
                        last = pe.matmul(ps[0:TP, 0:384], adj[:, b, TP * i:TP * i + TP], hrow[:, b, 384 * s:384 * s + 384],
                                         start=b == 0, stop=b == NT - 1)
                    filled(last, ("gnn", i, s))
            pe.wait_ge(k1_ok, NT)
            pe.wait_ge(vones_ok, 1)
            for s in range(2):
                taken(pe, ("v", NT - 1, s))
            for h in range(H):
                ps = fill(pe, ("kv", h))
                for m in range(3):
                    for i in range(NT):
                        last = pe.matmul(ps[0:MC, (HD + 1) * m:(HD + 1) * (m + 1)], kfeat[:, i, h, MC * m:MC * m + MC],
                                         vext[:, i, h, :], start=i == 0, stop=i == NT - 1)
                filled(last, ("kv", h))

            def q_project(i):
                for h in range(H):
                    project("ddq", qt, i, h)

            def turn_q(i, h):
                ps = fill(pe, ("q1t", i, h))
                for m in range(3):
                    last = pe.transpose(ps[0:MC, TP * m:TP * m + TP], q1[i % 2][:, h, MC * m:MC * m + MC], ident[0:TP, 0:TP])
                filled(last, ("q1t", i, h))
                if h == H - 1:
                    done(pe, ("q1t", i, h))
                    pe.sem_inc(q1_free, 1)

            def attend(i, h):
                ps = fill(pe, ("o", i, h // 6)) if h % 6 == 0 else bank[plan[("o", i, h // 6)][0]]
                taken(pe, ("q1t", i, h))
                g = h % 6
                for m in range(3):
                    last = pe.matmul(ps[0:TP, (HD + 1) * g:(HD + 1) * (g + 1)], q1t[:, (H * i + h) % 3, m, :],
                                     kv[:, h, m, :], start=m == 0, stop=m == 2)
                if g == 5:
                    filled(last, ("o", i, h // 6))
                    done(pe, ("o", i, h // 6))
                    pe.sem_inc(q1t_used, 1)
                else:
                    last.then_inc(q1t_used, 1)

            q_project(0)
            for h in range(H):
                taken(pe, ("kv", h))
            for i in range(NT):
                if i + 1 < NT:
                    q_project(i + 1)
                pe.wait_ge(q1_ok, i + 1)
                turn_q(i, 0)
                for h in range(H):
                    if h + 1 < H:
                        turn_q(i, h + 1)
                    attend(i, h)

            for i in range(NT):
                for g in range(2):
                    taken(pe, ("o", i, g))
            pe.wait_ge(const_ok, 3)
            turn_tokens(pe, "at", ao, const_ok, 0)
            all_turned(pe, "at")
            pe.wait_ge(ld_wp, 16)
            rows_times("pj", aot, wp, 0)
            turn_tokens(pe, "x2", xn2, xn2_ok, 1)
            all_turned(pe, "x2")
            pe.wait_ge(ld_gate, 16)
            ps = fill(pe, ("gate", 0))
            for i in range(NT):
                for c in range(C):
                    last = pe.matmul(ps[0:TP, E * i:E * i + E], xn2t[:, c, TP * i:TP * i + TP], gatew[:, c, :],
                                     start=c == 0, stop=c == C - 1)
            filled(last, ("gate", 0))
            pe.wait_ge(member_ok, 1)
            ps = fill(pe, ("cnt", 0))
            for i in range(NT):
                last = pe.matmul(ps[:, 0:E], onesb[:, :], member[:, i, :], start=i == 0, stop=i == NT - 1)
            filled(last, ("cnt", 0))
            ps = fill(pe, ("pos", 0))
            for i in range(NT):
                for b in range(i + 1):
                    last = pe.matmul(ps[0:TP, E * i:E * i + E], (prefix if b == i else onesb)[:, 0:TP], member[:, b, :],
                                     start=b == 0, stop=b == i)
            filled(last, ("pos", 0))

            def turn_x(b):
                pe.wait_ge(gathered, 16 * b + 16)
                for c in range(C):
                    last = pe.transpose(tr_ps[c // 4][:, 128 * (c % 4):128 * (c % 4) + 128], xg[:, c::C], ident[:, :])
                last.then_inc(x_turned, 1)

            def turn_h(j):
                pe.wait_ge(ln_ok, j)
                for c in range(FC):
                    last = pe.transpose(tr_ps[c // 4][:, 128 * (c % 4):128 * (c % 4) + 128], hid[:, c::FC], ident[:, :])
                last.then_inc(h_turned, 1)

            def bias(ps, e, a, b):
                return pe.matmul(ps, selw[:, bass.ds(e, 1), :].rearrange("p a t -> p (a t)"), bsplit[:, a:b],
                                 start=False, stop=True)

            def fc1(j, e, g):
                pe.wait_ge(xtlo_ok, j + 1)
                for c in range(C):
                    pe.wait_ge(w_lo, STG + C * g + c + 1)
                    for k, (a, w) in enumerate(((xthi, w1hi), (xthi, w1lo), (xtlo, w1hi))):
                        for n in range(3):
                            last = pe.matmul(hid_ps[n][:, :], a[:, c, :], w[:, c, 512 * n:512 * n + 512],
                                             start=c == 0 and k == 0, stop=False)
                    last.then_inc(w1_used, 1)
                for n in range(3):
                    bias(hid_ps[n][:, :], e, 512 * n, 512 * n + 512).then_inc(fc1_ok, 1)

            def fc2(j, e, g):
                pe.wait_ge(htlo_ok, j)
                for c in range(FC):
                    if c % 2 == 0:
                        pe.wait_ge(w_lo, STG + C * g + c // 2 + 1)
                    for k, (a, w) in enumerate(((hthi, w2hi), (hthi, w2lo), (htlo, w2hi))):
                        for s in range(2):
                            last = pe.matmul(y_ps[s][:, 0:384], a[:, c, :], w[:, c, 384 * s:384 * s + 384],
                                             start=c == 0 and k == 0, stop=False)
                    if c % 2:
                        last.then_inc(w2_used, 1)
                bias(y_ps[0][:, 0:384], e, F, F + 384)
                bias(y_ps[1][:, 0:384], e, F + 384, F + D).then_inc(fc2_ok, 1)

            pe.sem_inc(w2_used, 2 * C)

            for b in range(8):
                pe.wait_ge(free[b], uses[b])
            turn_x(0)
            pe.wait_ge(sel_ok, 4)
            fc1(0, 0, 0)
            turn_x(1)
            pe.wait_ge(btab_ok, 1)
            nb = pe.value_load(btab[0:1, LAST_OF, TW:TW + 1], min_val=NT + E - 1, max_val=BLOCKS)
            with pe.Fori(1, nb) as j:
                e_before = entry(pe, EXPERT, j - 1, E - 1)
                e = entry(pe, EXPERT, j, E - 1)
                g1, g2 = entry(pe, GROUP1, e, 2 * E), entry(pe, GROUP2, e_before, 2 * E)
                pe.wait_ge(xtlo_ok, j + 1)
                turn_h(j)
                fc1(j, e, g1)
                pe.wait_ge(v_scaled, j)
                turn_x(j + 1)
                pe.wait_ge(y_ok, j)
                fc2(j, e_before, g2)
            pe.wait_ge(xtlo_ok, nb + 1)
            turn_h(nb)
            pe.wait_ge(y_ok, nb)
            fc2(nb, E - 1, 2 * E - 1)


_INS = ["x", "src", "dst", "L0_gnn_W", "L0_gnn_b", "L0_mix_W_qkv", "L0_mix_W_proj", "L0_mix_b_proj",
        "L0_mix_proj_mat", "L0_ffn_gate_w", "L0_ffn_gate_b", "L0_ffn_fc1_w", "L0_ffn_fc1_b", "L0_ffn_ln_w",
        "L0_ffn_ln_b", "L0_ffn_fc2_w", "L0_ffn_fc2_b"]


def kernel(**inputs):
    import numpy as np
    import concourse.bacc as bacc
    from concourse.bass_utils import run_bass_kernel_spmd

    nc = bacc.Bacc("TRN2", target_bir_lowering=False, num_devices=1)
    arrays, args = {}, []
    for name in _INS:
        a = np.ascontiguousarray(inputs[name])
        arrays[f"in_{name}"] = a
        args.append(nc.dram_tensor(f"in_{name}", a.shape, mybir.dt.from_np(a.dtype), kind="ExternalInput").ap())
    out = nc.dram_tensor("out", (N, D), F32, kind="ExternalOutput").ap()
    xn2_dram = nc.dram_tensor("xn2_dram", (N + 1, D), F32, kind="Internal").ap()
    table_dram = nc.dram_tensor("table_dram", (128 * TW, 2), I32, kind="Internal").ap()
    gps_kernel(nc, *args, out, xn2_dram, table_dram)
    r = run_bass_kernel_spmd(nc, [arrays], core_ids=[0])
    return r.results[0]["out"]
```

```python
import math
from contextlib import ExitStack

import concourse.bass as bass
from concourse import mybir

F32 = mybir.dt.float32
F32R = mybir.dt.float32r
BF16 = mybir.dt.bfloat16
F16 = mybir.dt.float16
I32 = mybir.dt.int32
U32 = mybir.dt.uint32
ALU = mybir.AluOpType
ACT = mybir.ActivationFunctionType
AX = mybir.AxisListType

N, D = 625, 768
TP, NT = 125, 5
C = D // 128
EDGES = 20625
ET = EDGES // TP
HALF = 313
PACK = 4096
CHUNK, CHUNKS = 28, 5
LASTC = ET - CHUNK * CHUNKS
RING = 4
H, HD, M = 12, 64, 266
MC = 89
MP = 3 * MC
E, F = 16, 1536
FC = F // 128
LN_EPS, FEAT_EPS = 1e-5, 1e-4
NEG = -1e9
TOPK = 3
SLOTS = 128
BLOCKS = NT + (E - 1) + (N * TOPK - (E - 1)) // SLOTS
TW = BLOCKS + 2
ROUND = 12582912.0
EXPERT, LAST_OF, NEW_BEFORE = range(3)
RMAX = bass.bass_isa.ReduceOp.max
TSPLIT = [(0, 320), (320, N)]
ON_POOL = 3


class Chain:

    def __init__(self, eng, sem, base=0):
        self.eng, self.sem, self.base, self.n = eng, sem, base, 0

    def __call__(self, ins):
        ins.then_inc(self.sem, 1)
        self.n += 1
        self.eng.wait_ge(self.sem, self.base + self.n)


def row(v):
    return v.rearrange("(a n) -> a n", a=1)


def rsqrt(dve, link, y, v, half, tmp):
    seed_i, v_i = y.bitcast(I32), v.bitcast(I32)
    link(dve.tensor_scalar(seed_i, v_i, 1, None, ALU.arith_shift_right))
    link(dve.tensor_scalar(seed_i, seed_i, -1.0, float(0x5F3759DF), ALU.mult, ALU.add))
    link(dve.tensor_scalar(half, v, -0.5, None, ALU.mult))
    for _ in range(3):
        if v.shape[-1] == 1:
            link(dve.scalar_tensor_tensor(out=tmp, in0=y, scalar=half, in1=y, op0=ALU.mult, op1=ALU.mult))
        else:
            link(dve.tensor_tensor(tmp, y, y, ALU.mult))
            link(dve.tensor_tensor(tmp, tmp, half, ALU.mult))
        link(dve.scalar_tensor_tensor(out=y, in0=tmp, scalar=1.5, in1=y, op0=ALU.add, op1=ALU.mult))


def gps_kernel(nc, x, src, dst, gnn_w, gnn_b, w_qkv, w_proj, b_proj, proj_mat, gate_w, gate_b,
               fc1_w, fc1_b, ln_w, ln_b, fc2_w, fc2_b, out, xn2_dram, table_dram):
    ctx = ExitStack()
    with ctx:
        base0 = (nc.sbuf_base + 31) // 32 * 32

        def at(name, offset, shape, dt=F32):
            return nc.alloc_sbuf_tensor_at(name, shape, dt, offset=base0 + offset)

        KB6 = F * 4
        w1hi = at("w1hi", 0, [128, C, F], F32R)
        w1lo = at("w1lo", 6 * KB6, [128, C, F], F32R)
        w2hi = at("w2hi", 12 * KB6, [128, FC, D], F32R)
        w2lo = at("w2lo", 18 * KB6, [128, FC, D], F32R)
        w1raw = at("w1raw", 6 * KB6, [128, C, F])
        w2raw = at("w2raw", 18 * KB6, [128, FC, D])
        LOOP = 27 * KB6
        xg = at("xg", LOOP, [128, D])
        xthi = at("xthi", LOOP + 3072, [128, C, 128], F32R)
        xtlo = at("xtlo", LOOP + 6144, [128, C, 128], F32R)
        hid = at("hid", LOOP + 9216, [128, F])
        hthi = at("hthi", LOOP + 15360, [128, FC, 128], F32R)
        htlo = at("htlo", LOOP + 21504, [128, FC, 128], F32R)
        ysb = at("ysb", LOOP + 27648, [128, D])
        SMALL = LOOP + 30720 + 3104
        wqkv = at("wqkv", 0, [128, C, 3 * D])
        wg = at("wg", 55296, [128, C, D])
        kfeat = at("kfeat", 0, [TP, NT, H, MP])
        xnt = at("xnt", 73728, [128, C, N])
        kv = at("kv", 73728, [MC, H, 3, HD + 1])
        q1t = at("q1t", 83200, [MC, 3, 3, TP])
        aot = at("aot", 73728, [128, C, N])
        xn = at("xn", 88832, [TP, NT, D])
        ao = at("ao", 88832, [TP, NT, D])
        xn2 = at("xn2", 88832, [TP, NT, D])
        qt = at("qt", 104192, [128, C, N])
        xn2t = at("xn2t", 104192, [128, C, N])
        kt = at("kt", 119296, [128, C, N])
        q1 = [at("q1a", 119296, [TP, H, MP]), at("q1b", 132128, [TP, H, MP])]
        vext = at("vext", 134400, [TP, NT, H, HD + 1])
        adj = at("adj", 150016, [TP, NT, 2 * HALF])
        hrow = at("hrow", 162560, [TP, NT, D])
        wp = at("wp", 165888, [128, C, D])
        xs = at("xs", 184320, [TP, NT, D])
        ohs = at("ohs", 104192, [TP, RING, N], BF16)
        ohd = at("ohd", 109216, [TP, RING, HALF + 1], BF16)
        pk = at("pk", 111744, [TP, NT, HALF])
        pkh = at("pkh", 118016, [TP, NT, HALF])
        iota_n = at("iota_n", 124288, [TP, N], F16)
        iota_i = at("iota_i", 125568, [TP, N], I32)
        src_i = at("src_i", 128096, [TP, 2, ET], I32)
        ef = at("ef", 129440, [TP, 5, ET])
        bias2 = at("bias2", 132768, [TP, 2, D], F32)
        sq = at("sq", 177920, [128, 2, N])
        r0 = 24 * KB6

        def rt(name, shape, dt=F32):
            nonlocal r0
            size = 4 if dt != BF16 else 2
            t = at(name, r0, shape, dt)
            r0 += (math.prod(shape[1:]) * size + 31) // 32 * 32
            return t

        sc = rt("sc", [TP, NT, E])
        pr = rt("pr", [TP, NT, E])
        mx = rt("mx", [TP, NT])
        cmp1 = rt("cmp1", [TP, NT, E, E], BF16)
        cmp2 = rt("cmp2", [TP, NT, E, E], BF16)
        rank = rt("rank", [TP, NT, E])
        comb = rt("comb", [TP, NT, E])
        member = rt("member", [TP, NT, E], BF16)
        pos = rt("pos", [TP, NT, E])
        quo = rt("quo", [TP, NT, E])
        pick = rt("pick", [TP, 2, NT, E])
        slotf = rt("slotf", [TP, 4, NT])
        nblk = rt("nblk", [128, E])
        base = rt("base", [128, E])
        btmp = rt("btmp", [128, E, E])
        biota_i = rt("biota_i", [128, TW], I32)
        biota = rt("biota", [128, TW])
        bcmp = rt("bcmp", [128, TW, E])
        bsum = rt("bsum", [128, TW])
        gateb = rt("gateb", [TP, E])
        padt = rt("padt", [128, TW, 2], I32)
        selw = rt("selw", [128, E, 128], BF16)
        assert r0 <= LOOP, r0 - LOOP
        bl = at("bl", 0, [80, F + D])
        bl2 = at("bl2", 9216, [80, F + D])
        bh = at("bh", 18432, [80, F + D], BF16)
        padrow = at("padrow", 4 * KB6, [1, D])
        prow = at("prow", 138912, [MC, 3, 2 * HD])
        s0 = SMALL

        def small(name, shape, dt=F32):
            nonlocal s0
            size = 2 if dt in (BF16, F16) else 4
            t = at(name, s0, shape, dt)
            s0 += (math.prod(shape[1:]) * size + 31) // 32 * 32
            return t

        assert SMALL >= 184320 + NT * D * 4
        ident = small("ident", [128, 128])
        lnw = small("lnw", [128, E, FC])
        lnb = small("lnb", [128, E, FC])
        bsplit = small("bsplit", [128, F + D], BF16)
        projt = at("projt", s0, [128, M])
        gatew = at("gatew", s0 + 1088, [128, C, E])
        nbias = at("nbias", s0 + 1472, [TP, 4, 60])
        lnst = at("lnst", s0 + 1472, [TP, NT, 2, 6])
        lnmv = at("lnmv", s0 + 1728, [TP, NT, 2])
        lnrs = at("lnrs", s0 + 1792, [TP, 4, NT])
        sel2 = at("sel2", s0 + 2432, [128, 2])
        ones = at("ones", s0 + 2464, [128, 1])
        dinv = at("dinv", s0 + 2752, [TP, 5, NT])
        kmax = at("kmax", s0 + 2880, [128, 4])
        rden = at("rden", s0 + 2912, [TP, 6])
        prefix = at("prefix", s0 + 2944, [TP, 128], BF16)
        onesb = at("onesb", s0 + 3200, [TP, 128], BF16)
        kmax5 = at("kmax5", s0 + 3456, [TP, 5])
        s0 += 4096
        table = small("table", [128, TW, 2], I32)
        firstrow = small("firstrow", [128, 3], I32)
        pair = at("pair", s0, [TP, 4, NT, 2], I32)
        slot = at("slot", s0 + 160, [TP, 4, NT], U32)
        tri = at("tri", s0 + 256, [128, E, E], BF16)
        s0 += 768
        btab = small("btab", [128, 3, TW + 1], I32)
        st6 = small("st6", [128, 3, 6])
        mv = small("mv", [128, 2])
        rs = small("rs", [128, 4])
        gidx = small("gidx", [128, 1], U32)
        sidx = small("sidx", [128, 2], U32)
        assert base0 + s0 <= nc.sbuf_usable_end, (base0 + s0, nc.sbuf_usable_end)

        bank = [ctx.enter_context(nc.psum_tensor(f"bank{b}", [128, 512], F32)) for b in range(8)]
        hid_ps = bank[0:3]
        tr_ps = bank[3:6]
        y_ps = bank[6:8]

        def sem(name):
            return ctx.enter_context(nc.semaphore(name))

        plan, uses, turn = {}, [0] * 8, 0

        def groups(keys, banks):
            nonlocal turn
            for key in keys:
                b = banks[turn % len(banks)]
                turn += 1
                uses[b] += 1
                plan[key] = (b, uses[b])

        R3, R8 = [5, 6, 7], list(range(8))
        T8 = [("c", c) for c in range(C)] + [("l", 0), ("l", 4)]
        groups([("pt", 0)], R3)
        groups([("xt",) + k for k in T8], R3)
        groups([("v", i, s) for i in range(NT) for s in range(2)], R3)
        groups([("k", o, s) for o in range(C) for s in range(2)], R3)
        groups([("q", o, s) for o in range(C) for s in range(2)], R3)
        groups([("deg", 0)], R3)
        groups([("h", i, s) for i in range(NT) for s in range(2)], R3)
        turn = 0
        groups([("sqk", 0), ("sqq", 0)], [0, 1])
        groups([("ddk", i, h) for i in range(NT) for h in range(H)], R8)
        groups([("gnn", i, s) for i in range(NT) for s in range(2)], R8)
        groups([("kv", h) for h in range(H)], R8)

        def q_groups(i):
            groups([("ddq", i, h) for h in range(H)], R8)

        def o_groups(i):
            for g in range(2):
                for h in range(6 * g, 6 * g + 6):
                    groups([("q1t", i, h)], R8)
                groups([("o", i, g)], R8)

        q_groups(0)
        for i in range(NT):
            if i + 1 < NT:
                q_groups(i + 1)
            o_groups(i)
        groups([("at",) + k for k in T8], R8)
        turn = 0
        for i in range(NT + 2):
            if i < NT:
                groups([("pj", i, 0), ("pj", i, 1)], [0, 1, 2, 3, 4, 6, 7])
            if i == 2:
                before_gate = turn
                turn = 0
                groups([("gate", 0)], [5])
                turn = before_gate
            if i >= 2:
                groups([("x2", i - 2, 0), ("x2", i - 2, 1)], [0, 1, 2, 3, 4, 6, 7])
        turn = 0
        groups([("cnt", 0), ("pos", 0)], [6, 7])

        full = [sem(f"full{b}") for b in range(8)]
        free = [sem(f"free{b}") for b in range(8)]

        def fill(pe, key):
            b, n = plan[key]
            if n > 1:
                pe.wait_ge(free[b], n - 1)
            return bank[b]

        def filled(last, key):
            last.then_inc(full[plan[key][0]], 1)

        def read(eng, key):
            b, n = plan[key]
            eng.wait_ge(full[b], n)
            return bank[b]

        def emptied(ins, key):
            ins.then_inc(free[plan[key][0]], 1)

        def sems(names):
            return [sem(n) for n in names.split()]

        ld_x = [sem(f"ld_x{i}") for i in range(NT)]
        ld_idx, ld_bias, ld_qkv, ld_wg, ld_proj, ld_gate, ld_ln, ld_wp, ld_eb, ld_gb, ld_table = sems(
            "ld_idx ld_bias ld_qkv ld_wg ld_proj ld_gate ld_ln ld_wp ld_eb ld_gb ld_table")
        st_x1, st_xn2, st_padrow, st_pad, st_slot = sems("st_x1 st_xn2 st_padrow st_pad st_slot")
        const_ok, route_const, sel_ok, dve_own, passed = sems("const_ok route_const sel_ok dve_own passed")
        xn_ok, x_biased, edges_ok, oh_free, oh_ready, adj_full, adj_read, rounded, unpacked, pk_free, adj_ok, deg_ok = sems(
            "xn_ok x_biased edges_ok oh_free oh_ready adj_full adj_read rounded unpacked pk_free adj_ok deg_ok")
        xt_ok, vones_ok, sq_ok, sq_used, kmax_ok, kall_ok, kbias_ok, kexp_ok, k1_ok = sems(
            "xt_ok vones_ok sq_ok sq_used kmax_ok kall_ok kbias_ok kexp_ok k1_ok")
        qbias_ok, q1_ok, q1_free, q1t_used, ao_ok, bsplit_ok, bl_zero = sems("qbias_ok q1_ok q1_free q1t_used ao_ok bsplit_ok bl_zero")
        x1_ok, xn2_ok, pad_ok, sc_ok, ex_ok, member_ok, slots_ok, btab_ok = sems(
            "x1_ok xn2_ok pad_ok sc_ok ex_ok member_ok slots_ok btab_ok")
        ld_w1 = [sem(f"ld_w1_{u}") for u in range(C)]
        ld_w2 = [sem(f"ld_w2_{u}") for u in range(C)]
        w1_hi, w2_hi, w1_lo, w2_lo, w1_lo_pool, w2_lo_pool, w1_used, w2_used = sems(
            "w1_hi w2_hi w1_lo w2_lo w1_lo_pool w2_lo_pool w1_used w2_used")
        gidx_ok, gathered, x_turned, xthi_ok, xtlo_ok = sems("gidx_ok gathered x_turned xthi_ok xtlo_ok")
        fc1_ok, gelu_ok, ln_own, ln_ok, h_turned, v_scaled, hthi_ok, htlo_ok = sems(
            "fc1_ok gelu_ok ln_own ln_ok h_turned v_scaled hthi_ok htlo_ok")
        fc2_ok, y_ok, sidx_ok, scattered = sems("fc2_ok y_ok sidx_ok scattered")

        def done(eng, key):
            b, n = plan[key]
            eng.wait_ge(full[b], n)

        def taken(eng, key):
            b, n = plan[key]
            eng.wait_ge(free[b], n)

        def turn_tokens(pe, name, rows, ready, per_tile):
            for kind, k in T8:
                ps = fill(pe, (name, kind, k))
                if kind == "c":
                    todo = [(k, i, i) for i in range(4)]
                else:
                    todo = [(c, 4, c - k) for c in range(k, min(C, k + 4))]
                for c, i, place in todo:
                    pe.wait_ge(ready, per_tile * (i + 1))
                    last = pe.transpose(ps[:, place * TP:(place + 1) * TP], rows[:, i, c::C], ident[0:TP, 0:TP])
                filled(last, (name, kind, k))

        def take_turned(act, name, to):
            for kind, k in T8:
                ps = read(act, (name, kind, k))
                if kind == "c":
                    ins = act.activation(to[:, k, 0:4 * TP], ps[:, 0:4 * TP], ACT.Copy)
                else:
                    n = min(C, k + 4) - k
                    ins = act.activation(to[:, k:k + n, 4 * TP:N],
                                         ps[:, 0:n * TP].rearrange("p (c t) -> p c t", t=TP), ACT.Copy)
                emptied(ins, (name, kind, k))

        def all_turned(eng, name):
            for kind, k in T8:
                taken(eng, (name, kind, k))

        def edge(plane, t):
            return ef[:, plane, bass.ds(t, 1)]

        def take_q1t(eng, i, h, copy):
            n = H * i + h
            ps = read(eng, ("q1t", i, h))
            if n >= 3:
                eng.wait_ge(q1t_used, n - 2)
            emptied(copy(q1t[:, n % 3, :, :], ps[0:MC, 0:3 * TP].rearrange("p (m t) -> p m t", m=3)), ("q1t", i, h))

        def unit(w, second, u):
            return w[:, 2 * u:2 * u + 2, :].rearrange("p c n -> p (c n)") if second else w[:, u, :]

        def split_hi(act, second, e, units):
            for u in units:
                act.wait_ge((ld_w2 if second else ld_w1)[u], 16 * e + 16)
                act.activation(unit(w2hi if second else w1hi, second, u), unit(w2raw if second else w1raw, second, u),
                               ACT.Copy).then_inc(w2_hi if second else w1_hi, 1)

        def pools(u):
            return u % ON_POOL == ON_POOL - 1

        def split_lo(eng, second, e, units):
            mine = eng.engine == mybir.EngineType.Pool
            low = (w2_lo_pool if mine else w2_lo) if second else (w1_lo_pool if mine else w1_lo)
            for u in units:
                if pools(u) == mine:
                    eng.wait_ge(w2_hi if second else w1_hi, C * e + u + 1)
                    eng.tensor_tensor(unit(w2lo if second else w1lo, second, u), unit(w2raw if second else w1raw, second, u),
                                      unit(w2hi if second else w1hi, second, u).bitcast(F32), ALU.subtract).then_inc(low, 1)

        def wait_split(pe, second, e, u):
            per_expert = len([v for v in range(C) if pools(v) == pools(u)])
            before = len([v for v in range(u) if pools(v) == pools(u)])
            if pools(u):
                pe.wait_ge(w2_lo_pool if second else w1_lo_pool, per_expert * e + before + 1)
            else:
                pe.wait_ge(w2_lo if second else w1_lo, per_expert * e + before + 1)

        def entry(eng, r, j, top):
            return eng.value_load(btab[0:1, r, bass.ds(j, 1)], min_val=0, max_val=top)

        def with_first(eng, j, do):
            with eng.If(entry(eng, LAST_OF, j, 1)):
                do(eng, False, entry(eng, EXPERT, j + 1, E - 1))

        def with_second(eng, j, do):
            with eng.If(entry(eng, NEW_BEFORE, j, 1)):
                do(eng, True, entry(eng, EXPERT, j - 1, E - 1))

        def high(*units):
            return lambda eng, second, e: split_hi(eng, second, e, units)

        def low(*units):
            return lambda eng, second, e: split_lo(eng, second, e, units)

        block = ctx.enter_context(nc.Block())

        @block.sync
        def _(sp):
            for i in range(NT):
                sp.dma_start(xs[:, i, :], x[TP * i:TP * i + TP, :]).then_inc(ld_x[i], 16)
                if i == 0:
                    sp.dma_start(src_i[:, 0, :], src.rearrange("(p k) -> p k", p=TP)).then_inc(ld_idx, 16)
                    sp.dma_start(src_i[:, 1, :], dst.rearrange("(p k) -> p k", p=TP)).then_inc(ld_idx, 16)
            sp.dma_start(bias2[:, 0, :], row(gnn_b).broadcast_to([TP, D])).then_inc(ld_bias, 16)
            sp.dma_start(bias2[:, 1, :], row(b_proj).broadcast_to([TP, D])).then_inc(ld_bias, 16)
            for m in range(3):
                rows = min(MC, M - MC * m)
                for half in range(2):
                    sp.dma_start(prow[0:rows, m, HD * half:HD * half + HD],
                                 proj_mat[MC * m:MC * m + rows, :]).then_inc(ld_proj, 16)
            sp.dma_start(wqkv[:, :, :], w_qkv.rearrange("(p c) n -> p c n", c=C)).then_inc(ld_qkv, 16)
            sp.dma_start(wg[:, :, :], gnn_w.rearrange("(p c) n -> p c n", c=C)).then_inc(ld_wg, 16)
            sp.dma_start(gatew[:, :, :], gate_w.rearrange("(p c) n -> p c n", c=C)).then_inc(ld_gate, 16)
            sp.dma_start(lnw[:, :, :], ln_w.rearrange("e (p c) -> p e c", c=FC)).then_inc(ld_ln, 16)
            sp.dma_start(lnb[:, :, :], ln_b.rearrange("e (p c) -> p e c", c=FC)).then_inc(ld_ln, 16)
            done(sp, ("gnn", NT - 1, 1))
            sp.dma_start(wp[:, :, :], w_proj.rearrange("(p c) n -> p c n", c=C)).then_inc(ld_wp, 16)
            sp.wait_ge(bl_zero, 1)
            for g in range(3):
                sp.dma_start(bl[32 * g:32 * g + E, 0:F], fc1_b).then_inc(ld_eb, 16)
                sp.dma_start(bl[32 * g:32 * g + E, F:F + D], fc2_b).then_inc(ld_eb, 16)

            fc1_units = fc1_w.rearrange("e (p c) n -> e p c n", c=C)
            fc2_units = fc2_w.rearrange("e (p c) n -> e p (c n)", c=FC)

            def load(second, e, u):
                of = fc2_units[bass.ds(e, 1), :, F * u:F * u + F] if second else fc1_units[bass.ds(e, 1), :, u, :]
                sp.dma_start(unit(w2raw if second else w1raw, second, u),
                             of.rearrange("a p n -> (a p) n")).then_inc((ld_w2 if second else ld_w1)[u], 16)

            done(sp, ("kv", H - 1))
            for u in range(C):
                load(False, 0, u)
            sp.dma_start(gateb[:, :], row(gate_b).broadcast_to([TP, E])).then_inc(ld_gb, 16)
            sp.wait_ge(pad_ok, 1)
            sp.dma_start(xn2_dram[N:N + 1, :], padrow[0:1, :]).then_inc(st_padrow, 16)
            sp.wait_ge(route_const, 2)
            sp.dma_start(table_dram.rearrange("(p w) a -> p w a", p=128), padt[:, :, :]).then_inc(st_pad, 16)
            for i in range(NT):
                sp.wait_ge(x1_ok, i + 1)
                sp.dma_start(out[TP * i:TP * i + TP, :], xs[:, i, :]).then_inc(st_x1, 16)
                sp.wait_ge(xn2_ok, i + 1)
                sp.dma_start(xn2_dram[TP * i:TP * i + TP, :], xn2[:, i, :]).then_inc(st_xn2, 16)
            done(sp, ("gate", 0))
            sp.wait_ge(st_xn2, 16 * NT)
            for u in range(C):
                load(True, 0, u)
            sp.wait_ge(st_slot, 16 * 4 * NT)
            sp.dma_start(table[:, :, :], table_dram.rearrange("(p w) a -> p w a", p=128)).then_inc(ld_table, 16)
            sp.wait_ge(btab_ok, 1)
            nb = sp.value_load(btab[0:1, LAST_OF, TW:TW + 1], min_val=NT + E - 1, max_val=BLOCKS)

            def load_first(j):
                with sp.If(entry(sp, LAST_OF, j, 1)):
                    e = entry(sp, EXPERT, j + 1, E - 1)
                    for u in range(C):
                        sp.wait_ge(w1_used, C * j + u + 1)
                        load(False, e, u)

            def load_second(j):
                with sp.If(entry(sp, NEW_BEFORE, j, 1)):
                    e = entry(sp, EXPERT, j - 1, E - 1)
                    for u in range(C):
                        sp.wait_ge(w2_used, C * j + u + 1)
                        load(True, e, u)

            with sp.Fori(1, nb) as j:
                load_second(j)
                load_first(j)
            load_second(nb)
            sp.wait_ge(st_x1, 16 * NT)

        @block.gpsimd
        def _(pool):
            pool.iota(iota_i[:, :], [[1, N]], base=0, channel_multiplier=0)
            pool.memset(ident[:, :], 0.0)
            pool.memset(onesb[:, :], 1.0)
            pool.memset(prefix[:, :], 1.0)
            pool.memset(tri[:, :, :], 1.0)
            pool.memset(ones[:, :], 1.0)
            pool.memset(sel2[:, :], 0.0)
            pool.memset(bsplit[:, :], 0.0)
            pool.memset(adj[:, :, :], 0.0).then_inc(const_ok, 1)
            pool.wait_ge(const_ok, 1)
            pool.affine_select(out=ident[:, :], in_=ident[:, :], compare_op=ALU.not_equal, fill=1.0, base=0,
                               pattern=[[-1, 128]], channel_multiplier=1)
            pool.affine_select(out=prefix[:, :], in_=prefix[:, :], compare_op=ALU.is_ge, fill=0.0, base=-1,
                               pattern=[[1, 128]], channel_multiplier=-1)
            pool.affine_select(out=tri[:, :, :], in_=tri[:, :, :], compare_op=ALU.is_ge, fill=0.0, base=-1,
                               pattern=[[1, E], [-1, E]], channel_multiplier=0)
            pool.memset(sel2[0:64, 0:1], 0.5).then_inc(const_ok, 1)
            pool.wait_ge(const_ok, 2)
            pool.memset(sel2[64:128, 1:2], 0.5).then_inc(const_ok, 1)
            pool.wait_ge(const_ok, 3)
            pool.wait_ge(ld_bias, 32)
            pool.wait_ge(xn_ok, NT)
            for i in range(NT):
                for b in range(2):
                    pool.tensor_tensor(xs[:, i, :], xs[:, i, :], bias2[:, b, :], ALU.add).then_inc(x_biased, 1)
                    pool.wait_ge(x_biased, 2 * i + b + 1)

            def add_counts(c):
                pool.wait_ge(rounded, 2 * c)
                pool.wait_ge(pk_free, 2 * c - 1)
                high_part, low_part = adj[:, :, HALF:2 * HALF], adj[:, :, 0:HALF]
                pool.tensor_tensor(high_part, high_part, pkh[:, :, :], ALU.add).then_inc(pk_free, 1)
                pool.wait_ge(unpacked, c)
                pool.tensor_tensor(low_part, low_part, pk[:, :, :], ALU.add).then_inc(pk_free, 1)

            pool.sem_inc(pk_free, 1)
            with pool.Fori(1, CHUNKS + 2) as c:
                add_counts(c)
            pool.wait_ge(pk_free, 2 * CHUNKS + 3)
            for b in range(NT):
                last = pool.tensor_tensor(adj[:, b, TP * b:TP * b + TP], adj[:, b, TP * b:TP * b + TP],
                                          ident[0:TP, 0:TP], ALU.add)
            last.then_inc(adj_ok, 1)
            pool.wait_ge(adj_ok, 1)
            done(pool, ("pt", 0))
            pool.memset(vext[:, :, :, HD:HD + 1], 1.0).then_inc(vones_ok, 1)
            pool.wait_ge(kmax_ok, 1)
            pool.partition_all_reduce(kmax[0:TP, 1:2], kmax[0:TP, 0:1], TP, RMAX).then_inc(kall_ok, 1)
            done(pool, ("kv", H - 1))
            pool.memset(bl[:, :], 0.0).then_inc(bl_zero, 1)
            pool.iota(biota_i[:, :], [[1, TW]], base=0, channel_multiplier=0)
            pool.memset(padrow[0:1, :], 0.0).then_inc(pad_ok, 1)
            pool.iota(padt[:, :, 0], [[0, TW]], base=N, channel_multiplier=0)
            pool.memset(padt[:, :, 1], 0)
            pool.iota(firstrow[:, :], [[128, 3]], base=0, channel_multiplier=1)
            pool.iota(pair[:, :, :, 0], [[0, 4], [TP, NT]], base=0, channel_multiplier=1).then_inc(route_const, 2)
            pool.memset(selw[:, :, :], 0.0).then_inc(sel_ok, 1)
            for g in range(3):
                pool.wait_ge(sel_ok, g + 1)
                pool.affine_select(out=selw[:, :, :], in_=selw[:, :, :], compare_op=ALU.not_equal, fill=1.0,
                                   base=-32 * g, pattern=[[-1, E], [0, 128]], channel_multiplier=1).then_inc(sel_ok, 1)
            pool.wait_ge(bsplit_ok, 1)
            split_lo(pool, False, 0, range(C))

            pool.wait_ge(st_padrow, 16)
            pool.wait_ge(st_xn2, 16 * NT)
            pool.wait_ge(st_x1, 16 * NT)
            taken(pool, ("pj", NT - 1, 1))
            pool.wait_ge(route_const, 2)
            for b in range(3):
                if b:
                    pool.wait_ge(x_turned, b)
                    pool.wait_ge(gathered, 16 * b)
                pool.indirect_dma_start(out=xg[:, :], out_offset=None, in_=xn2_dram,
                                        in_offset=bass.IndirectOffsetOnAxis(ap=firstrow[:, b:b + 1].bitcast(U32), axis=0)
                                        ).then_inc(gathered, 16)
            split_lo(pool, True, 0, range(C))
            pool.wait_ge(slots_ok, 1)
            pool.wait_ge(st_pad, 16)
            for k in range(4):
                for i in range(NT):
                    pool.indirect_dma_start(
                        out=table_dram, out_offset=bass.IndirectOffsetOnAxis(ap=slot[:, k, i:i + 1], axis=0),
                        in_=pair[:, k, i, :], in_offset=None).then_inc(st_slot, 16)
            pool.wait_ge(ld_table, 16)

            def gather(b):
                pool.tensor_copy(gidx[:, 0:1], table[:, bass.ds(b, 1), 0]).then_inc(gidx_ok, 1)
                pool.wait_ge(gidx_ok, b - 2)
                pool.sem_inc(passed, 1)
                pool.indirect_dma_start(out=xg[:, :], out_offset=None, in_=xn2_dram,
                                        in_offset=bass.IndirectOffsetOnAxis(ap=gidx[:, 0:1], axis=0)).then_inc(gathered, 16)

            def scatter(j):
                pool.tensor_copy(sidx[:, :], table[:, bass.ds(j - 1, 1), :].rearrange("p w a -> p (w a)")).then_inc(sidx_ok, 1)
                pool.wait_ge(y_ok, j + 1)
                pool.sem_inc(passed, 1)
                pool.indirect_dma_start(out=out, out_offset=bass.IndirectOffsetOnAxis(ap=sidx[:, 0:1], axis=0),
                                        in_=ysb[:, :], in_offset=None, bounds_check=N - 1, oob_is_err=False,
                                        compute_op=ALU.add).then_inc(scattered, 16)
                pool.wait_ge(scattered, 16 * j)

            pool.wait_ge(btab_ok, 1)
            nb = pool.value_load(btab[0:1, LAST_OF, TW:TW + 1], min_val=NT + E - 1, max_val=BLOCKS)
            with pool.Fori(1, nb) as j:
                with_second(pool, j, low(5))
                with_first(pool, j, low(2))
                pool.wait_ge(x_turned, j + 2)
                pool.wait_ge(gathered, 16 * j + 32)
                gather(j + 2)
                with_first(pool, j, low(5))
                with_second(pool, j + 1, low(2))
                scatter(j)
            with_second(pool, nb, low(5))
            scatter(nb)
            pool.wait_ge(gathered, 16 * nb + 32)

        @block.vector
        def _(dve):
            link = Chain(dve, dve_own)
            def norm(rows, to, p, own):
                width = rows.shape[-1]
                step = 512 if width % 512 == 0 else 384
                parts = width // step
                for n in range(parts):
                    last = dve.bn_stats(st6[0:p, n, :], rows[:, n * step:(n + 1) * step])
                own(last)
                dve.sem_inc(passed, 1)
                own(dve.bn_aggr(mv[0:p, :], st6[0:p, 0:parts, :]))
                own(dve.tensor_scalar(rs[0:p, 0:1], mv[0:p, 1:2], LN_EPS, None, ALU.add))
                rsqrt(dve, own, rs[0:p, 3:4], rs[0:p, 0:1], rs[0:p, 1:2], rs[0:p, 2:3])
                return dve.tensor_scalar(to, rows, mv[0:p, 0:1], rs[0:p, 3:4], ALU.subtract, ALU.mult)

            for i in range(NT):
                dve.wait_ge(ld_x[i], 16)
                for n in range(2):
                    last = dve.bn_stats(lnst[:, i, n, :], xs[:, i, 384 * n:384 * n + 384])
            link(last)
            dve.sem_inc(passed, 1)
            for i in range(NT):
                last = dve.bn_aggr(lnmv[:, i, :], lnst[:, i, :, :])
            link(last)
            link(dve.tensor_scalar(lnrs[:, 0, :], lnmv[:, :, 1], LN_EPS, None, ALU.add))
            rsqrt(dve, link, lnrs[:, 3, :], lnrs[:, 0, :], lnrs[:, 1, :], lnrs[:, 2, :])
            for i in range(NT):
                dve.tensor_scalar(xn[:, i, :], xs[:, i, :], lnmv[:, i, 0:1], lnrs[:, 3, i:i + 1],
                                  ALU.subtract, ALU.mult).then_inc(xn_ok, 1)
            dve.wait_ge(ld_idx, 32)
            dve.tensor_copy(ef[:, 0, :], src_i[:, 0, :])
            link(dve.tensor_copy(ef[:, 1, :], src_i[:, 1, :]))
            link(dve.tensor_scalar(ef[:, 2, :], ef[:, 1, :], float(HALF), None, ALU.is_ge))
            dve.scalar_tensor_tensor(out=ef[:, 3, :], in0=ef[:, 2, :], scalar=-float(HALF), in1=ef[:, 1, :],
                                     op0=ALU.mult, op1=ALU.add)
            link(dve.tensor_scalar(ef[:, 4, :], ef[:, 2, :], PACK - 1.0, 1.0, ALU.mult, ALU.add))
            dve.wait_ge(const_ok, 3)
            link(dve.tensor_copy(iota_n[:, :], iota_i[:, :]))

            def low_counts(c):
                dve.wait_ge(rounded, 2 * c)
                dve.scalar_tensor_tensor(out=pk[:, :, :], in0=pkh[:, :, :], scalar=-float(PACK), in1=pk[:, :, :],
                                         op0=ALU.mult, op1=ALU.add).then_inc(unpacked, 1)

            def one_hots(c, tiles, before):
                for k in range(tiles):
                    t = CHUNK * c + k
                    dve.wait_ge(oh_free, t + 1)
                    dve.tensor_scalar(ohs[:, k % RING, :], iota_n[:, :], edge(0, t), None, ALU.is_equal)
                    dve.tensor_scalar(ohd[:, k % RING, 0:HALF], iota_n[:, 0:HALF], edge(3, t), edge(4, t),
                                      ALU.is_equal, ALU.mult).then_inc(oh_ready, 1)
                    if before and k == 8:
                        low_counts(c)

            dve.wait_ge(const_ok, 3)
            one_hots(0, CHUNK, False)
            with dve.Fori(1, CHUNKS) as c:
                one_hots(c, CHUNK, True)
            one_hots(CHUNKS, LASTC, True)
            low_counts(CHUNKS + 1)

            ps = read(dve, ("deg", 0))
            emptied(dve.tensor_copy(dinv[:, 0, :], ps[0:TP, 0:NT]), ("deg", 0))
            taken(dve, ("deg", 0))
            rsqrt(dve, link, dinv[:, 3, :], dinv[:, 0, :], dinv[:, 1, :], dinv[:, 2, :])
            for i in range(NT):
                for s in range(2):
                    ps = read(dve, ("h", i, s))
                    emptied(dve.tensor_scalar(hrow[:, i, 384 * s:384 * s + 384], ps[0:TP, 0:384], dinv[:, 3, i:i + 1],
                                              None, ALU.mult), ("h", i, s))

            for n, name in ((0, "sqk"), (1, "sqq")):
                ps = read(dve, (name, 0))
                emptied(dve.tensor_copy(nbias[:, n, :], ps[0:TP, 0:60]), (name, 0))
            for i in range(NT):
                taken(dve, ("ddk", i, H - 1))
                last = dve.tensor_reduce(kmax5[:, i:i + 1], kfeat[:, i, :, 0:M], AX.XY, ALU.max)
            link(last)
            dve.tensor_reduce(kmax[0:TP, 0:1], kmax5[:, :], AX.X, ALU.max).then_inc(kmax_ok, 1)
            dve.wait_ge(kall_ok, 1)
            taken(dve, ("sqk", 0))
            taken(dve, ("sqq", 0))
            dve.tensor_scalar(nbias[:, 2, :], nbias[:, 0, :], -1.0, kmax[0:TP, 1:2], ALU.mult, ALU.subtract).then_inc(kbias_ok, 1)

            ratio = 1.0 / math.sqrt(M)
            dve.wait_ge(x_biased, 2 * NT)
            for i in range(NT):
                for s in range(2):
                    ps = read(dve, ("gnn", i, s))
                    part = xs[:, i, 384 * s:384 * s + 384]
                    emptied(dve.scalar_tensor_tensor(out=part, in0=ps[0:TP, 0:384], scalar=dinv[:, 3, i:i + 1], in1=part,
                                                     op0=ALU.mult, op1=ALU.add), ("gnn", i, s))
                dve.wait_ge(kexp_ok, i + 1)
                feat = kfeat[:, i, :, 0:M]
                dve.memset(kfeat[:, i, :, M:MP], 0.0)
                dve.tensor_scalar(feat, feat, FEAT_EPS, ratio, ALU.add, ALU.mult).then_inc(k1_ok, 1)
            for h in range(H):
                ps = read(dve, ("kv", h))
                emptied(dve.tensor_copy(kv[:, h, :, :], ps[0:MC, 0:3 * (HD + 1)].rearrange("p (m d) -> p m d", m=3)), ("kv", h))

            def q_bias(i):
                for h in range(H):
                    ps = read(dve, ("ddq", i, h))
                    n = H * i + h
                    link(dve.tensor_reduce(nbias[:, 3, n:n + 1], ps[0:TP, 0:M], AX.X, ALU.max, negate=True))
                    dve.tensor_tensor(nbias[:, 3, n:n + 1], nbias[:, 3, n:n + 1], nbias[:, 1, n:n + 1],
                                      ALU.subtract).then_inc(qbias_ok, 1)

            def q_features(i):
                taken(dve, ("ddq", i, H - 1))
                feat = q1[i % 2][:, :, 0:M]
                dve.memset(q1[i % 2][:, :, M:MP], 0.0)
                dve.tensor_scalar(feat, feat, FEAT_EPS, ratio, ALU.add, ALU.mult).then_inc(q1_ok, 1)

            q_bias(0)
            q_features(0)
            for i in range(NT):
                if i + 1 < NT:
                    q_bias(i + 1)
                for h in range(H):
                    if h % 2:
                        take_q1t(dve, i, h, lambda o, a: dve.tensor_copy(o, a))
                    if h % 6 == 5:
                        g = h // 6
                        ps = read(dve, ("o", i, g))
                        sums = ps[0:TP, 0:6 * (HD + 1)].rearrange("p (h d) -> p h d", h=6)
                        link(dve.reciprocal(rden[:, :], sums[:, :, HD]))
                        emptied(dve.tensor_tensor(
                            ao[:, i, 384 * g:384 * g + 384].rearrange("p (h d) -> p h d", h=6), sums[:, :, 0:HD],
                            rden[:, :].unsqueeze(2).broadcast_to([TP, 6, HD]), ALU.mult), ("o", i, g))
                if i + 1 < NT:
                    q_features(i + 1)

            dve.wait_ge(ld_eb, 96)
            link(dve.tensor_copy(bh[:, :], bl[:, :]))
            link(dve.tensor_tensor(bl2[:, :], bl[:, :], bh[:, :], ALU.subtract))
            dve.tensor_copy(bsplit[0:E, :], bl[0:E, :])
            dve.tensor_copy(bsplit[32:32 + E, :], bl2[32:32 + E, :])
            link(dve.tensor_copy(bh[64:64 + E, :], bl2[64:64 + E, :]))
            link(dve.tensor_tensor(bl[64:64 + E, :], bl2[64:64 + E, :], bh[64:64 + E, :], ALU.subtract))
            dve.tensor_copy(bsplit[64:64 + E, :], bl[64:64 + E, :]).then_inc(bsplit_ok, 1)
            split_lo(dve, False, 0, range(C))

            for i in range(NT):
                for s in range(2):
                    ps = read(dve, ("pj", i, s))
                    part = xs[:, i, 384 * s:384 * s + 384]
                    last = dve.tensor_tensor(part, ps[0:TP, 0:384], part, ALU.add)
                    emptied(last, ("pj", i, s))
                taken(dve, ("pj", i, 1))
                dve.sem_inc(x1_ok, 1)
                norm(xs[:, i, :], xn2[:, i, :], TP, link).then_inc(xn2_ok, 1)

            def x_low(b):
                dve.wait_ge(xthi_ok, b + 1)
                dve.tensor_tensor(xtlo[:, 0:4, :].rearrange("p c t -> p (c t)"), tr_ps[0][:, :],
                                  xthi[:, 0:4, :].rearrange("p c t -> p (c t)").bitcast(F32), ALU.subtract)
                dve.tensor_tensor(xtlo[:, 4:6, :].rearrange("p c t -> p (c t)"), tr_ps[1][:, 0:256],
                                  xthi[:, 4:6, :].rearrange("p c t -> p (c t)").bitcast(F32), ALU.subtract).then_inc(xtlo_ok, 1)

            STEPS = 12

            def hidden_scale(j, e):
                dve.wait_ge(h_turned, j)
                for c in range(FC):
                    last = dve.tensor_scalar(hid[:, 128 * c:128 * c + 128], tr_ps[c // 4][:, 128 * (c % 4):128 * (c % 4) + 128],
                                             lnw[:, bass.ds(e, 1), c], lnb[:, bass.ds(e, 1), c], ALU.mult, ALU.add)
                last.then_inc(v_scaled, 1)

            def hidden_low(j):
                dve.wait_ge(hthi_ok, j)
                dve.tensor_tensor(htlo[:, :, :].rearrange("p c t -> p (c t)"), hid[:, :],
                                  hthi[:, :, :].rearrange("p c t -> p (c t)").bitcast(F32), ALU.subtract).then_inc(htlo_ok, 1)

            def normalise(j):
                dve.wait_ge(gelu_ok, 3 * j + 3)
                norm(hid[:, :], hid[:, :], 128, Chain(dve, ln_own, STEPS * j)).then_inc(ln_ok, 1)

            ps = read(dve, ("gate", 0))
            dve.wait_ge(ld_gb, 16)
            link(dve.tensor_tensor(sc[:, :, :], ps[0:TP, 0:NT * E].rearrange("p (i e) -> p i e", e=E),
                                   gateb[:, :].unsqueeze(1).broadcast_to([TP, NT, E]), ALU.add))
            dve.sem_inc(free[plan[("gate", 0)][0]], 1)
            link(dve.memset(sc[:, :, 0:1], NEG))
            link(dve.tensor_reduce(mx[:, :], sc[:, :, :], AX.X, ALU.max))
            dve.tensor_tensor(sc[:, :, :], sc[:, :, :], mx[:, :].unsqueeze(2).broadcast_to([TP, NT, E]),
                              ALU.subtract).then_inc(sc_ok, 1)
            dve.wait_ge(ex_ok, 1)
            link(dve.tensor_reduce(mx[:, :], sc[:, :, :], AX.X, ALU.add))
            link(dve.reciprocal(mx[:, :], mx[:, :]))
            link(dve.tensor_tensor(pr[:, :, :], sc[:, :, :], mx[:, :].unsqueeze(2).broadcast_to([TP, NT, E]), ALU.mult))
            x_low(0)
            mine = pr[:, :, :].unsqueeze(3).broadcast_to([TP, NT, E, E])
            other = pr[:, :, :].unsqueeze(2).broadcast_to([TP, NT, E, E])
            before = tri[0:TP, :, :].unsqueeze(1).broadcast_to([TP, NT, E, E])
            dve.tensor_tensor(cmp1[:, :, :, :], other, mine, ALU.is_gt)
            link(dve.tensor_tensor(cmp2[:, :, :, :], other, mine, ALU.is_equal))
            link(dve.tensor_tensor(cmp2[:, :, :, :], cmp2[:, :, :, :], before, ALU.mult))
            link(dve.tensor_tensor(cmp1[:, :, :, :], cmp1[:, :, :, :], cmp2[:, :, :, :], ALU.add))
            link(dve.tensor_reduce(rank[:, :, :], cmp1[:, :, :, :], AX.X, ALU.add))
            link(dve.tensor_scalar(member[:, :, :], rank[:, :, :], float(TOPK), None, ALU.is_lt))
            link(dve.tensor_tensor(comb[:, :, :], member[:, :, :], pr[:, :, :], ALU.mult))
            link(dve.tensor_scalar(comb[:, :, 0:1], comb[:, :, 0:1], 1.0, None, ALU.add))
            dve.memset(member[:, :, 0:1], 1.0).then_inc(member_ok, 1)
            ps = read(dve, ("cnt", 0))
            link(dve.tensor_scalar(nblk[:, :], ps[:, 0:E], 1.0 / SLOTS, (SLOTS - 1.0) / SLOTS - 0.5 + 0.5 / SLOTS,
                                   ALU.mult, ALU.add))
            dve.sem_inc(free[plan[("cnt", 0)][0]], 1)
            link(dve.tensor_scalar(nblk[:, :], nblk[:, :], ROUND, ROUND, ALU.add, ALU.subtract))
            link(dve.tensor_scalar(nblk[:, :], nblk[:, :], 1.0, None, ALU.max))
            link(dve.tensor_tensor(btmp[:, :, :], tri[:, :, :], nblk[:, :].unsqueeze(1).broadcast_to([128, E, E]), ALU.mult))
            link(dve.tensor_reduce(base[:, :], btmp[:, :, :], AX.X, ALU.add))
            ps = read(dve, ("pos", 0))
            link(dve.tensor_copy(pos[:, :, :], ps[0:TP, 0:NT * E].rearrange("p (i e) -> p i e", e=E)))
            dve.sem_inc(free[plan[("pos", 0)][0]], 1)
            link(dve.tensor_scalar(quo[:, :, :], pos[:, :, :], 1.0 / SLOTS, -0.5 + 0.5 / SLOTS, ALU.mult, ALU.add))
            link(dve.tensor_scalar(quo[:, :, :], quo[:, :, :], ROUND, ROUND, ALU.add, ALU.subtract))
            link(dve.tensor_scalar(quo[:, :, :], quo[:, :, :], 1.0 - SLOTS * TW, None, ALU.mult))
            link(dve.scalar_tensor_tensor(out=pos[:, :, :], in0=pos[:, :, :], scalar=float(TW), in1=quo[:, :, :],
                                          op0=ALU.mult, op1=ALU.add))
            link(dve.tensor_tensor(pos[:, :, :], pos[:, :, :], base[0:TP, :].unsqueeze(1).broadcast_to([TP, NT, E]), ALU.add))
            dve.wait_ge(route_const, 2)
            wcol = pair[:, :, :, 1].bitcast(F32)
            for k in range(TOPK):
                dve.scalar_tensor_tensor(out=pick[:, 0, :, :], in0=rank[:, :, :], scalar=float(k), in1=pos[:, :, :],
                                         op0=ALU.is_equal, op1=ALU.mult)
                link(dve.scalar_tensor_tensor(out=pick[:, 1, :, :], in0=rank[:, :, :], scalar=float(k), in1=comb[:, :, :],
                                              op0=ALU.is_equal, op1=ALU.mult))
                dve.tensor_reduce(slotf[:, k, :], pick[:, 0, :, :], AX.X, ALU.add)
                link(dve.tensor_reduce(wcol[:, k, :], pick[:, 1, :, :], AX.X, ALU.add))
            dve.tensor_copy(wcol[:, TOPK, :], comb[:, :, 0])
            link(dve.tensor_copy(slotf[:, TOPK, :], pos[:, :, 0]))
            dve.tensor_copy(slot[:, :, :], slotf[:, :, :]).then_inc(slots_ok, 1)
            normalise(0)
            x_low(1)
            link(dve.tensor_copy(biota[:, :], biota_i[:, :]))
            link(dve.tensor_tensor(bcmp[:, :, :], base[:, :].unsqueeze(1).broadcast_to([128, TW, E]),
                                   biota[:, :].unsqueeze(2).broadcast_to([128, TW, E]), ALU.is_le))
            link(dve.tensor_reduce(bsum[:, :], bcmp[:, :, :], AX.X, ALU.add))
            dve.tensor_scalar(btab[:, EXPERT, 0:TW], bsum[:, :], -1.0, None, ALU.add)
            dve.tensor_tensor(btab[:, LAST_OF, 0:TW - 1], bsum[:, 1:TW], bsum[:, 0:TW - 1], ALU.subtract)
            dve.memset(btab[:, NEW_BEFORE, 0:2], 0)
            dve.tensor_tensor(btab[:, NEW_BEFORE, 2:TW], bsum[:, 1:TW - 1], bsum[:, 0:TW - 2], ALU.subtract)
            dve.tensor_tensor(btab[:, LAST_OF, TW:TW + 1], base[:, E - 1:E], nblk[:, E - 1:E], ALU.add).then_inc(btab_ok, 1)

            split_lo(dve, True, 0, range(C))
            dve.wait_ge(ld_ln, 32)
            dve.wait_ge(btab_ok, 1)
            nb = dve.value_load(btab[0:1, LAST_OF, TW:TW + 1], min_val=NT + E - 1, max_val=BLOCKS)
            with dve.Fori(1, nb) as j:
                hidden_scale(j, entry(dve, EXPERT, j - 1, E - 1))
                with_second(dve, j, low(4))
                hidden_low(j)
                with_first(dve, j, low(0, 1, 3))
                normalise(j)
                x_low(j + 1)
                with_first(dve, j, low(4))
                with_second(dve, j + 1, low(0, 1, 3))
            hidden_scale(nb, E - 1)
            with_second(dve, nb, low(4))
            hidden_low(nb)

        @block.scalar
        def _(act):
            ps = read(act, ("pt", 0))
            emptied(act.activation(projt[:, :], ps[:, 0:M], ACT.Copy), ("pt", 0))
            take_turned(act, "xt", xnt)

            def counts(c):
                act.wait_ge(adj_full, c + 1)
                act.wait_ge(pk_free, 2 * c + 1)
                for b in range(NT):
                    act.activation(pkh[:, b, :], bank[b][0:TP, 0:HALF], ACT.Copy, scale=1.0 / PACK, bias=-0.4375)
                    act.activation(pk[:, b, :], bank[b][0:TP, 0:HALF], ACT.Copy).then_inc(adj_read, 1)
                act.wait_ge(adj_read, NT * c + 2 * NT)
                act.activation(pkh[:, :, :], pkh[:, :, :], ACT.Copy, bias=ROUND).then_inc(rounded, 1)
                act.wait_ge(rounded, 2 * c + 1)
                act.activation(pkh[:, :, :], pkh[:, :, :], ACT.Copy, bias=-ROUND).then_inc(rounded, 1)

            counts(0)
            with act.Fori(1, CHUNKS) as c:
                counts(c)
            counts(CHUNKS)
            act.wait_ge(x_biased, 2 * NT)
            for i in range(NT):
                for s in range(2):
                    ps = read(act, ("v", i, s))
                    emptied(act.activation(vext[:, i, 6 * s:6 * s + 6, 0:HD],
                                           ps[0:TP, 0:384].rearrange("p (h d) -> p h d", d=HD), ACT.Copy), ("v", i, s))
            squares = [(n, name, of, o) for n, (name, of) in enumerate((("k", kt), ("q", qt))) for o in range(C)]

            def square(g):
                n, name, of, o = squares[g]
                taken(act, (name, o, 1))
                taken(act, (name, o, 0))
                if g >= 2:
                    act.wait_ge(sq_used, g - 1)
                act.activation(sq[:, g % 2, :], of[:, o, :], ACT.Square).then_inc(sq_ok, 1)

            act.wait_ge(adj_ok, 1)
            for name, to in (("k", kt), ("q", qt)):
                for o in range(C):
                    for s, (a, b) in enumerate(TSPLIT):
                        ps = read(act, (name, o, s))
                        emptied(act.activation(to[:, o, a:b], ps[:, 0:b - a], ACT.Copy, scale=HD ** -0.25), (name, o, s))
                    if name == "q":
                        square(o)
            for g in range(C, 2 * C):
                square(g)
            for i in range(NT):
                for h in range(H):
                    ps = read(act, ("ddk", i, h))
                    emptied(act.activation(kfeat[:, i, h, 0:M], ps[0:TP, 0:M], ACT.Copy), ("ddk", i, h))
            act.wait_ge(kbias_ok, 1)
            for i in range(NT):
                for h in range(H):
                    n = H * i + h
                    last = act.activation(kfeat[:, i, h, 0:M], kfeat[:, i, h, 0:M], ACT.Exp, bias=nbias[:, 2, n:n + 1])
                last.then_inc(kexp_ok, 1)

            def q_exp(i):
                if i >= 1:
                    done(act, ("kv", H - 1))
                if i >= 2:
                    act.wait_ge(q1_free, i - 1)
                for h in range(H):
                    n = H * i + h
                    ps = read(act, ("ddq", i, h))
                    act.wait_ge(qbias_ok, n + 1)
                    emptied(act.activation(q1[i % 2][:, h, 0:M], ps[0:TP, 0:M], ACT.Exp, bias=nbias[:, 3, n:n + 1]), ("ddq", i, h))

            q_exp(0)
            for i in range(NT):
                if i + 1 < NT:
                    q_exp(i + 1)
                for h in range(0, H, 2):
                    take_q1t(act, i, h, lambda o, a: act.activation(o, a, ACT.Copy))
            take_turned(act, "at", aot)
            act.wait_ge(bsplit_ok, 1)
            act.wait_ge(st_padrow, 16)
            split_hi(act, False, 0, range(C))
            for i in range(NT):
                for s, n in ((0, 4), (1, 2)):
                    ps = read(act, ("x2", i, s))
                    emptied(act.activation(xn2t[:, 4 * s:4 * s + n, TP * i:TP * i + TP],
                                           ps[:, 0:n * TP].rearrange("p (c t) -> p c t", t=TP), ACT.Copy), ("x2", i, s))
            act.wait_ge(sc_ok, 1)
            act.activation(sc[:, :, :], sc[:, :, :], ACT.Exp).then_inc(ex_ok, 1)

            def hidden_high(j):
                act.wait_ge(v_scaled, j)
                act.activation(hthi[:, :, :].rearrange("p c t -> p (c t)"), hid[:, :], ACT.Copy).then_inc(hthi_ok, 1)

            def gelu(j):
                for n in range(3):
                    act.wait_ge(fc1_ok, 3 * j + n + 1)
                    act.activation(hid[:, 512 * n:512 * n + 512], hid_ps[n][:, :], ACT.Gelu).then_inc(gelu_ok, 1)

            def x_high(b):
                act.wait_ge(x_turned, b + 1)
                act.activation(xthi[:, 0:4, :].rearrange("p c t -> p (c t)"), tr_ps[0][:, :], ACT.Copy)
                act.activation(xthi[:, 4:6, :].rearrange("p c t -> p (c t)"), tr_ps[1][:, 0:256], ACT.Copy).then_inc(xthi_ok, 1)

            def weigh(j):
                act.wait_ge(fc2_ok, j)
                act.wait_ge(sidx_ok, j)
                act.activation(ysb[:, 0:384], y_ps[0][:, 0:384], ACT.Copy, scale=sidx[:, 1:2].bitcast(F32))
                act.activation(ysb[:, 384:768], y_ps[1][:, 0:384], ACT.Copy, scale=sidx[:, 1:2].bitcast(F32)).then_inc(y_ok, 1)

            act.sem_inc(y_ok, 1)
            x_high(0)
            split_hi(act, True, 0, range(C))
            gelu(0)
            x_high(1)
            act.wait_ge(btab_ok, 1)
            nb = act.value_load(btab[0:1, LAST_OF, TW:TW + 1], min_val=NT + E - 1, max_val=BLOCKS)

            with act.Fori(1, nb) as j:
                with_second(act, j, high(4))
                hidden_high(j)
                with_second(act, j, high(5))
                with_first(act, j, high(0, 1, 2, 3))
                act.wait_ge(htlo_ok, j)
                gelu(j)
                x_high(j + 1)
                with_first(act, j, high(4, 5))
                with_second(act, j + 1, high(0, 1, 2, 3))
                weigh(j)
            with_second(act, nb, high(4))
            hidden_high(nb)
            with_second(act, nb, high(5))
            weigh(nb)

        @block.tensor
        def _(pe):
            pe.wait_ge(const_ok, 3)
            pe.wait_ge(ld_proj, 96)
            ps = fill(pe, ("pt", 0))
            for m in range(3):
                rows = min(MC, M - MC * m)
                last = pe.transpose(ps[:, MC * m:MC * m + rows], prow[0:rows, m, :], ident[0:rows, 0:rows])
            filled(last, ("pt", 0))
            turn_tokens(pe, "xt", xn, xn_ok, 1)

            pe.sem_inc(oh_free, RING)
            pe.sem_inc(adj_read, NT)

            def count(c, tiles):
                for k in range(tiles):
                    pe.wait_ge(oh_ready, CHUNK * c + k + 1)
                    for b in range(NT):
                        if k == 0:
                            pe.wait_ge(adj_read, NT * c + b + 1)
                        last = pe.matmul(bank[b][0:TP, 0:HALF], ohs[:, k % RING, TP * b:TP * b + TP],
                                         ohd[:, k % RING, 0:HALF], start=k == 0, stop=k == tiles - 1)
                    if k == tiles - 1:
                        last.then_inc(adj_full, 1)
                        pe.wait_ge(adj_full, c + 1)
                        pe.sem_inc(oh_free, 1)
                    else:
                        last.then_inc(oh_free, 1)

            count(0, CHUNK)
            with pe.Fori(1, CHUNKS) as c:
                count(c, CHUNK)
            count(CHUNKS, LASTC)

            pe.wait_ge(ld_qkv, 16)
            all_turned(pe, "xt")

            def half_squares(g):
                name, o = ("sqk", "sqq")[g // C], g % C
                ps = fill(pe, (name, 0)) if o == 0 else bank[plan[(name, 0)][0]]
                pe.wait_ge(sq_ok, g + 1)
                for i in range(NT):
                    last = pe.matmul(ps[0:TP, H * i + 2 * o:H * i + 2 * o + 2], sq[:, g % 2, TP * i:TP * i + TP],
                                     sel2[:, :], start=True, stop=True)
                if o == C - 1:
                    filled(last, (name, 0))
                    done(pe, (name, 0))
                    pe.sem_inc(sq_used, 1)
                else:
                    last.then_inc(sq_used, 1)

            def rows_times(name, xt_, w, first, also=lambda t: None):
                for i in range(NT):
                    for s in range(2):
                        ps = fill(pe, (name, i, s))
                        for c in range(C):
                            last = pe.matmul(ps[0:TP, 0:384], xt_[:, c, TP * i:TP * i + TP],
                                             w[:, c, first + 384 * s:first + 384 * s + 384], start=c == 0, stop=c == C - 1)
                        filled(last, (name, i, s))
                        also(2 * i + s)

            rows_times("v", xnt, wqkv, 2 * D)
            pe.wait_ge(adj_ok, 1)
            for name, first in (("k", D), ("q", 0)):
                for o in range(C):
                    for s, (a, b) in enumerate(TSPLIT):
                        ps = fill(pe, (name, o, s))
                        for c in range(C):
                            last = pe.matmul(ps[:, 0:b - a], wqkv[:, c, first + 128 * o:first + 128 * o + 128],
                                             xnt[:, c, a:b], start=c == 0, stop=c == C - 1)
                        filled(last, (name, o, s))
                    if name == "q":
                        half_squares(o)

            ps = fill(pe, ("deg", 0))
            for i in range(NT):
                for b in range(NT):
                    last = pe.matmul(ps[0:TP, i:i + 1], adj[:, b, TP * i:TP * i + TP], ones[0:TP, :],
                                     start=b == 0, stop=b == NT - 1)
            filled(last, ("deg", 0))
            pe.wait_ge(ld_wg, 16)
            rows_times("h", xnt, wg, 0, lambda t: half_squares(C + t) if t < C else None)

            def project(name, of, i, h):
                ps = fill(pe, (name, i, h))
                r = HD * (h % 2)
                filled(pe.matmul(ps[0:TP, 0:M], of[r:r + HD, h // 2, TP * i:TP * i + TP], projt[r:r + HD, :],
                                 start=True, stop=True), (name, i, h))

            taken(pe, ("pt", 0))
            for i in range(NT):
                for h in range(H):
                    project("ddk", kt, i, h)
            taken(pe, ("h", NT - 1, 0))
            taken(pe, ("h", NT - 1, 1))
            for i in range(NT):
                for s in range(2):
                    ps = fill(pe, ("gnn", i, s))
                    for b in range(NT):
                        last = pe.matmul(ps[0:TP, 0:384], adj[:, b, TP * i:TP * i + TP], hrow[:, b, 384 * s:384 * s + 384],
                                         start=b == 0, stop=b == NT - 1)
                    filled(last, ("gnn", i, s))
            pe.wait_ge(k1_ok, NT)
            pe.wait_ge(vones_ok, 1)
            for s in range(2):
                taken(pe, ("v", NT - 1, s))
            for h in range(H):
                ps = fill(pe, ("kv", h))
                for m in range(3):
                    for i in range(NT):
                        last = pe.matmul(ps[0:MC, (HD + 1) * m:(HD + 1) * (m + 1)], kfeat[:, i, h, MC * m:MC * m + MC],
                                         vext[:, i, h, :], start=i == 0, stop=i == NT - 1)
                filled(last, ("kv", h))

            def q_project(i):
                for h in range(H):
                    project("ddq", qt, i, h)

            def turn_q(i, h):
                ps = fill(pe, ("q1t", i, h))
                for m in range(3):
                    last = pe.transpose(ps[0:MC, TP * m:TP * m + TP], q1[i % 2][:, h, MC * m:MC * m + MC], ident[0:TP, 0:TP])
                filled(last, ("q1t", i, h))
                if h == H - 1:
                    done(pe, ("q1t", i, h))
                    pe.sem_inc(q1_free, 1)

            def attend(i, h):
                ps = fill(pe, ("o", i, h // 6)) if h % 6 == 0 else bank[plan[("o", i, h // 6)][0]]
                taken(pe, ("q1t", i, h))
                g = h % 6
                for m in range(3):
                    last = pe.matmul(ps[0:TP, (HD + 1) * g:(HD + 1) * (g + 1)], q1t[:, (H * i + h) % 3, m, :],
                                     kv[:, h, m, :], start=m == 0, stop=m == 2)
                if g == 5:
                    filled(last, ("o", i, h // 6))
                    done(pe, ("o", i, h // 6))
                    pe.sem_inc(q1t_used, 1)
                else:
                    last.then_inc(q1t_used, 1)

            q_project(0)
            for h in range(H):
                taken(pe, ("kv", h))
            for i in range(NT):
                if i + 1 < NT:
                    q_project(i + 1)
                pe.wait_ge(q1_ok, i + 1)
                turn_q(i, 0)
                for h in range(H):
                    if h + 1 < H:
                        turn_q(i, h + 1)
                    attend(i, h)

            for i in range(NT):
                for g in range(2):
                    taken(pe, ("o", i, g))
            pe.wait_ge(const_ok, 3)
            turn_tokens(pe, "at", ao, const_ok, 0)
            all_turned(pe, "at")
            pe.wait_ge(ld_wp, 16)
            pe.wait_ge(ld_gate, 16)

            def project_out(i):
                for s in range(2):
                    ps = fill(pe, ("pj", i, s))
                    for c in range(C):
                        last = pe.matmul(ps[0:TP, 0:384], aot[:, c, TP * i:TP * i + TP], wp[:, c, 384 * s:384 * s + 384],
                                         start=c == 0, stop=c == C - 1)
                    filled(last, ("pj", i, s))

            def turn_xn2(i):
                for s, n in ((0, 4), (1, 2)):
                    ps = fill(pe, ("x2", i, s))
                    pe.wait_ge(xn2_ok, i + 1)
                    for c in range(n):
                        last = pe.transpose(ps[:, c * TP:c * TP + TP], xn2[:, i, 4 * s + c::C], ident[0:TP, 0:TP])
                    filled(last, ("x2", i, s))

            def gate(i):
                ps = fill(pe, ("gate", 0)) if i == 0 else bank[plan[("gate", 0)][0]]
                for s in range(2):
                    taken(pe, ("x2", i, s))
                for c in range(C):
                    last = pe.matmul(ps[0:TP, E * i:E * i + E], xn2t[:, c, TP * i:TP * i + TP], gatew[:, c, :],
                                     start=c == 0, stop=c == C - 1)
                if i == NT - 1:
                    filled(last, ("gate", 0))

            for i in range(NT + 2):
                if i < NT:
                    project_out(i)
                if i >= 2:
                    turn_xn2(i - 2)
                if i >= 3:
                    gate(i - 3)
            gate(NT - 1)

            def turn_x(b):
                pe.wait_ge(gathered, 16 * b + 16)
                for c in range(C):
                    last = pe.transpose(tr_ps[c // 4][:, 128 * (c % 4):128 * (c % 4) + 128], xg[:, c::C], ident[:, :])
                last.then_inc(x_turned, 1)

            def turn_h(j):
                pe.wait_ge(ln_ok, j)
                for c in range(FC):
                    last = pe.transpose(tr_ps[c // 4][:, 128 * (c % 4):128 * (c % 4) + 128], hid[:, c::FC], ident[:, :])
                last.then_inc(h_turned, 1)

            def bias(ps, e, a, b):
                return pe.matmul(ps, selw[:, bass.ds(e, 1), :].rearrange("p a t -> p (a t)"), bsplit[:, a:b],
                                 start=False, stop=True)

            def fc1(j, e):
                pe.wait_ge(xtlo_ok, j + 1)
                for c in range(C):
                    wait_split(pe, False, e, c)
                    for k, (a, w) in enumerate(((xthi, w1hi), (xthi, w1lo), (xtlo, w1hi))):
                        for n in range(3):
                            last = pe.matmul(hid_ps[n][:, :], a[:, c, :], w[:, c, 512 * n:512 * n + 512],
                                             start=c == 0 and k == 0, stop=False)
                    last.then_inc(w1_used, 1)
                for n in range(3):
                    bias(hid_ps[n][:, :], e, 512 * n, 512 * n + 512).then_inc(fc1_ok, 1)

            def fc2(j, e):
                pe.wait_ge(htlo_ok, j)
                for c in range(FC):
                    if c % 2 == 0:
                        wait_split(pe, True, e, c // 2)
                    for k, (a, w) in enumerate(((hthi, w2hi), (hthi, w2lo), (htlo, w2hi))):
                        for s in range(2):
                            last = pe.matmul(y_ps[s][:, 0:384], a[:, c, :], w[:, c, 384 * s:384 * s + 384],
                                             start=c == 0 and k == 0, stop=False)
                    if c % 2:
                        last.then_inc(w2_used, 1)
                bias(y_ps[0][:, 0:384], e, F, F + 384)
                bias(y_ps[1][:, 0:384], e, F + 384, F + D).then_inc(fc2_ok, 1)

            pe.sem_inc(w2_used, 2 * C)

            for b in range(8):
                pe.wait_ge(free[b], uses[b] - (b == plan[("cnt", 0)][0]) - (b == plan[("pos", 0)][0]))
            turn_x(0)
            pe.wait_ge(sel_ok, 4)
            fc1(0, 0)
            turn_x(1)
            pe.wait_ge(member_ok, 1)
            ps = fill(pe, ("cnt", 0))
            for i in range(NT):
                last = pe.matmul(ps[:, 0:E], onesb[:, :], member[:, i, :], start=i == 0, stop=i == NT - 1)
            filled(last, ("cnt", 0))
            ps = fill(pe, ("pos", 0))
            for i in range(NT):
                for b in range(i + 1):
                    last = pe.matmul(ps[0:TP, E * i:E * i + E], (prefix if b == i else onesb)[:, 0:TP], member[:, b, :],
                                     start=b == 0, stop=b == i)
            filled(last, ("pos", 0))

            taken(pe, ("cnt", 0))
            taken(pe, ("pos", 0))
            pe.wait_ge(btab_ok, 1)
            nb = pe.value_load(btab[0:1, LAST_OF, TW:TW + 1], min_val=NT + E - 1, max_val=BLOCKS)
            with pe.Fori(1, nb) as j:
                e_before = entry(pe, EXPERT, j - 1, E - 1)
                e = entry(pe, EXPERT, j, E - 1)
                pe.wait_ge(xtlo_ok, j + 1)
                turn_h(j)
                fc1(j, e)
                pe.wait_ge(v_scaled, j)
                turn_x(j + 1)
                pe.wait_ge(y_ok, j)
                fc2(j, e_before)
            pe.wait_ge(xtlo_ok, nb + 1)
            turn_h(nb)
            pe.wait_ge(y_ok, nb)
            fc2(nb, E - 1)


_INS = ["x", "src", "dst", "L0_gnn_W", "L0_gnn_b", "L0_mix_W_qkv", "L0_mix_W_proj", "L0_mix_b_proj",
        "L0_mix_proj_mat", "L0_ffn_gate_w", "L0_ffn_gate_b", "L0_ffn_fc1_w", "L0_ffn_fc1_b", "L0_ffn_ln_w",
        "L0_ffn_ln_b", "L0_ffn_fc2_w", "L0_ffn_fc2_b"]


def kernel(**inputs):
    import numpy as np
    import concourse.bacc as bacc
    from concourse.bass_utils import run_bass_kernel_spmd

    nc = bacc.Bacc("TRN2", target_bir_lowering=False, num_devices=1)
    arrays, args = {}, []
    for name in _INS:
        a = np.ascontiguousarray(inputs[name])
        arrays[f"in_{name}"] = a
        args.append(nc.dram_tensor(f"in_{name}", a.shape, mybir.dt.from_np(a.dtype), kind="ExternalInput").ap())
    out = nc.dram_tensor("out", (N, D), F32, kind="ExternalOutput").ap()
    xn2_dram = nc.dram_tensor("xn2_dram", (N + 1, D), F32, kind="Internal").ap()
    table_dram = nc.dram_tensor("table_dram", (128 * TW, 2), I32, kind="Internal").ap()
    gps_kernel(nc, *args, out, xn2_dram, table_dram)
    r = run_bass_kernel_spmd(nc, [arrays], core_ids=[0])
    return r.results[0]["out"]
```

```python
import math
from contextlib import ExitStack

import concourse.bass as bass
from concourse import mybir

F32 = mybir.dt.float32
F32R = mybir.dt.float32r
BF16 = mybir.dt.bfloat16
F16 = mybir.dt.float16
I32 = mybir.dt.int32
U32 = mybir.dt.uint32
ALU = mybir.AluOpType
ACT = mybir.ActivationFunctionType
AX = mybir.AxisListType

N, D = 625, 768
TP, NT = 125, 5
C = D // 128
EDGES = 20625
ET = EDGES // TP
HALF = 313
PACK = 4096
CHUNK, CHUNKS = 28, 5
LASTC = ET - CHUNK * CHUNKS
KQ = 5
RING = 4
H, HD, M = 12, 64, 266
MAIN = 256
TAIL = M - MAIN
TAILS = H * TAIL
MC = 89
E, F = 16, 1536
FC = F // 128
LN_EPS, FEAT_EPS = 1e-5, 1e-4
NEG = -1e9
TOPK = 3
SLOTS = 128
BLOCKS = NT + (E - 1) + (N * TOPK - (E - 1)) // SLOTS
TW = BLOCKS + 2
ROUND = 12582912.0
EXPERT, LAST_OF, NEW_BEFORE = range(3)
RMAX = bass.bass_isa.ReduceOp.max
AHEAD = [(0, 1, 2), (3, 4), (5,), (), (), ()]
TSPLIT = [(0, 320), (320, N)]
ON_POOL = 3


class Chain:

    def __init__(self, eng, sem, base=0):
        self.eng, self.sem, self.base, self.n = eng, sem, base, 0

    def __call__(self, ins):
        ins.then_inc(self.sem, 1)
        self.n += 1
        self.eng.wait_ge(self.sem, self.base + self.n)


def row(v):
    return v.rearrange("(a n) -> a n", a=1)


def rsqrt(dve, link, y, v, half, tmp):
    seed_i, v_i = y.bitcast(I32), v.bitcast(I32)
    link(dve.tensor_scalar(seed_i, v_i, 1, None, ALU.arith_shift_right))
    link(dve.tensor_scalar(seed_i, seed_i, -1.0, float(0x5F3759DF), ALU.mult, ALU.add))
    link(dve.tensor_scalar(half, v, -0.5, None, ALU.mult))
    for _ in range(3):
        if v.shape[-1] == 1:
            link(dve.scalar_tensor_tensor(out=tmp, in0=y, scalar=half, in1=y, op0=ALU.mult, op1=ALU.mult))
        else:
            link(dve.tensor_tensor(tmp, y, y, ALU.mult))
            link(dve.tensor_tensor(tmp, tmp, half, ALU.mult))
        link(dve.scalar_tensor_tensor(out=y, in0=tmp, scalar=1.5, in1=y, op0=ALU.add, op1=ALU.mult))


def gps_kernel(nc, x, src, dst, gnn_w, gnn_b, w_qkv, w_proj, b_proj, proj_mat, gate_w, gate_b,
               fc1_w, fc1_b, ln_w, ln_b, fc2_w, fc2_b, out, xn2_dram, table_dram):
    ctx = ExitStack()
    with ctx:
        base0 = (nc.sbuf_base + 31) // 32 * 32

        def at(name, offset, shape, dt=F32):
            return nc.alloc_sbuf_tensor_at(name, shape, dt, offset=base0 + offset)

        KB6 = F * 4
        w1hi = at("w1hi", 0, [128, C, F], F32R)
        w1lo = at("w1lo", 6 * KB6, [128, C, F], F32R)
        w2hi = at("w2hi", 12 * KB6, [128, FC, D], F32R)
        w2lo = at("w2lo", 18 * KB6, [128, FC, D], F32R)
        w1raw = at("w1raw", 6 * KB6, [128, C, F])
        w2raw = at("w2raw", 18 * KB6, [128, FC, D])
        LOOP = 27 * KB6
        xg = at("xg", LOOP, [128, D])
        xthi = at("xthi", LOOP + 3072, [128, C, 128], F32R)
        xtlo = at("xtlo", LOOP + 6144, [128, C, 128], F32R)
        hid = at("hid", LOOP + 9216, [128, F])
        hthi = at("hthi", LOOP + 15360, [128, FC, 128], F32R)
        htlo = at("htlo", LOOP + 21504, [128, FC, 128], F32R)
        ysb = at("ysb", LOOP + 27648, [128, D])
        SMALL = LOOP + 30720 + 3104
        wqkv = at("wqkv", 0, [128, C, 3 * D])
        wg = at("wg", 55296, [128, C, D])
        kfeat = at("kfeat", 0, [TP, NT, H, M])
        ktail = at("ktail", 63872, [TP, NT, H, TAIL])
        q1tail = at("q1tail", 145984, [TP, 2, H, TAIL])
        xnt = at("xnt", 73728, [128, C, N + 1])
        kv = at("kv", 73728, [128, H, 2, HD + 1])
        kvt = at("kvt", 80000, [TAILS, H, HD + 1])
        q1t = at("q1t", 83200, [128, 2, 4, TP])
        q1tt = at("q1tt", 144960, [TAILS, 2, TP])
        aot = at("aot", 73728, [128, C, N])
        xn = at("xn", 88832, [TP, NT, D])
        xhi = at("xhi", 88832, [128, C, N + 1], F32R)
        xlo = at("xlo", 73728, [128, C, N + 1], F32R)
        wqkvlo = at("wqkvlo", 0, [128, C, 3 * D], F32R)
        wglo = at("wglo", 55296, [128, C, D], F32R)
        vhi = at("vhi", 162560, [128, 2, C, 384], F32R)
        kqhi = at("kqhi", 162560, [128, KQ, C, 128], F32R)
        ao = at("ao", 88832, [TP, NT, D])
        xn2 = at("xn2", 88832, [TP, NT, D])
        qt = at("qt", 104192, [128, C, N])
        xn2t = at("xn2t", 104192, [128, C, N])
        kt = at("kt", 119296, [128, C, N])
        q1 = [at("q1a", 119296, [TP, H, M]), at("q1b", 132128, [TP, H, M])]
        vext = at("vext", 134400, [TP, NT, H, HD + 1])
        adj = at("adj", 150016, [TP, NT, 2 * HALF])
        hrow = at("hrow", 162560, [TP, NT, D])
        wp = at("wp", 165888, [128, C, D])
        xs = at("xs", 184320, [TP, NT, D])
        ohs = at("ohs", 104192, [TP, RING, N], BF16)
        ohd = at("ohd", 109216, [TP, RING, HALF + 1], BF16)
        pk = at("pk", 111744, [TP, NT, HALF])
        pkh = at("pkh", 118016, [TP, NT, HALF])
        iota_n = at("iota_n", 124288, [TP, N], F16)
        iota_i = at("iota_i", 125568, [TP, N], I32)
        src_i = at("src_i", 128096, [TP, 2, ET], I32)
        ef = at("ef", 129440, [TP, 5, ET])
        bias2 = at("bias2", 132768, [TP, 2, D], F32)
        sq = at("sq", 177920, [128, 2, N])
        r0 = 24 * KB6

        def rt(name, shape, dt=F32):
            nonlocal r0
            size = 4 if dt != BF16 else 2
            t = at(name, r0, shape, dt)
            r0 += (math.prod(shape[1:]) * size + 31) // 32 * 32
            return t

        sc = rt("sc", [TP, NT, E])
        pr = rt("pr", [TP, NT, E])
        mx = rt("mx", [TP, NT])
        cmp1 = rt("cmp1", [TP, NT, E, E], BF16)
        cmp2 = rt("cmp2", [TP, NT, E, E], BF16)
        rank = rt("rank", [TP, NT, E])
        comb = rt("comb", [TP, NT, E])
        member = rt("member", [TP, NT, E], BF16)
        pos = rt("pos", [TP, NT, E])
        quo = rt("quo", [TP, NT, E])
        pick = rt("pick", [TP, 2, NT, E])
        slotf = rt("slotf", [TP, 4, NT])
        nblk = rt("nblk", [128, E])
        base = rt("base", [128, E])
        btmp = rt("btmp", [128, E, E])
        biota_i = rt("biota_i", [128, TW], I32)
        biota = rt("biota", [128, TW])
        bcmp = rt("bcmp", [128, TW, E])
        bsum = rt("bsum", [128, TW])
        gateb = rt("gateb", [TP, E])
        padt = rt("padt", [128, TW, 2], I32)
        selw = rt("selw", [128, E, 128], BF16)
        assert r0 <= LOOP, r0 - LOOP
        bl = at("bl", 0, [80, F + D])
        bl2 = at("bl2", 9216, [80, F + D])
        bh = at("bh", 18432, [80, F + D], BF16)
        padrow = at("padrow", 4 * KB6, [1, D])
        prow = at("prow", 138912, [MC, 3, 2 * HD])
        s0 = SMALL

        def small(name, shape, dt=F32):
            nonlocal s0
            size = 2 if dt in (BF16, F16) else 4
            t = at(name, s0, shape, dt)
            s0 += (math.prod(shape[1:]) * size + 31) // 32 * 32
            return t

        assert SMALL >= 184320 + NT * D * 4
        ident = small("ident", [128, 128])
        lnw = small("lnw", [128, E, FC])
        lnb = small("lnb", [128, E, FC])
        bsplit = small("bsplit", [128, F + D], BF16)
        projt = at("projt", s0, [128, M])
        gatew = at("gatew", s0 + 1088, [128, C, E])
        nbias = at("nbias", s0 + 1472, [TP, 4, 60])
        lnst = at("lnst", s0 + 1472, [TP, NT, 2, 6])
        lnmv = at("lnmv", s0 + 1728, [TP, NT, 2])
        lnrs = at("lnrs", s0 + 1792, [TP, 4, NT])
        sel2 = at("sel2", s0 + 2432, [128, 2])
        ones = at("ones", s0 + 2464, [128, 1])
        diag = at("diag", s0 + 2496, [TAILS, H])
        dinv = at("dinv", s0 + 2752, [TP, 5, NT])
        kmax = at("kmax", s0 + 2880, [128, 4])
        rden = at("rden", s0 + 2592, [TP, 2, 6])
        prefix = at("prefix", s0 + 2944, [TP, 128], BF16)
        onesb = at("onesb", s0 + 3200, [TP, 128], BF16)
        kmax5 = at("kmax5", s0 + 3456, [TP, 5])
        s0 += 4096
        table = small("table", [128, TW, 2], I32)
        firstrow = small("firstrow", [128, 3], I32)
        pair = at("pair", s0, [TP, 4, NT, 2], I32)
        slot = at("slot", s0 + 160, [TP, 4, NT], U32)
        tri = at("tri", s0 + 256, [128, E, E], BF16)
        s0 += 768
        btab = small("btab", [128, 3, TW + 1], I32)
        st6 = small("st6", [128, 3, 6])
        mv = small("mv", [128, 2])
        rs = small("rs", [128, 4])
        gidx = small("gidx", [128, 1], U32)
        sidx = small("sidx", [128, 2], U32)
        assert base0 + s0 <= nc.sbuf_usable_end, (base0 + s0, nc.sbuf_usable_end)

        bank = [ctx.enter_context(nc.psum_tensor(f"bank{b}", [128, 512], F32)) for b in range(8)]
        hid_ps = bank[0:3]
        tr_ps = bank[3:6]
        y_ps = bank[6:8]

        def sem(name):
            return ctx.enter_context(nc.semaphore(name))

        plan, uses, turn = {}, [0] * 8, 0

        def groups(keys, banks):
            nonlocal turn
            for key in keys:
                b = banks[turn % len(banks)]
                turn += 1
                uses[b] += 1
                plan[key] = (b, uses[b])

        R3, R8 = [5, 6, 7], list(range(8))
        T8 = [("c", c) for c in range(C)] + [("l", 0), ("l", 4)]
        groups([("pt", 0)], R3)
        groups([("xt",) + k for k in T8], R3)
        groups([("v", i, s) for s in range(2) for i in range(NT)], R3)
        groups([("k", o, s) for o in range(C) for s in range(2)], R3)
        groups([("q", o, s) for o in range(C) for s in range(2)], R3)
        groups([("h", i, s) for s in range(2) for i in range(NT)], R3)
        turn = 0
        groups([("sqk", 0), ("sqq", 0), ("deg", 0)], [0, 1, 2])
        groups([("ddk", i, h) for i in range(NT) for h in range(H)], R8)
        groups([("gnn", i, s) for i in range(NT) for s in range(2)], R8)
        for g in range(2):
            groups([("kvt", g)] + [("kv", h) for h in range(6 * g, 6 * g + 6)], R8)
        turn = 0
        R6 = [0, 1, 2, 3, 4, 5]
        groups([("ddq", 0, h) for h in range(H)], R6)
        for i in range(NT):
            groups([("q1t", i, 0), ("tail", i)], R6)
            for p in range(H // 2):
                if p + 1 < H // 2:
                    groups([("q1t", i, p + 1)], R6)
                if i + 1 < NT:
                    groups([("ddq", i + 1, 2 * r + k) for r in AHEAD[p] for k in range(2)], R6)
        for i in range(NT):
            before_o, turn = turn, 0
            groups([("o", i, 0), ("o", i, 1)], [6, 7])
            turn = before_o
        turn = 0
        groups([("at",) + k for k in T8], R8)
        turn = 0
        for i in range(NT + 2):
            if i < NT:
                groups([("pj", i, 0), ("pj", i, 1)], [0, 1, 2, 3, 4, 6, 7])
            if i == 3:
                before_gate = turn
                turn = 0
                groups([("gate", 0)], [5])
                turn = before_gate
            if i >= 2:
                groups([("x2", i - 2, 0), ("x2", i - 2, 1)], [0, 1, 2, 3, 4, 6, 7])
        turn = 0
        groups([("cnt", 0), ("pos", 0)], [6, 7])

        full = [sem(f"full{b}") for b in range(8)]
        free = [sem(f"free{b}") for b in range(8)]

        def fill(pe, key):
            b, n = plan[key]
            if n > 1:
                pe.wait_ge(free[b], n - 1)
            return bank[b]

        def filled(last, key):
            last.then_inc(full[plan[key][0]], 1)

        def read(eng, key):
            b, n = plan[key]
            eng.wait_ge(full[b], n)
            return bank[b]

        def emptied(ins, key):
            ins.then_inc(free[plan[key][0]], 1)

        def sems(names):
            return [sem(n) for n in names.split()]

        ld_x = [sem(f"ld_x{i}") for i in range(NT)]
        ld_idx, ld_bias, ld_qkv, ld_wg, ld_proj, ld_gate, ld_ln, ld_wp, ld_eb, ld_gb, ld_table = sems(
            "ld_idx ld_bias ld_qkv ld_wg ld_proj ld_gate ld_ln ld_wp ld_eb ld_gb ld_table")
        st_x1, st_xn2, st_padrow, st_pad, st_slot = sems("st_x1 st_xn2 st_padrow st_pad st_slot")
        const_ok, route_const, sel_ok, dve_own, passed = sems("const_ok route_const sel_ok dve_own passed")
        xn_ok, x_biased, edges_ok, oh_free, oh_ready, adj_full, adj_read, rounded, unpacked, pk_free, adj_ok, deg_ok = sems(
            "xn_ok x_biased edges_ok oh_free oh_ready adj_full adj_read rounded unpacked pk_free adj_ok deg_ok")
        piece_hi, piece_lo, vones_ok, sq_ok, sq_used, kmax_ok, kall_ok, kbias_ok, kexp_ok, k1_ok = sems(
            "piece_hi piece_lo vones_ok sq_ok sq_used kmax_ok kall_ok kbias_ok kexp_ok k1_ok")
        qbias_ok, q1_ok, q1t_used, bsplit_ok, bl_zero = sems("qbias_ok q1_ok q1t_used bsplit_ok bl_zero")
        x1_ok, xn2_ok, pad_ok, sc_ok, ex_ok, member_ok, slots_ok, btab_ok = sems(
            "x1_ok xn2_ok pad_ok sc_ok ex_ok member_ok slots_ok btab_ok")
        ld_w1 = [sem(f"ld_w1_{u}") for u in range(C)]
        ld_w2 = [sem(f"ld_w2_{u}") for u in range(C)]
        w1_hi, w2_hi, w1_lo, w2_lo, w1_lo_pool, w2_lo_pool, w1_used, w2_used = sems(
            "w1_hi w2_hi w1_lo w2_lo w1_lo_pool w2_lo_pool w1_used w2_used")
        gidx_ok, gathered, x_turned, xthi_ok, xtlo_ok = sems("gidx_ok gathered x_turned xthi_ok xtlo_ok")
        fc1_ok, gelu_ok, ln_own, ln_ok, h_turned, v_scaled, hthi_ok, htlo_ok = sems(
            "fc1_ok gelu_ok ln_own ln_ok h_turned v_scaled hthi_ok htlo_ok")
        fc2_ok, y_ok, sidx_ok, scattered = sems("fc2_ok y_ok sidx_ok scattered")

        def done(eng, key):
            b, n = plan[key]
            eng.wait_ge(full[b], n)

        def taken(eng, key):
            b, n = plan[key]
            eng.wait_ge(free[b], n)

        def turn_tokens(pe, name, rows, ready, per_tile):
            for kind, k in T8:
                ps = fill(pe, (name, kind, k))
                if kind == "c":
                    todo = [(k, i, i) for i in range(4)]
                else:
                    todo = [(c, 4, c - k) for c in range(k, min(C, k + 4))]
                for c, i, place in todo:
                    pe.wait_ge(ready, per_tile * (i + 1))
                    last = pe.transpose(ps[:, place * TP:(place + 1) * TP], rows[:, i, c::C], ident[0:TP, 0:TP])
                filled(last, (name, kind, k))

        def take_turned(act, name, to):
            for kind, k in T8:
                ps = read(act, (name, kind, k))
                if kind == "c":
                    ins = act.activation(to[:, k, 0:4 * TP], ps[:, 0:4 * TP], ACT.Copy)
                else:
                    n = min(C, k + 4) - k
                    ins = act.activation(to[:, k:k + n, 4 * TP:N],
                                         ps[:, 0:n * TP].rearrange("p (c t) -> p c t", t=TP), ACT.Copy)
                emptied(ins, (name, kind, k))

        def all_turned(eng, name):
            for kind, k in T8:
                taken(eng, (name, kind, k))

        def edge(plane, t):
            return ef[:, plane, bass.ds(t, 1)]

        PIECES = [("x", 0), ("v", 0)] + [("k", o) for o in range(C)] + [("q", o) for o in range(C)] + [("g", 0)]

        def piece(name, o):
            if name == "x":
                return xnt[:, :, :], xhi[:, :, :], xlo[:, :, :]
            if name == "v":
                return [w[:, :, 2 * D:3 * D].rearrange("p c (s n) -> p s c n", s=2) for w in (wqkv,)] + [
                    vhi[:, :, :, :], wqkvlo[:, :, 2 * D:3 * D].rearrange("p c (s n) -> p s c n", s=2)]
            if name == "g":
                return wg[:, :, :], wqkvlo[:, :, 2 * D:3 * D], wglo[:, :, :]
            a = (D if name == "k" else 0) + 128 * o
            slot = (o if name == "k" else C + o) % KQ
            return wqkv[:, :, a:a + 128], kqhi[:, slot, :, :], wqkvlo[:, :, a:a + 128]

        def high_piece(act, name, o=0):
            whole, hi, _ = piece(name, o)
            act.activation(hi, whole, ACT.Copy).then_inc(piece_hi, 1)

        def low_piece(pool, name, o=0):
            whole, hi, lo = piece(name, o)
            pool.wait_ge(piece_hi, PIECES.index((name, o)) + 1)
            pool.tensor_tensor(lo, whole, hi.bitcast(F32), ALU.subtract).then_inc(piece_lo, 1)

        def wait_piece(pe, name, o=0):
            pe.wait_ge(piece_lo, PIECES.index((name, o)) + 1)

        def unit(w, second, u):
            return w[:, 2 * u:2 * u + 2, :].rearrange("p c n -> p (c n)") if second else w[:, u, :]

        def split_hi(act, second, e, units):
            for u in units:
                act.wait_ge((ld_w2 if second else ld_w1)[u], 16 * e + 16)
                act.activation(unit(w2hi if second else w1hi, second, u), unit(w2raw if second else w1raw, second, u),
                               ACT.Copy).then_inc(w2_hi if second else w1_hi, 1)

        def pools(u):
            return u % ON_POOL == ON_POOL - 1

        def split_lo(eng, second, e, units):
            mine = eng.engine == mybir.EngineType.Pool
            low = (w2_lo_pool if mine else w2_lo) if second else (w1_lo_pool if mine else w1_lo)
            for u in units:
                if pools(u) == mine:
                    eng.wait_ge(w2_hi if second else w1_hi, C * e + u + 1)
                    eng.tensor_tensor(unit(w2lo if second else w1lo, second, u), unit(w2raw if second else w1raw, second, u),
                                      unit(w2hi if second else w1hi, second, u).bitcast(F32), ALU.subtract).then_inc(low, 1)

        def wait_split(pe, second, e, u):
            per_expert = len([v for v in range(C) if pools(v) == pools(u)])
            before = len([v for v in range(u) if pools(v) == pools(u)])
            if pools(u):
                pe.wait_ge(w2_lo_pool if second else w1_lo_pool, per_expert * e + before + 1)
            else:
                pe.wait_ge(w2_lo if second else w1_lo, per_expert * e + before + 1)

        def entry(eng, r, j, top):
            return eng.value_load(btab[0:1, r, bass.ds(j, 1)], min_val=0, max_val=top)

        def with_first(eng, j, do):
            with eng.If(entry(eng, LAST_OF, j, 1)):
                do(eng, False, entry(eng, EXPERT, j + 1, E - 1))

        def with_second(eng, j, do):
            with eng.If(entry(eng, NEW_BEFORE, j, 1)):
                do(eng, True, entry(eng, EXPERT, j - 1, E - 1))

        def high(*units):
            return lambda eng, second, e: split_hi(eng, second, e, units)

        def low(*units):
            return lambda eng, second, e: split_lo(eng, second, e, units)

        block = ctx.enter_context(nc.Block())

        @block.sync
        def _(sp):
            for i in range(NT):
                sp.dma_start(xs[:, i, :], x[TP * i:TP * i + TP, :]).then_inc(ld_x[i], 16)
                if i == 0:
                    sp.dma_start(src_i[:, 0, :], src.rearrange("(p k) -> p k", p=TP)).then_inc(ld_idx, 16)
                    sp.dma_start(src_i[:, 1, :], dst.rearrange("(p k) -> p k", p=TP)).then_inc(ld_idx, 16)
            sp.dma_start(bias2[:, 0, :], row(gnn_b).broadcast_to([TP, D])).then_inc(ld_bias, 16)
            sp.dma_start(bias2[:, 1, :], row(b_proj).broadcast_to([TP, D])).then_inc(ld_bias, 16)
            for m in range(3):
                rows = min(MC, M - MC * m)
                for half in range(2):
                    sp.dma_start(prow[0:rows, m, HD * half:HD * half + HD],
                                 proj_mat[MC * m:MC * m + rows, :]).then_inc(ld_proj, 16)
            sp.dma_start(wqkv[:, :, :], w_qkv.rearrange("(p c) n -> p c n", c=C)).then_inc(ld_qkv, 16)
            sp.dma_start(wg[:, :, :], gnn_w.rearrange("(p c) n -> p c n", c=C)).then_inc(ld_wg, 16)
            sp.dma_start(gatew[:, :, :], gate_w.rearrange("(p c) n -> p c n", c=C)).then_inc(ld_gate, 16)
            sp.dma_start(lnw[:, :, :], ln_w.rearrange("e (p c) -> p e c", c=FC)).then_inc(ld_ln, 16)
            sp.dma_start(lnb[:, :, :], ln_b.rearrange("e (p c) -> p e c", c=FC)).then_inc(ld_ln, 16)
            done(sp, ("gnn", NT - 1, 1))
            sp.dma_start(wp[:, :, :], w_proj.rearrange("(p c) n -> p c n", c=C)).then_inc(ld_wp, 16)
            sp.wait_ge(bl_zero, 1)
            for g in range(3):
                sp.dma_start(bl[32 * g:32 * g + E, 0:F], fc1_b).then_inc(ld_eb, 16)
                sp.dma_start(bl[32 * g:32 * g + E, F:F + D], fc2_b).then_inc(ld_eb, 16)

            fc1_units = fc1_w.rearrange("e (p c) n -> e p c n", c=C)
            fc2_units = fc2_w.rearrange("e (p c) n -> e p (c n)", c=FC)

            def load(second, e, u):
                of = fc2_units[bass.ds(e, 1), :, F * u:F * u + F] if second else fc1_units[bass.ds(e, 1), :, u, :]
                sp.dma_start(unit(w2raw if second else w1raw, second, u),
                             of.rearrange("a p n -> (a p) n")).then_inc((ld_w2 if second else ld_w1)[u], 16)

            done(sp, ("kv", H - 1))
            for u in range(C):
                load(False, 0, u)
            sp.dma_start(gateb[:, :], row(gate_b).broadcast_to([TP, E])).then_inc(ld_gb, 16)
            sp.wait_ge(pad_ok, 1)
            sp.dma_start(xn2_dram[N:N + 1, :], padrow[0:1, :]).then_inc(st_padrow, 16)
            sp.wait_ge(route_const, 2)
            sp.dma_start(table_dram.rearrange("(p w) a -> p w a", p=128), padt[:, :, :]).then_inc(st_pad, 16)
            for i in range(NT):
                sp.wait_ge(x1_ok, i + 1)
                sp.dma_start(out[TP * i:TP * i + TP, :], xs[:, i, :]).then_inc(st_x1, 16)
                sp.wait_ge(xn2_ok, i + 1)
                sp.dma_start(xn2_dram[TP * i:TP * i + TP, :], xn2[:, i, :]).then_inc(st_xn2, 16)
            done(sp, ("gate", 0))
            sp.wait_ge(st_xn2, 16 * NT)
            for u in range(C):
                load(True, 0, u)
            sp.wait_ge(st_slot, 16 * 4 * NT)
            sp.dma_start(table[:, :, :], table_dram.rearrange("(p w) a -> p w a", p=128)).then_inc(ld_table, 16)
            sp.wait_ge(btab_ok, 1)
            nb = sp.value_load(btab[0:1, LAST_OF, TW:TW + 1], min_val=NT + E - 1, max_val=BLOCKS)

            def load_first(j):
                with sp.If(entry(sp, LAST_OF, j, 1)):
                    e = entry(sp, EXPERT, j + 1, E - 1)
                    for u in range(C):
                        sp.wait_ge(w1_used, C * j + u + 1)
                        load(False, e, u)

            def load_second(j):
                with sp.If(entry(sp, NEW_BEFORE, j, 1)):
                    e = entry(sp, EXPERT, j - 1, E - 1)
                    for u in range(C):
                        sp.wait_ge(w2_used, C * j + u + 1)
                        load(True, e, u)

            with sp.Fori(1, nb) as j:
                load_second(j)
                load_first(j)
            load_second(nb)
            sp.wait_ge(st_x1, 16 * NT)

        @block.gpsimd
        def _(pool):
            pool.iota(iota_i[:, :], [[1, N]], base=0, channel_multiplier=0)
            pool.memset(ident[:, :], 0.0)
            pool.memset(onesb[:, :], 1.0)
            pool.memset(prefix[:, :], 1.0)
            pool.memset(tri[:, :, :], 1.0)
            pool.memset(ones[:, :], 1.0)
            pool.memset(sel2[:, :], 0.0)
            pool.memset(bsplit[:, :], 0.0)
            pool.memset(diag[:, :], 1.0)
            pool.memset(xnt[:, :, N:N + 1], 0.0)
            pool.memset(adj[:, :, :], 0.0).then_inc(const_ok, 1)
            pool.wait_ge(const_ok, 1)
            pool.affine_select(out=ident[:, :], in_=ident[:, :], compare_op=ALU.not_equal, fill=1.0, base=0,
                               pattern=[[-1, 128]], channel_multiplier=1)
            pool.affine_select(out=prefix[:, :], in_=prefix[:, :], compare_op=ALU.is_ge, fill=0.0, base=-1,
                               pattern=[[1, 128]], channel_multiplier=-1)
            pool.affine_select(out=tri[:, :, :], in_=tri[:, :, :], compare_op=ALU.is_ge, fill=0.0, base=-1,
                               pattern=[[1, E], [-1, E]], channel_multiplier=0)
            pool.affine_select(out=diag[:, :], in_=diag[:, :], compare_op=ALU.is_ge, fill=0.0, base=0,
                               pattern=[[-TAIL, H]], channel_multiplier=1)
            pool.memset(sel2[0:64, 0:1], 0.5).then_inc(const_ok, 1)
            pool.wait_ge(const_ok, 2)
            pool.memset(sel2[64:128, 1:2], 0.5).then_inc(const_ok, 1)
            pool.wait_ge(const_ok, 3)
            pool.affine_select(out=diag[:, :], in_=diag[:, :], compare_op=ALU.is_ge, fill=0.0, base=TAIL - 1,
                               pattern=[[TAIL, H]], channel_multiplier=-1).then_inc(const_ok, 1)
            pool.wait_ge(const_ok, 4)
            pool.wait_ge(ld_bias, 32)
            pool.wait_ge(xn_ok, NT)
            for i in range(NT):
                for b in range(2):
                    pool.tensor_tensor(xs[:, i, :], xs[:, i, :], bias2[:, b, :], ALU.add).then_inc(x_biased, 1)
                    pool.wait_ge(x_biased, 2 * i + b + 1)
            low_piece(pool, "x")
            low_piece(pool, "v")

            def add_counts(c):
                pool.wait_ge(rounded, 3 * c)
                pool.wait_ge(pk_free, 2 * c - 1)
                high_part, low_part = adj[:, :, HALF:2 * HALF], adj[:, :, 0:HALF]
                pool.tensor_tensor(high_part, high_part, pkh[:, :, :], ALU.add).then_inc(pk_free, 1)
                pool.wait_ge(unpacked, c)
                pool.tensor_tensor(low_part, low_part, pk[:, :, :], ALU.add).then_inc(pk_free, 1)

            pool.sem_inc(pk_free, 1)
            with pool.Fori(1, CHUNKS + 2) as c:
                add_counts(c)
            pool.wait_ge(pk_free, 2 * CHUNKS + 3)
            for b in range(NT):
                last = pool.tensor_tensor(adj[:, b, TP * b:TP * b + TP], adj[:, b, TP * b:TP * b + TP],
                                          ident[0:TP, 0:TP], ALU.add)
            last.then_inc(adj_ok, 1)
            for name, o in PIECES[2:]:
                low_piece(pool, name, o)
            pool.wait_ge(adj_ok, 1)
            done(pool, ("pt", 0))
            pool.memset(vext[:, :, :, HD:HD + 1], 1.0).then_inc(vones_ok, 1)
            pool.wait_ge(kmax_ok, 1)
            pool.partition_all_reduce(kmax[0:TP, 1:2], kmax[0:TP, 0:1], TP, RMAX).then_inc(kall_ok, 1)
            done(pool, ("kv", H - 1))
            pool.memset(bl[:, :], 0.0).then_inc(bl_zero, 1)
            pool.iota(biota_i[:, :], [[1, TW]], base=0, channel_multiplier=0)
            pool.memset(padrow[0:1, :], 0.0).then_inc(pad_ok, 1)
            pool.iota(padt[:, :, 0], [[0, TW]], base=N, channel_multiplier=0)
            pool.memset(padt[:, :, 1], 0)
            pool.iota(firstrow[:, :], [[128, 3]], base=0, channel_multiplier=1)
            pool.iota(pair[:, :, :, 0], [[0, 4], [TP, NT]], base=0, channel_multiplier=1).then_inc(route_const, 2)
            pool.memset(selw[:, :, :], 0.0).then_inc(sel_ok, 1)
            for g in range(3):
                pool.wait_ge(sel_ok, g + 1)
                pool.affine_select(out=selw[:, :, :], in_=selw[:, :, :], compare_op=ALU.not_equal, fill=1.0,
                                   base=-32 * g, pattern=[[-1, E], [0, 128]], channel_multiplier=1).then_inc(sel_ok, 1)
            pool.wait_ge(bsplit_ok, 1)
            split_lo(pool, False, 0, range(C))

            pool.wait_ge(st_padrow, 16)
            pool.wait_ge(st_xn2, 16 * NT)
            pool.wait_ge(st_x1, 16 * NT)
            taken(pool, ("pj", NT - 1, 1))
            pool.wait_ge(route_const, 2)
            for b in range(3):
                if b:
                    pool.wait_ge(x_turned, b)
                    pool.wait_ge(gathered, 16 * b)
                pool.indirect_dma_start(out=xg[:, :], out_offset=None, in_=xn2_dram,
                                        in_offset=bass.IndirectOffsetOnAxis(ap=firstrow[:, b:b + 1].bitcast(U32), axis=0)
                                        ).then_inc(gathered, 16)
            split_lo(pool, True, 0, range(C))
            pool.wait_ge(slots_ok, 1)
            pool.wait_ge(st_pad, 16)
            for k in range(4):
                for i in range(NT):
                    pool.indirect_dma_start(
                        out=table_dram, out_offset=bass.IndirectOffsetOnAxis(ap=slot[:, k, i:i + 1], axis=0),
                        in_=pair[:, k, i, :], in_offset=None).then_inc(st_slot, 16)
            pool.wait_ge(ld_table, 16)

            def gather(b):
                pool.tensor_copy(gidx[:, 0:1], table[:, bass.ds(b, 1), 0]).then_inc(gidx_ok, 1)
                pool.wait_ge(gidx_ok, b - 2)
                pool.sem_inc(passed, 1)
                pool.indirect_dma_start(out=xg[:, :], out_offset=None, in_=xn2_dram,
                                        in_offset=bass.IndirectOffsetOnAxis(ap=gidx[:, 0:1], axis=0)).then_inc(gathered, 16)

            def scatter(j):
                pool.tensor_copy(sidx[:, :], table[:, bass.ds(j - 1, 1), :].rearrange("p w a -> p (w a)")).then_inc(sidx_ok, 1)
                pool.wait_ge(y_ok, j + 1)
                pool.sem_inc(passed, 1)
                pool.indirect_dma_start(out=out, out_offset=bass.IndirectOffsetOnAxis(ap=sidx[:, 0:1], axis=0),
                                        in_=ysb[:, :], in_offset=None, bounds_check=N - 1, oob_is_err=False,
                                        compute_op=ALU.add).then_inc(scattered, 16)
                pool.wait_ge(scattered, 16 * j)

            pool.wait_ge(btab_ok, 1)
            nb = pool.value_load(btab[0:1, LAST_OF, TW:TW + 1], min_val=NT + E - 1, max_val=BLOCKS)
            with pool.Fori(1, nb) as j:
                with_second(pool, j, low(5))
                with_first(pool, j, low(2))
                pool.wait_ge(x_turned, j + 2)
                pool.wait_ge(gathered, 16 * j + 32)
                gather(j + 2)
                with_first(pool, j, low(5))
                with_second(pool, j + 1, low(2))
                scatter(j)
            with_second(pool, nb, low(5))
            scatter(nb)
            pool.wait_ge(gathered, 16 * nb + 32)

        @block.vector
        def _(dve):
            link = Chain(dve, dve_own)
            def norm(rows, to, p, own):
                width = rows.shape[-1]
                step = 512 if width % 512 == 0 else 384
                parts = width // step
                for n in range(parts):
                    last = dve.bn_stats(st6[0:p, n, :], rows[:, n * step:(n + 1) * step])
                own(last)
                dve.sem_inc(passed, 1)
                own(dve.bn_aggr(mv[0:p, :], st6[0:p, 0:parts, :]))
                own(dve.tensor_scalar(rs[0:p, 0:1], mv[0:p, 1:2], LN_EPS, None, ALU.add))
                rsqrt(dve, own, rs[0:p, 3:4], rs[0:p, 0:1], rs[0:p, 1:2], rs[0:p, 2:3])
                return dve.tensor_scalar(to, rows, mv[0:p, 0:1], rs[0:p, 3:4], ALU.subtract, ALU.mult)

            for i in range(NT):
                dve.wait_ge(ld_x[i], 16)
                for n in range(2):
                    last = dve.bn_stats(lnst[:, i, n, :], xs[:, i, 384 * n:384 * n + 384])
            link(last)
            dve.sem_inc(passed, 1)
            for i in range(NT):
                last = dve.bn_aggr(lnmv[:, i, :], lnst[:, i, :, :])
            link(last)
            link(dve.tensor_scalar(lnrs[:, 0, :], lnmv[:, :, 1], LN_EPS, None, ALU.add))
            rsqrt(dve, link, lnrs[:, 3, :], lnrs[:, 0, :], lnrs[:, 1, :], lnrs[:, 2, :])
            for i in range(NT):
                dve.tensor_scalar(xn[:, i, :], xs[:, i, :], lnmv[:, i, 0:1], lnrs[:, 3, i:i + 1],
                                  ALU.subtract, ALU.mult).then_inc(xn_ok, 1)
            dve.wait_ge(ld_idx, 32)
            dve.tensor_copy(ef[:, 0, :], src_i[:, 0, :])
            link(dve.tensor_copy(ef[:, 1, :], src_i[:, 1, :]))
            link(dve.tensor_scalar(ef[:, 2, :], ef[:, 1, :], float(HALF), None, ALU.is_ge))
            dve.scalar_tensor_tensor(out=ef[:, 3, :], in0=ef[:, 2, :], scalar=-float(HALF), in1=ef[:, 1, :],
                                     op0=ALU.mult, op1=ALU.add)
            link(dve.tensor_scalar(ef[:, 4, :], ef[:, 2, :], PACK - 1.0, 1.0, ALU.mult, ALU.add))
            dve.wait_ge(const_ok, 3)
            link(dve.tensor_copy(iota_n[:, :], iota_i[:, :]))

            def low_counts(c):
                dve.wait_ge(rounded, 3 * c)
                dve.scalar_tensor_tensor(out=pk[:, :, :], in0=pkh[:, :, :], scalar=-float(PACK), in1=pk[:, :, :],
                                         op0=ALU.mult, op1=ALU.add).then_inc(unpacked, 1)

            def one_hots(c, tiles, before):
                for k in range(tiles):
                    t = CHUNK * c + k
                    dve.wait_ge(oh_free, t + 1)
                    dve.tensor_scalar(ohs[:, k % RING, :], iota_n[:, :], edge(0, t), None, ALU.is_equal)
                    dve.tensor_scalar(ohd[:, k % RING, 0:HALF], iota_n[:, 0:HALF], edge(3, t), edge(4, t),
                                      ALU.is_equal, ALU.mult).then_inc(oh_ready, 1)
                    if before and k == 8:
                        low_counts(c)

            dve.wait_ge(const_ok, 3)
            one_hots(0, CHUNK, False)
            with dve.Fori(1, CHUNKS) as c:
                one_hots(c, CHUNK, True)
            one_hots(CHUNKS, LASTC, True)
            low_counts(CHUNKS + 1)

            ps = read(dve, ("deg", 0))
            emptied(dve.tensor_copy(dinv[:, 0, :], ps[0:TP, 0:NT]), ("deg", 0))
            taken(dve, ("deg", 0))
            rsqrt(dve, link, dinv[:, 3, :], dinv[:, 0, :], dinv[:, 1, :], dinv[:, 2, :])
            for s in range(2):
                for i in range(NT):
                    ps = read(dve, ("h", i, s))
                    emptied(dve.tensor_scalar(hrow[:, i, 384 * s:384 * s + 384], ps[0:TP, 0:384], dinv[:, 3, i:i + 1],
                                              None, ALU.mult), ("h", i, s))

            for n, name in ((0, "sqk"), (1, "sqq")):
                ps = read(dve, (name, 0))
                emptied(dve.tensor_copy(nbias[:, n, :], ps[0:TP, 0:60]), (name, 0))
            for i in range(NT):
                taken(dve, ("ddk", i, H - 1))
                last = dve.tensor_reduce(kmax5[:, i:i + 1], kfeat[:, i, :, :], AX.XY, ALU.max)
            link(last)
            dve.tensor_reduce(kmax[0:TP, 0:1], kmax5[:, :], AX.X, ALU.max).then_inc(kmax_ok, 1)
            dve.wait_ge(kall_ok, 1)
            taken(dve, ("sqk", 0))
            taken(dve, ("sqq", 0))
            dve.tensor_scalar(nbias[:, 2, :], nbias[:, 0, :], -1.0, kmax[0:TP, 1:2], ALU.mult, ALU.subtract).then_inc(kbias_ok, 1)

            ratio = 1.0 / math.sqrt(M)
            dve.wait_ge(x_biased, 2 * NT)
            for i in range(NT):
                for s in range(2):
                    ps = read(dve, ("gnn", i, s))
                    part = xs[:, i, 384 * s:384 * s + 384]
                    emptied(dve.scalar_tensor_tensor(out=part, in0=ps[0:TP, 0:384], scalar=dinv[:, 3, i:i + 1], in1=part,
                                                     op0=ALU.mult, op1=ALU.add), ("gnn", i, s))
                dve.wait_ge(kexp_ok, i + 1)
                main = kfeat[:, i, :, 0:MAIN]
                dve.tensor_scalar(main, main, FEAT_EPS, ratio, ALU.add, ALU.mult)
                dve.tensor_scalar(ktail[:, i, :, :], kfeat[:, i, :, MAIN:M], FEAT_EPS, ratio, ALU.add, ALU.mult).then_inc(k1_ok, 1)
            for g in range(2):
                ps = read(dve, ("kvt", g))
                dve.wait_ge(const_ok, 4)
                emptied(dve.tensor_tensor(kvt[:, 6 * g:6 * g + 6, :], ps[0:TAILS, 0:6 * (HD + 1)].rearrange("p (h d) -> p h d", h=6),
                                          diag[:, 6 * g:6 * g + 6].unsqueeze(2).broadcast_to([TAILS, 6, HD + 1]), ALU.mult),
                        ("kvt", g))
                for h in range(6 * g, 6 * g + 6):
                    ps = read(dve, ("kv", h))
                    emptied(dve.tensor_copy(kv[:, h, :, :], ps[:, 0:2 * (HD + 1)].rearrange("p (m d) -> p m d", m=2)), ("kv", h))

            def q_bias(i, p):
                n = H * i + 2 * p
                for h in (2 * p, 2 * p + 1):
                    ps = read(dve, ("ddq", i, h))
                    last = dve.tensor_reduce(nbias[:, 3, H * i + h:H * i + h + 1], ps[0:TP, 0:M], AX.X, ALU.max, negate=True)
                link(last)
                dve.tensor_tensor(nbias[:, 3, n:n + 2], nbias[:, 3, n:n + 2], nbias[:, 1, n:n + 2],
                                  ALU.subtract).then_inc(qbias_ok, 1)

            def q_features(i):
                for h in range(H):
                    taken(dve, ("ddq", i, h))
                main = q1[i % 2][:, :, 0:MAIN]
                dve.tensor_scalar(main, main, FEAT_EPS, ratio, ALU.add, ALU.mult)
                dve.tensor_scalar(q1tail[:, i % 2, :, :], q1[i % 2][:, :, MAIN:M], FEAT_EPS, ratio,
                                  ALU.add, ALU.mult).then_inc(q1_ok, 1)

            for p in range(H // 2):
                q_bias(0, p)
            q_features(0)
            for i in range(NT):
                for p in range(H // 2):
                    for r in AHEAD[p] if i + 1 < NT else ():
                        q_bias(i + 1, r)
                    if p == 4 and i + 1 < NT:
                        q_features(i + 1)
                    if p % 3 == 2:
                        g = p // 3
                        ps = read(dve, ("o", i, g))
                        sums = ps[0:TP, 0:6 * (HD + 1)].rearrange("p (h d) -> p h d", h=6)
                        link(dve.reciprocal(rden[:, g, :], sums[:, :, HD]))
                        emptied(dve.tensor_tensor(
                            ao[:, i, 384 * g:384 * g + 384].rearrange("p (h d) -> p h d", h=6), sums[:, :, 0:HD],
                            rden[:, g, :].unsqueeze(2).broadcast_to([TP, 6, HD]), ALU.mult), ("o", i, g))

            dve.wait_ge(ld_eb, 96)
            link(dve.tensor_copy(bh[:, :], bl[:, :]))
            link(dve.tensor_tensor(bl2[:, :], bl[:, :], bh[:, :], ALU.subtract))
            dve.tensor_copy(bsplit[0:E, :], bl[0:E, :])
            dve.tensor_copy(bsplit[32:32 + E, :], bl2[32:32 + E, :])
            link(dve.tensor_copy(bh[64:64 + E, :], bl2[64:64 + E, :]))
            link(dve.tensor_tensor(bl[64:64 + E, :], bl2[64:64 + E, :], bh[64:64 + E, :], ALU.subtract))
            dve.tensor_copy(bsplit[64:64 + E, :], bl[64:64 + E, :]).then_inc(bsplit_ok, 1)
            split_lo(dve, False, 0, range(C))

            for i in range(NT):
                for s in range(2):
                    ps = read(dve, ("pj", i, s))
                    part = xs[:, i, 384 * s:384 * s + 384]
                    last = dve.tensor_tensor(part, ps[0:TP, 0:384], part, ALU.add)
                    emptied(last, ("pj", i, s))
                taken(dve, ("pj", i, 1))
                dve.sem_inc(x1_ok, 1)
                norm(xs[:, i, :], xn2[:, i, :], TP, link).then_inc(xn2_ok, 1)

            def x_low(b):
                dve.wait_ge(xthi_ok, b + 1)
                dve.tensor_tensor(xtlo[:, 0:4, :].rearrange("p c t -> p (c t)"), tr_ps[0][:, :],
                                  xthi[:, 0:4, :].rearrange("p c t -> p (c t)").bitcast(F32), ALU.subtract)
                dve.tensor_tensor(xtlo[:, 4:6, :].rearrange("p c t -> p (c t)"), tr_ps[1][:, 0:256],
                                  xthi[:, 4:6, :].rearrange("p c t -> p (c t)").bitcast(F32), ALU.subtract).then_inc(xtlo_ok, 1)

            STEPS = 12

            def hidden_scale(j, e):
                dve.wait_ge(h_turned, j)
                for c in range(FC):
                    last = dve.tensor_scalar(hid[:, 128 * c:128 * c + 128], tr_ps[c // 4][:, 128 * (c % 4):128 * (c % 4) + 128],
                                             lnw[:, bass.ds(e, 1), c], lnb[:, bass.ds(e, 1), c], ALU.mult, ALU.add)
                last.then_inc(v_scaled, 1)

            def hidden_low(j):
                dve.wait_ge(hthi_ok, j)
                dve.tensor_tensor(htlo[:, :, :].rearrange("p c t -> p (c t)"), hid[:, :],
                                  hthi[:, :, :].rearrange("p c t -> p (c t)").bitcast(F32), ALU.subtract).then_inc(htlo_ok, 1)

            def normalise(j):
                dve.wait_ge(gelu_ok, 3 * j + 3)
                norm(hid[:, :], hid[:, :], 128, Chain(dve, ln_own, STEPS * j)).then_inc(ln_ok, 1)

            ps = read(dve, ("gate", 0))
            dve.wait_ge(ld_gb, 16)
            link(dve.tensor_tensor(sc[:, :, :], ps[0:TP, 0:NT * E].rearrange("p (i e) -> p i e", e=E),
                                   gateb[:, :].unsqueeze(1).broadcast_to([TP, NT, E]), ALU.add))
            dve.sem_inc(free[plan[("gate", 0)][0]], 1)
            link(dve.memset(sc[:, :, 0:1], NEG))
            link(dve.tensor_reduce(mx[:, :], sc[:, :, :], AX.X, ALU.max))
            dve.tensor_tensor(sc[:, :, :], sc[:, :, :], mx[:, :].unsqueeze(2).broadcast_to([TP, NT, E]),
                              ALU.subtract).then_inc(sc_ok, 1)
            dve.wait_ge(ex_ok, 1)
            link(dve.tensor_reduce(mx[:, :], sc[:, :, :], AX.X, ALU.add))
            link(dve.reciprocal(mx[:, :], mx[:, :]))
            link(dve.tensor_tensor(pr[:, :, :], sc[:, :, :], mx[:, :].unsqueeze(2).broadcast_to([TP, NT, E]), ALU.mult))
            x_low(0)
            mine = pr[:, :, :].unsqueeze(3).broadcast_to([TP, NT, E, E])
            other = pr[:, :, :].unsqueeze(2).broadcast_to([TP, NT, E, E])
            before = tri[0:TP, :, :].unsqueeze(1).broadcast_to([TP, NT, E, E])
            dve.tensor_tensor(cmp1[:, :, :, :], other, mine, ALU.is_gt)
            link(dve.tensor_tensor(cmp2[:, :, :, :], other, mine, ALU.is_equal))
            link(dve.tensor_tensor(cmp2[:, :, :, :], cmp2[:, :, :, :], before, ALU.mult))
            link(dve.tensor_tensor(cmp1[:, :, :, :], cmp1[:, :, :, :], cmp2[:, :, :, :], ALU.add))
            link(dve.tensor_reduce(rank[:, :, :], cmp1[:, :, :, :], AX.X, ALU.add))
            link(dve.tensor_scalar(member[:, :, :], rank[:, :, :], float(TOPK), None, ALU.is_lt))
            link(dve.tensor_tensor(comb[:, :, :], member[:, :, :], pr[:, :, :], ALU.mult))
            link(dve.tensor_scalar(comb[:, :, 0:1], comb[:, :, 0:1], 1.0, None, ALU.add))
            dve.memset(member[:, :, 0:1], 1.0).then_inc(member_ok, 1)
            ps = read(dve, ("cnt", 0))
            link(dve.tensor_scalar(nblk[:, :], ps[:, 0:E], 1.0 / SLOTS, (SLOTS - 1.0) / SLOTS - 0.5 + 0.5 / SLOTS,
                                   ALU.mult, ALU.add))
            dve.sem_inc(free[plan[("cnt", 0)][0]], 1)
            link(dve.tensor_scalar(nblk[:, :], nblk[:, :], ROUND, ROUND, ALU.add, ALU.subtract))
            link(dve.tensor_scalar(nblk[:, :], nblk[:, :], 1.0, None, ALU.max))
            link(dve.tensor_tensor(btmp[:, :, :], tri[:, :, :], nblk[:, :].unsqueeze(1).broadcast_to([128, E, E]), ALU.mult))
            link(dve.tensor_reduce(base[:, :], btmp[:, :, :], AX.X, ALU.add))
            ps = read(dve, ("pos", 0))
            link(dve.tensor_copy(pos[:, :, :], ps[0:TP, 0:NT * E].rearrange("p (i e) -> p i e", e=E)))
            dve.sem_inc(free[plan[("pos", 0)][0]], 1)
            link(dve.tensor_scalar(quo[:, :, :], pos[:, :, :], 1.0 / SLOTS, -0.5 + 0.5 / SLOTS, ALU.mult, ALU.add))
            link(dve.tensor_scalar(quo[:, :, :], quo[:, :, :], ROUND, ROUND, ALU.add, ALU.subtract))
            link(dve.tensor_scalar(quo[:, :, :], quo[:, :, :], 1.0 - SLOTS * TW, None, ALU.mult))
            link(dve.scalar_tensor_tensor(out=pos[:, :, :], in0=pos[:, :, :], scalar=float(TW), in1=quo[:, :, :],
                                          op0=ALU.mult, op1=ALU.add))
            link(dve.tensor_tensor(pos[:, :, :], pos[:, :, :], base[0:TP, :].unsqueeze(1).broadcast_to([TP, NT, E]), ALU.add))
            dve.wait_ge(route_const, 2)
            wcol = pair[:, :, :, 1].bitcast(F32)
            for k in range(TOPK):
                dve.scalar_tensor_tensor(out=pick[:, 0, :, :], in0=rank[:, :, :], scalar=float(k), in1=pos[:, :, :],
                                         op0=ALU.is_equal, op1=ALU.mult)
                link(dve.scalar_tensor_tensor(out=pick[:, 1, :, :], in0=rank[:, :, :], scalar=float(k), in1=comb[:, :, :],
                                              op0=ALU.is_equal, op1=ALU.mult))
                dve.tensor_reduce(slotf[:, k, :], pick[:, 0, :, :], AX.X, ALU.add)
                link(dve.tensor_reduce(wcol[:, k, :], pick[:, 1, :, :], AX.X, ALU.add))
            dve.tensor_copy(wcol[:, TOPK, :], comb[:, :, 0])
            link(dve.tensor_copy(slotf[:, TOPK, :], pos[:, :, 0]))
            dve.tensor_copy(slot[:, :, :], slotf[:, :, :]).then_inc(slots_ok, 1)
            link(dve.tensor_copy(biota[:, :], biota_i[:, :]))
            link(dve.tensor_tensor(bcmp[:, :, :], base[:, :].unsqueeze(1).broadcast_to([128, TW, E]),
                                   biota[:, :].unsqueeze(2).broadcast_to([128, TW, E]), ALU.is_le))
            link(dve.tensor_reduce(bsum[:, :], bcmp[:, :, :], AX.X, ALU.add))
            dve.tensor_scalar(btab[:, EXPERT, 0:TW], bsum[:, :], -1.0, None, ALU.add)
            dve.tensor_tensor(btab[:, LAST_OF, 0:TW - 1], bsum[:, 1:TW], bsum[:, 0:TW - 1], ALU.subtract)
            dve.memset(btab[:, NEW_BEFORE, 0:2], 0)
            dve.tensor_tensor(btab[:, NEW_BEFORE, 2:TW], bsum[:, 1:TW - 1], bsum[:, 0:TW - 2], ALU.subtract)
            dve.tensor_tensor(btab[:, LAST_OF, TW:TW + 1], base[:, E - 1:E], nblk[:, E - 1:E], ALU.add).then_inc(btab_ok, 1)
            normalise(0)
            x_low(1)

            split_lo(dve, True, 0, range(C))
            dve.wait_ge(ld_ln, 32)
            dve.wait_ge(btab_ok, 1)
            nb = dve.value_load(btab[0:1, LAST_OF, TW:TW + 1], min_val=NT + E - 1, max_val=BLOCKS)
            with dve.Fori(1, nb) as j:
                hidden_scale(j, entry(dve, EXPERT, j - 1, E - 1))
                with_second(dve, j, low(4))
                hidden_low(j)
                with_first(dve, j, low(0, 1, 3))
                normalise(j)
                x_low(j + 1)
                with_first(dve, j, low(4))
                with_second(dve, j + 1, low(0, 1, 3))
            hidden_scale(nb, E - 1)
            with_second(dve, nb, low(4))
            hidden_low(nb)

        @block.scalar
        def _(act):
            ps = read(act, ("pt", 0))
            emptied(act.activation(projt[:, :], ps[:, 0:M], ACT.Copy), ("pt", 0))
            take_turned(act, "xt", xnt)
            all_turned(act, "xt")
            act.wait_ge(const_ok, 1)
            high_piece(act, "x")
            act.wait_ge(ld_qkv, 16)
            high_piece(act, "v")

            def counts(c):
                act.wait_ge(adj_full, c + 1)
                act.wait_ge(pk_free, 2 * c + 1)
                for b in range(NT):
                    act.activation(pk[:, b, :], bank[b][0:TP, 0:HALF], ACT.Copy).then_inc(adj_read, 1)
                act.wait_ge(adj_read, NT * c + 2 * NT)
                act.activation(pkh[:, :, :], pk[:, :, :], ACT.Copy, scale=1.0 / PACK, bias=-0.4375).then_inc(rounded, 1)
                act.wait_ge(rounded, 3 * c + 1)
                act.activation(pkh[:, :, :], pkh[:, :, :], ACT.Copy, bias=ROUND).then_inc(rounded, 1)
                act.wait_ge(rounded, 3 * c + 2)
                act.activation(pkh[:, :, :], pkh[:, :, :], ACT.Copy, bias=-ROUND).then_inc(rounded, 1)

            counts(0)
            with act.Fori(1, CHUNKS) as c:
                counts(c)
            counts(CHUNKS)
            act.wait_ge(x_biased, 2 * NT)

            def take_v(s):
                for i in range(NT):
                    ps = read(act, ("v", i, s))
                    emptied(act.activation(vext[:, i, 6 * s:6 * s + 6, 0:HD],
                                           ps[0:TP, 0:384].rearrange("p (h d) -> p h d", d=HD), ACT.Copy), ("v", i, s))

            take_v(0)
            for o in range(3):
                high_piece(act, "k", o)
            take_v(1)
            for o in range(3, KQ):
                high_piece(act, "k", o)
            squares = [(n, name, of, o) for n, (name, of) in enumerate((("k", kt), ("q", qt))) for o in range(C)]

            def square(g):
                n, name, of, o = squares[g]
                taken(act, (name, o, 1))
                taken(act, (name, o, 0))
                if g >= 2:
                    act.wait_ge(sq_used, g - 1)
                act.activation(sq[:, g % 2, :], of[:, o, :], ACT.Square).then_inc(sq_ok, 1)

            act.wait_ge(adj_ok, 1)
            for name, to in (("k", kt), ("q", qt)):
                for o in range(C):
                    for s, (a, b) in enumerate(TSPLIT):
                        ps = read(act, (name, o, s))
                        emptied(act.activation(to[:, o, a:b], ps[:, 0:b - a], ACT.Copy, scale=HD ** -0.25), (name, o, s))
                    n = 2 + KQ + o + (C if name == "q" else 0)
                    if n < len(PIECES) and PIECES[n][0] != "g":
                        high_piece(act, *PIECES[n])
                    elif n == len(PIECES) - 1:
                        act.wait_ge(ld_wg, 16)
                        high_piece(act, "g")
                    if name == "q":
                        square(o)
            for g in range(C, 2 * C):
                square(g)
            for i in range(NT):
                for h in range(H):
                    ps = read(act, ("ddk", i, h))
                    emptied(act.activation(kfeat[:, i, h, :], ps[0:TP, 0:M], ACT.Copy), ("ddk", i, h))
            act.wait_ge(kbias_ok, 1)
            for i in range(NT):
                for h in range(H):
                    n = H * i + h
                    last = act.activation(kfeat[:, i, h, :], kfeat[:, i, h, :], ACT.Exp, bias=nbias[:, 2, n:n + 1])
                last.then_inc(kexp_ok, 1)

            def q_exp(i, p):
                for h in (2 * p, 2 * p + 1):
                    n = H * i + h
                    ps = read(act, ("ddq", i, h))
                    act.wait_ge(qbias_ok, H // 2 * i + p + 1)
                    emptied(act.activation(q1[i % 2][:, h, :], ps[0:TP, 0:M], ACT.Exp, bias=nbias[:, 3, n:n + 1]), ("ddq", i, h))

            def take_pair(i, p):
                ps = read(act, ("q1t", i, p))
                n = H // 2 * i + p
                if n >= 2:
                    act.wait_ge(q1t_used, n - 1)
                emptied(act.activation(q1t[:, n % 2, :, :], ps[:, 0:4 * TP].rearrange("p (m t) -> p m t", m=4), ACT.Copy),
                        ("q1t", i, p))

            def take_tail(i):
                ps = read(act, ("tail", i))
                if i >= 2:
                    done(act, ("o", i - 2, 1))
                emptied(act.activation(q1tt[:, i % 2, :], ps[0:TAILS, 0:TP], ACT.Copy), ("tail", i))

            for p in range(H // 2):
                q_exp(0, p)
            done(act, ("kv", H - 1))
            for i in range(NT):
                take_pair(i, 0)
                take_tail(i)
                if i >= 1:
                    done(act, ("tail", i - 1))
                    for p in range(H // 2):
                        done(act, ("q1t", i - 1, p))
                for p in range(H // 2):
                    if p + 1 < H // 2:
                        take_pair(i, p + 1)
                    for r in AHEAD[p] if i + 1 < NT else ():
                        q_exp(i + 1, r)
            take_turned(act, "at", aot)
            act.wait_ge(bsplit_ok, 1)
            act.wait_ge(st_padrow, 16)
            split_hi(act, False, 0, range(C))
            for i in range(NT):
                for s, n in ((0, 4), (1, 2)):
                    ps = read(act, ("x2", i, s))
                    emptied(act.activation(xn2t[:, 4 * s:4 * s + n, TP * i:TP * i + TP],
                                           ps[:, 0:n * TP].rearrange("p (c t) -> p c t", t=TP), ACT.Copy), ("x2", i, s))
            act.wait_ge(sc_ok, 1)
            act.activation(sc[:, :, :], sc[:, :, :], ACT.Exp).then_inc(ex_ok, 1)

            def hidden_high(j):
                act.wait_ge(v_scaled, j)
                act.activation(hthi[:, :, :].rearrange("p c t -> p (c t)"), hid[:, :], ACT.Copy).then_inc(hthi_ok, 1)

            def gelu(j):
                for n in range(3):
                    act.wait_ge(fc1_ok, 3 * j + n + 1)
                    act.activation(hid[:, 512 * n:512 * n + 512], hid_ps[n][:, :], ACT.Gelu).then_inc(gelu_ok, 1)

            def x_high(b):
                act.wait_ge(x_turned, b + 1)
                act.activation(xthi[:, 0:4, :].rearrange("p c t -> p (c t)"), tr_ps[0][:, :], ACT.Copy)
                act.activation(xthi[:, 4:6, :].rearrange("p c t -> p (c t)"), tr_ps[1][:, 0:256], ACT.Copy).then_inc(xthi_ok, 1)

            def weigh(j):
                act.wait_ge(fc2_ok, j)
                act.wait_ge(sidx_ok, j)
                act.activation(ysb[:, 0:384], y_ps[0][:, 0:384], ACT.Copy, scale=sidx[:, 1:2].bitcast(F32))
                act.activation(ysb[:, 384:768], y_ps[1][:, 0:384], ACT.Copy, scale=sidx[:, 1:2].bitcast(F32)).then_inc(y_ok, 1)

            act.sem_inc(y_ok, 1)
            x_high(0)
            split_hi(act, True, 0, range(C))
            gelu(0)
            x_high(1)
            act.wait_ge(btab_ok, 1)
            nb = act.value_load(btab[0:1, LAST_OF, TW:TW + 1], min_val=NT + E - 1, max_val=BLOCKS)

            with act.Fori(1, nb) as j:
                with_second(act, j, high(4))
                hidden_high(j)
                with_second(act, j, high(5))
                with_first(act, j, high(0, 1, 2, 3))
                act.wait_ge(htlo_ok, j)
                gelu(j)
                x_high(j + 1)
                with_first(act, j, high(4, 5))
                with_second(act, j + 1, high(0, 1, 2, 3))
                weigh(j)
            with_second(act, nb, high(4))
            hidden_high(nb)
            with_second(act, nb, high(5))
            weigh(nb)

        @block.tensor
        def _(pe):
            pe.wait_ge(const_ok, 3)
            pe.wait_ge(ld_proj, 96)
            ps = fill(pe, ("pt", 0))
            for m in range(3):
                rows = min(MC, M - MC * m)
                last = pe.transpose(ps[:, MC * m:MC * m + rows], prow[0:rows, m, :], ident[0:rows, 0:rows])
            filled(last, ("pt", 0))
            turn_tokens(pe, "xt", xn, xn_ok, 1)

            pe.sem_inc(oh_free, RING)
            pe.sem_inc(adj_read, NT)

            def count(c, tiles):
                for k in range(tiles):
                    pe.wait_ge(oh_ready, CHUNK * c + k + 1)
                    for b in range(NT):
                        if k == 0:
                            pe.wait_ge(adj_read, NT * c + b + 1)
                        last = pe.matmul(bank[b][0:TP, 0:HALF], ohs[:, k % RING, TP * b:TP * b + TP],
                                         ohd[:, k % RING, 0:HALF], start=k == 0, stop=k == tiles - 1)
                    if k == tiles - 1:
                        last.then_inc(adj_full, 1)
                        pe.wait_ge(adj_full, c + 1)
                        pe.sem_inc(oh_free, 1)
                    else:
                        last.then_inc(oh_free, 1)

            count(0, CHUNK)
            with pe.Fori(1, CHUNKS) as c:
                count(c, CHUNK)
            count(CHUNKS, LASTC)

            pe.wait_ge(ld_qkv, 16)
            all_turned(pe, "xt")

            def half_squares(g):
                name, o = ("sqk", "sqq")[g // C], g % C
                ps = fill(pe, (name, 0)) if o == 0 else bank[plan[(name, 0)][0]]
                pe.wait_ge(sq_ok, g + 1)
                for i in range(NT):
                    last = pe.matmul(ps[0:TP, H * i + 2 * o:H * i + 2 * o + 2], sq[:, g % 2, TP * i:TP * i + TP],
                                     sel2[:, :], start=True, stop=True)
                if o == C - 1:
                    filled(last, (name, 0))
                    done(pe, (name, 0))
                    pe.sem_inc(sq_used, 1)
                else:
                    last.then_inc(sq_used, 1)

            def rows_times(name, first, whi, wlo, also=lambda t: None):
                wait_piece(pe, first)
                for s in range(2):
                    for i in range(NT):
                        ps = fill(pe, (name, i, s))
                        t = slice(TP * i, TP * i + TP)
                        for c in range(C):
                            for k, (a, w) in enumerate(((xhi, whi), (xhi, wlo), (xlo, whi))):
                                last = pe.matmul(ps[0:TP, 0:384], a[:, c, t], w(c, s), start=c == 0 and k == 0,
                                                 stop=c == C - 1 and k == 2)
                        filled(last, (name, i, s))
                        also(NT * s + i)

            rows_times("v", "v", lambda c, s: vhi[:, s, c, :], lambda c, s: wqkvlo[:, c, 2 * D + 384 * s:2 * D + 384 * s + 384])
            for name, first in (("k", D), ("q", 0)):
                for o in range(C):
                    wait_piece(pe, name, o)
                    _, whi, wlo = piece(name, o)
                    for s, (a, b) in enumerate(TSPLIT):
                        ps = fill(pe, (name, o, s))
                        for c in range(C):
                            for k, (w, xt_) in enumerate(((whi, xhi), (wlo, xhi), (whi, xlo))):
                                last = pe.matmul(ps[:, 0:b - a + b % 2], w[:, c, :], xt_[:, c, a:b + b % 2],
                                                 start=c == 0 and k == 0, stop=c == C - 1 and k == 2)
                        filled(last, (name, o, s))
                    if name == "q":
                        pe.wait_ge(adj_ok, 1)
                        if o:
                            half_squares(o - 1)
                        if o < NT:
                            ps = fill(pe, ("deg", 0)) if o == 0 else bank[plan[("deg", 0)][0]]
                            for b in range(NT):
                                last = pe.matmul(ps[0:TP, o:o + 1], adj[:, b, TP * o:TP * o + TP], ones[0:TP, :],
                                                 start=b == 0, stop=b == NT - 1)
                            if o == NT - 1:
                                filled(last, ("deg", 0))

            rows_times("h", "g", lambda c, s: wqkvlo[:, c, 2 * D + 384 * s:2 * D + 384 * s + 384],
                       lambda c, s: wglo[:, c, 384 * s:384 * s + 384], lambda t: half_squares(C - 1 + t) if t <= C else None)

            def project(name, of, i, h):
                ps = fill(pe, (name, i, h))
                r = HD * (h % 2)
                filled(pe.matmul(ps[0:TP, 0:M], of[r:r + HD, h // 2, TP * i:TP * i + TP], projt[r:r + HD, :],
                                 start=True, stop=True), (name, i, h))

            taken(pe, ("pt", 0))
            for i in range(NT):
                for h in range(H):
                    project("ddk", kt, i, h)
            taken(pe, ("h", NT - 1, 0))
            taken(pe, ("h", NT - 1, 1))
            for i in range(NT):
                for s in range(2):
                    ps = fill(pe, ("gnn", i, s))
                    for b in range(NT):
                        last = pe.matmul(ps[0:TP, 0:384], adj[:, b, TP * i:TP * i + TP], hrow[:, b, 384 * s:384 * s + 384],
                                         start=b == 0, stop=b == NT - 1)
                    filled(last, ("gnn", i, s))
            pe.wait_ge(k1_ok, NT)
            pe.wait_ge(vones_ok, 1)
            for s in range(2):
                taken(pe, ("v", NT - 1, s))
            for g in range(2):
                ps = fill(pe, ("kvt", g))
                for i in range(NT):
                    last = pe.matmul(ps[0:TAILS, 0:6 * (HD + 1)], ktail[:, i, :, :].rearrange("p h m -> p (h m)"), vext[:, i, 6 * g:6 * g + 6, :],
                                     start=i == 0, stop=i == NT - 1)
                filled(last, ("kvt", g))
                for h in range(6 * g, 6 * g + 6):
                    ps = fill(pe, ("kv", h))
                    for m in range(2):
                        for i in range(NT):
                            last = pe.matmul(ps[:, (HD + 1) * m:(HD + 1) * (m + 1)], kfeat[:, i, h, 128 * m:128 * m + 128],
                                             vext[:, i, h, :], start=i == 0, stop=i == NT - 1)
                    filled(last, ("kv", h))

            def turn_pair(i, p):
                ps = fill(pe, ("q1t", i, p))
                for k in range(4):
                    last = pe.transpose(ps[:, TP * k:TP * k + TP], q1[i % 2][:, 2 * p + k // 2, 128 * (k % 2):128 * (k % 2) + 128],
                                        ident[0:TP, 0:TP])
                filled(last, ("q1t", i, p))

            def attend(i, p):
                g = p // 3
                if p % 3 == 0:
                    ps = fill(pe, ("o", i, g))
                    taken(pe, ("tail", i))
                    pe.matmul(ps[0:TP, 0:6 * (HD + 1)], q1tt[:, i % 2, :], kvt[:, 6 * g:6 * g + 6, :], start=True, stop=False)
                ps = bank[plan[("o", i, g)][0]]
                taken(pe, ("q1t", i, p))
                for k in range(4):
                    h = 2 * p + k // 2
                    a = (HD + 1) * (h % 6)
                    last = pe.matmul(ps[0:TP, a:a + HD + 1], q1t[:, (H // 2 * i + p) % 2, k, :], kv[:, h, k % 2, :],
                                     start=False, stop=p % 3 == 2 and k == 3)
                if p % 3 == 2:
                    filled(last, ("o", i, g))
                    done(pe, ("o", i, g))
                    pe.sem_inc(q1t_used, 1)
                else:
                    last.then_inc(q1t_used, 1)

            for h in range(H):
                project("ddq", qt, 0, h)
            for g in range(2):
                taken(pe, ("kvt", g))
            for h in range(H):
                taken(pe, ("kv", h))
            for i in range(NT):
                pe.wait_ge(q1_ok, i + 1)
                turn_pair(i, 0)
                ps = fill(pe, ("tail", i))
                filled(pe.transpose(ps[0:TAILS, 0:TP], q1tail[:, i % 2, :, :].rearrange("p h m -> p (h m)"), ident[0:TP, 0:TP]), ("tail", i))
                for p in range(H // 2):
                    if p + 1 < H // 2:
                        turn_pair(i, p + 1)
                    for r in AHEAD[p] if i + 1 < NT else ():
                        project("ddq", qt, i + 1, 2 * r)
                        project("ddq", qt, i + 1, 2 * r + 1)
                    attend(i, p)

            for i in range(NT):
                for g in range(2):
                    taken(pe, ("o", i, g))
            pe.wait_ge(const_ok, 3)
            turn_tokens(pe, "at", ao, const_ok, 0)
            all_turned(pe, "at")
            pe.wait_ge(ld_wp, 16)
            pe.wait_ge(ld_gate, 16)

            def project_out(i):
                for s in range(2):
                    ps = fill(pe, ("pj", i, s))
                    for c in range(C):
                        last = pe.matmul(ps[0:TP, 0:384], aot[:, c, TP * i:TP * i + TP], wp[:, c, 384 * s:384 * s + 384],
                                         start=c == 0, stop=c == C - 1)
                    filled(last, ("pj", i, s))

            def turn_xn2(i):
                for s, n in ((0, 4), (1, 2)):
                    ps = fill(pe, ("x2", i, s))
                    pe.wait_ge(xn2_ok, i + 1)
                    for c in range(n):
                        last = pe.transpose(ps[:, c * TP:c * TP + TP], xn2[:, i, 4 * s + c::C], ident[0:TP, 0:TP])
                    filled(last, ("x2", i, s))

            def gate(i):
                ps = fill(pe, ("gate", 0)) if i == 0 else bank[plan[("gate", 0)][0]]
                for s in range(2):
                    taken(pe, ("x2", i, s))
                for c in range(C):
                    last = pe.matmul(ps[0:TP, E * i:E * i + E], xn2t[:, c, TP * i:TP * i + TP], gatew[:, c, :],
                                     start=c == 0, stop=c == C - 1)
                if i == NT - 1:
                    filled(last, ("gate", 0))

            for i in range(NT + 2):
                if i < NT:
                    project_out(i)
                if i >= 3:
                    gate(i - 3)
                if i >= 2:
                    turn_xn2(i - 2)
            gate(NT - 1)

            def turn_x(b):
                pe.wait_ge(gathered, 16 * b + 16)
                for c in range(C):
                    last = pe.transpose(tr_ps[c // 4][:, 128 * (c % 4):128 * (c % 4) + 128], xg[:, c::C], ident[:, :])
                last.then_inc(x_turned, 1)

            def turn_h(j):
                pe.wait_ge(ln_ok, j)
                for c in range(FC):
                    last = pe.transpose(tr_ps[c // 4][:, 128 * (c % 4):128 * (c % 4) + 128], hid[:, c::FC], ident[:, :])
                last.then_inc(h_turned, 1)

            def bias(ps, e, a, b):
                return pe.matmul(ps, selw[:, bass.ds(e, 1), :].rearrange("p a t -> p (a t)"), bsplit[:, a:b],
                                 start=False, stop=True)

            def fc1(j, e, halfway=lambda: None):
                pe.wait_ge(xtlo_ok, j + 1)
                for c in range(C):
                    if c == C // 2:
                        halfway()
                    wait_split(pe, False, e, c)
                    for k, (a, w) in enumerate(((xthi, w1hi), (xthi, w1lo), (xtlo, w1hi))):
                        for n in range(3):
                            last = pe.matmul(hid_ps[n][:, :], a[:, c, :], w[:, c, 512 * n:512 * n + 512],
                                             start=c == 0 and k == 0, stop=False)
                    last.then_inc(w1_used, 1)
                for n in range(3):
                    bias(hid_ps[n][:, :], e, 512 * n, 512 * n + 512).then_inc(fc1_ok, 1)

            def fc2(j, e):
                pe.wait_ge(htlo_ok, j)
                for c in range(FC):
                    if c % 2 == 0:
                        wait_split(pe, True, e, c // 2)
                    for k, (a, w) in enumerate(((hthi, w2hi), (hthi, w2lo), (htlo, w2hi))):
                        for s in range(2):
                            last = pe.matmul(y_ps[s][:, 0:384], a[:, c, :], w[:, c, 384 * s:384 * s + 384],
                                             start=c == 0 and k == 0, stop=False)
                    if c % 2:
                        last.then_inc(w2_used, 1)
                bias(y_ps[0][:, 0:384], e, F, F + 384)
                bias(y_ps[1][:, 0:384], e, F + 384, F + D).then_inc(fc2_ok, 1)

            pe.sem_inc(w2_used, 2 * C)

            def places():
                pe.wait_ge(member_ok, 1)
                ps = fill(pe, ("cnt", 0))
                for i in range(NT):
                    last = pe.matmul(ps[:, 0:E], onesb[:, :], member[:, i, :], start=i == 0, stop=i == NT - 1)
                filled(last, ("cnt", 0))
                ps = fill(pe, ("pos", 0))
                for i in range(NT):
                    for b in range(i + 1):
                        last = pe.matmul(ps[0:TP, E * i:E * i + E], (prefix if b == i else onesb)[:, 0:TP], member[:, b, :],
                                         start=b == 0, stop=b == i)
                filled(last, ("pos", 0))

            for b in range(8):
                pe.wait_ge(free[b], uses[b] - (b == plan[("cnt", 0)][0]) - (b == plan[("pos", 0)][0]))
            turn_x(0)
            pe.wait_ge(sel_ok, 4)
            fc1(0, 0, places)
            turn_x(1)
            taken(pe, ("cnt", 0))
            taken(pe, ("pos", 0))
            pe.wait_ge(btab_ok, 1)
            nb = pe.value_load(btab[0:1, LAST_OF, TW:TW + 1], min_val=NT + E - 1, max_val=BLOCKS)
            with pe.Fori(1, nb) as j:
                e_before = entry(pe, EXPERT, j - 1, E - 1)
                e = entry(pe, EXPERT, j, E - 1)
                pe.wait_ge(xtlo_ok, j + 1)
                turn_h(j)
                fc1(j, e)
                pe.wait_ge(v_scaled, j)
                turn_x(j + 1)
                pe.wait_ge(y_ok, j)
                fc2(j, e_before)
            pe.wait_ge(xtlo_ok, nb + 1)
            turn_h(nb)
            pe.wait_ge(y_ok, nb)
            fc2(nb, E - 1)


_INS = ["x", "src", "dst", "L0_gnn_W", "L0_gnn_b", "L0_mix_W_qkv", "L0_mix_W_proj", "L0_mix_b_proj",
        "L0_mix_proj_mat", "L0_ffn_gate_w", "L0_ffn_gate_b", "L0_ffn_fc1_w", "L0_ffn_fc1_b", "L0_ffn_ln_w",
        "L0_ffn_ln_b", "L0_ffn_fc2_w", "L0_ffn_fc2_b"]


def kernel(**inputs):
    import numpy as np
    import concourse.bacc as bacc
    from concourse.bass_utils import run_bass_kernel_spmd

    nc = bacc.Bacc("TRN2", target_bir_lowering=False, num_devices=1)
    arrays, args = {}, []
    for name in _INS:
        a = np.ascontiguousarray(inputs[name])
        arrays[f"in_{name}"] = a
        args.append(nc.dram_tensor(f"in_{name}", a.shape, mybir.dt.from_np(a.dtype), kind="ExternalInput").ap())
    out = nc.dram_tensor("out", (N, D), F32, kind="ExternalOutput").ap()
    xn2_dram = nc.dram_tensor("xn2_dram", (N + 1, D), F32, kind="Internal").ap()
    table_dram = nc.dram_tensor("table_dram", (128 * TW, 2), I32, kind="Internal").ap()
    gps_kernel(nc, *args, out, xn2_dram, table_dram)
    r = run_bass_kernel_spmd(nc, [arrays], core_ids=[0])
    return r.results[0]["out"]
```
